# Optimizing a Trainium2 kernel written in Bass

```python
import numpy as np
import jax
import jax.numpy as jnp

def _softmax(x, axis=-1):
    return jax.nn.softmax(x, axis=axis)

def _gelu(x):
    return jax.nn.gelu(x, approximate=True)

def _silu(x):
    return jax.nn.silu(x)

def _sigmoid(x):
    return jax.nn.sigmoid(x)

def _layernorm(x, axis=-1, eps=1e-05):
    m = jnp.mean(x, axis=axis, keepdims=True)
    v = jnp.var(x, axis=axis, keepdims=True)
    return (x - m) / jnp.sqrt(v + eps)

def _scatter_add(tgt, idx, src, axis=0):
    return tgt.at[idx].add(src)

def _segment_sum(src, seg, n):
    return jax.ops.segment_sum(src, seg, n)
kernel_name = 'mk_xattn_seq_d2_seqx_r4_214e10'

def setup_inputs(seed: int=0):
    np.random.seed(seed)
    _w = jnp.asarray

    def _rec_inputs():
        import jax
        import jax.numpy as jnp
        _rk = jax.random.key(seed)
        x = -0.0002928 + 1 * jax.random.normal(jax.random.fold_in(_rk, 1), (8, 112, 256), jnp.float32)
        _lenS = 112 - jax.random.randint(jax.random.fold_in(_rk, 7), (8,), 0, max(1, 112 // 4) + 1, jnp.int32)
        _lenS2 = 375 - jax.random.randint(jax.random.fold_in(_rk, 8), (8,), 0, max(1, 375 // 4) + 1, jnp.int32)
        _ctx_1024P = jax.random.normal(jax.random.fold_in(_rk, 11), (8, 16, 256), jnp.float32)
        _ctx_1024c = jax.random.dirichlet(jax.random.fold_in(_rk, 511), 0.3 * jnp.ones((16,), jnp.float32), (8, 375))
        _ctx_1024t = jnp.einsum('bsk,bkd->bsd', _ctx_1024c, _ctx_1024P)
        _ctx_1024t = _ctx_1024t * jax.lax.rsqrt(jnp.mean(jnp.square(_ctx_1024t)) + 1e-12) * 0.953939
        ctx_1024 = -1.39393e-06 + 0.999914 * (_ctx_1024t + 0.3 * jax.random.normal(jax.random.fold_in(_rk, 611), (8, 375, 256), jnp.float32))
        _validS = jnp.arange(112)[None, :] < _lenS[:, None]
        _validS2 = jnp.arange(375)[None, :] < _lenS2[:, None]
        _causal = jnp.tril(jnp.ones((112, 112), dtype=bool))
        mask_BxS_bf0 = jnp.logical_not(jnp.ones((8, 112), dtype=bool))
        return (x, ctx_1024, mask_BxS_bf0)
    x, ctx_1024, mask_BxS_bf0 = _rec_inputs()

    def _L0_xattn_setup():
        import jax, jax.numpy as jnp
        import numpy as np
        NUM_UNITS = 256
        NUM_HEADS = 16
        CAUSALITY = True
        EPS = 1e-08
        NEG = jnp.float32(-2 ** 32 + 1)

        def _split_heads(x, H):
            B, S, U = x.shape
            d = U // H
            return x.reshape(B, S, H, d).transpose(2, 0, 1, 3).reshape(H * B, S, d)

        def _merge_heads(x, H):
            HB, S, d = x.shape
            B = HB // H
            return x.reshape(H, B, S, d).transpose(1, 2, 0, 3).reshape(B, S, H * d)

        def _layer_norm(x, gamma, beta):
            mean = jnp.mean(x, axis=-1, keepdims=True)
            std = jnp.std(x, axis=-1, keepdims=True, ddof=1)
            return gamma * (x - mean) / (std + EPS) + beta
        key = jax.random.key(seed)
        ks = jax.random.split(key, 12)
        B, S, U = (2, 512, NUM_UNITS)
        s = 1.0 / np.sqrt(U)
        return {'queries': jax.random.normal(ks[0], (B, S, U), jnp.float32), 'keys': jax.random.normal(ks[1], (B, S, U), jnp.float32), 'values': jax.random.normal(ks[2], (B, S, U), jnp.float32), 'Wq': jax.random.normal(ks[3], (U, U), jnp.float32) * s, 'bq': jax.random.normal(ks[4], (U,), jnp.float32) * s, 'Wk': jax.random.normal(ks[5], (U, U), jnp.float32) * s, 'bk': jax.random.normal(ks[6], (U,), jnp.float32) * s, 'Wv': jax.random.normal(ks[7], (U, U), jnp.float32) * s, 'bv': jax.random.normal(ks[8], (U,), jnp.float32) * s, 'gamma': jnp.ones((U,), jnp.float32), 'beta': jnp.zeros((U,), jnp.float32)}
    _L0_xattn_all = _L0_xattn_setup()
    _L0_xattn_in = {k: v for k, v in _L0_xattn_all.items() if k in ('Wq', 'bq', 'Wk', 'bk', 'Wv', 'bv', 'gamma', 'beta')}
    del _L0_xattn_all

    def _L1_xattn_setup():
        import jax, jax.numpy as jnp
        import numpy as np
        B, T, J, C, H = (16, 112, 112, 256, 16)
        HD = C // H
        NEG_INF = float('-inf')

        def _layernorm(x, g, b, eps=1e-05):
            mu = jnp.mean(x, axis=-1, keepdims=True)
            var = jnp.var(x, axis=-1, keepdims=True)
            return (x - mu) * jax.lax.rsqrt(var + eps) * g + b

        def _heads(x):
            Bv, S, _ = x.shape
            return x.reshape(Bv, S, H, HD).transpose(0, 2, 1, 3)

        def _merge(x):
            Bv, _, S, _ = x.shape
            return x.transpose(0, 2, 1, 3).reshape(Bv, S, C)

        def _forward(tgt, src, sa_wqkv, sa_wproj, sa_bproj, ed_wkv, ed_wq, ed_wproj, ed_bproj, ff_w1, ff_b1, ff_w2, ff_b2, ln1_g, ln1_b, ln2_g, ln2_b, ln3_g, ln3_b, tgt_padding_mask):
            scale = C ** (-0.5)
            x = _layernorm(tgt, ln1_g, ln1_b)
            qkv = x @ sa_wqkv
            q, k, v = (_heads(t) for t in jnp.split(qkv, 3, axis=-1))
            wei = jnp.einsum('bhtd,bhsd->bhts', q, k) * scale
            causal = jnp.tril(jnp.ones((T, T), bool))
            wei = jnp.where(causal[None, None], wei, NEG_INF)
            wei = jnp.where(tgt_padding_mask[:, None, None, :], NEG_INF, wei)
            wei = jax.nn.softmax(wei, axis=-1)
            sa_out = _merge(jnp.einsum('bhts,bhsd->bhtd', wei, v)) @ sa_wproj + sa_bproj
            result = tgt + sa_out
            xq = _layernorm(result, ln2_g, ln2_b)
            xs = _layernorm(src, ln2_g, ln2_b)
            kv = xs @ ed_wkv
            k2, v2 = (_heads(t) for t in jnp.split(kv, 2, axis=-1))
            q2 = _heads(xq @ ed_wq)
            wei2 = jnp.einsum('bhtd,bhjd->bhtj', q2, k2) * scale
            wei2 = jax.nn.softmax(wei2, axis=-1)
            ed_out = _merge(jnp.einsum('bhtj,bhjd->bhtd', wei2, v2)) @ ed_wproj + ed_bproj
            result = result + ed_out
            h = jax.nn.relu(_layernorm(tgt, ln3_g, ln3_b) @ ff_w1 + ff_b1)
            result = result + (h @ ff_w2 + ff_b2)
            return result
        key = jax.random.key(seed)
        ks = jax.random.split(key, 16)
        s = 0.02
        return {'tgt': jax.random.normal(ks[0], (B, T, C), jnp.float32), 'src': jax.random.normal(ks[1], (B, J, C), jnp.float32), 'sa_wqkv': jax.random.normal(ks[2], (C, 3 * C), jnp.float32) * s, 'sa_wproj': jax.random.normal(ks[3], (C, C), jnp.float32) * s, 'sa_bproj': jnp.zeros((C,), jnp.float32), 'ed_wkv': jax.random.normal(ks[4], (C, 2 * C), jnp.float32) * s, 'ed_wq': jax.random.normal(ks[5], (C, C), jnp.float32) * s, 'ed_wproj': jax.random.normal(ks[6], (C, C), jnp.float32) * s, 'ed_bproj': jnp.zeros((C,), jnp.float32), 'ff_w1': jax.random.normal(ks[7], (C, 4 * C), jnp.float32) * s, 'ff_b1': jnp.zeros((4 * C,), jnp.float32), 'ff_w2': jax.random.normal(ks[8], (4 * C, C), jnp.float32) * s, 'ff_b2': jnp.zeros((C,), jnp.float32), 'ln1_g': jnp.ones((C,), jnp.float32), 'ln1_b': jnp.zeros((C,), jnp.float32), 'ln2_g': jnp.ones((C,), jnp.float32), 'ln2_b': jnp.zeros((C,), jnp.float32), 'ln3_g': jnp.ones((C,), jnp.float32), 'ln3_b': jnp.zeros((C,), jnp.float32), 'tgt_padding_mask': jnp.zeros((B, T), bool)}
    _L1_xattn_all = _L1_xattn_setup()
    _L1_xattn_in = {k: v for k, v in _L1_xattn_all.items() if k in ('sa_wqkv', 'sa_wproj', 'sa_bproj', 'ed_wkv', 'ed_wq', 'ed_wproj', 'ed_bproj', 'ff_w1', 'ff_b1', 'ff_w2', 'ff_b2', 'ln1_g', 'ln1_b', 'ln2_g', 'ln2_b', 'ln3_g', 'ln3_b')}
    del _L1_xattn_all
    return {'x': x, 'ctx_1024': ctx_1024, 'mask_BxS_bf0': mask_BxS_bf0, 'L0_xattn_Wq': _L0_xattn_in['Wq'], 'L0_xattn_bq': _L0_xattn_in['bq'], 'L0_xattn_Wk': _L0_xattn_in['Wk'], 'L0_xattn_bk': _L0_xattn_in['bk'], 'L0_xattn_Wv': _L0_xattn_in['Wv'], 'L0_xattn_bv': _L0_xattn_in['bv'], 'L0_xattn_gamma': _L0_xattn_in['gamma'], 'L0_xattn_beta': _L0_xattn_in['beta'], 'L1_xattn_sa_wqkv': _L1_xattn_in['sa_wqkv'], 'L1_xattn_sa_wproj': _L1_xattn_in['sa_wproj'], 'L1_xattn_sa_bproj': _L1_xattn_in['sa_bproj'], 'L1_xattn_ed_wkv': _L1_xattn_in['ed_wkv'], 'L1_xattn_ed_wq': _L1_xattn_in['ed_wq'], 'L1_xattn_ed_wproj': _L1_xattn_in['ed_wproj'], 'L1_xattn_ed_bproj': _L1_xattn_in['ed_bproj'], 'L1_xattn_ff_w1': _L1_xattn_in['ff_w1'], 'L1_xattn_ff_b1': _L1_xattn_in['ff_b1'], 'L1_xattn_ff_w2': _L1_xattn_in['ff_w2'], 'L1_xattn_ff_b2': _L1_xattn_in['ff_b2'], 'L1_xattn_ln1_g': _L1_xattn_in['ln1_g'], 'L1_xattn_ln1_b': _L1_xattn_in['ln1_b'], 'L1_xattn_ln2_g': _L1_xattn_in['ln2_g'], 'L1_xattn_ln2_b': _L1_xattn_in['ln2_b'], 'L1_xattn_ln3_g': _L1_xattn_in['ln3_g'], 'L1_xattn_ln3_b': _L1_xattn_in['ln3_b']}

def reference(x, ctx_1024, mask_BxS_bf0, L0_xattn_Wq, L0_xattn_bq, L0_xattn_Wk, L0_xattn_bk, L0_xattn_Wv, L0_xattn_bv, L0_xattn_gamma, L0_xattn_beta, L1_xattn_sa_wqkv, L1_xattn_sa_wproj, L1_xattn_sa_bproj, L1_xattn_ed_wkv, L1_xattn_ed_wq, L1_xattn_ed_wproj, L1_xattn_ed_bproj, L1_xattn_ff_w1, L1_xattn_ff_b1, L1_xattn_ff_w2, L1_xattn_ff_b2, L1_xattn_ln1_g, L1_xattn_ln1_b, L1_xattn_ln2_g, L1_xattn_ln2_b, L1_xattn_ln3_g, L1_xattn_ln3_b):
    import jax
    import jax.numpy as jnp

    def _L0_xattn_ref(queries, keys, values, Wq, bq, Wk, bk, Wv, bv, gamma, beta):
        import jax, jax.numpy as jnp
        import numpy as np
        NUM_UNITS = 256
        NUM_HEADS = 16
        CAUSALITY = True
        EPS = 1e-08
        NEG = jnp.float32(-2 ** 32 + 1)

        def _split_heads(x, H):
            B, S, U = x.shape
            d = U // H
            return x.reshape(B, S, H, d).transpose(2, 0, 1, 3).reshape(H * B, S, d)

        def _merge_heads(x, H):
            HB, S, d = x.shape
            B = HB // H
            return x.reshape(H, B, S, d).transpose(1, 2, 0, 3).reshape(B, S, H * d)

        def _layer_norm(x, gamma, beta):
            mean = jnp.mean(x, axis=-1, keepdims=True)
            std = jnp.std(x, axis=-1, keepdims=True, ddof=1)
            return gamma * (x - mean) / (std + EPS) + beta
        H = NUM_HEADS
        B, Sq, U = queries.shape
        Sk = keys.shape[1]
        d = U // H
        Q = jax.nn.relu(queries @ Wq.T + bq)
        K = jax.nn.relu(keys @ Wk.T + bk)
        V = jax.nn.relu(values @ Wv.T + bv)
        Q_ = _split_heads(Q, H)
        K_ = _split_heads(K, H)
        V_ = _split_heads(V, H)
        scores = jnp.einsum('bqd,bkd->bqk', Q_, K_) / jnp.sqrt(jnp.float32(d))
        key_mask = jnp.sign(jnp.abs(jnp.sum(keys, axis=-1)))
        key_mask = jnp.tile(key_mask, (H, 1))[:, None, :]
        scores = jnp.where(key_mask == 0.0, NEG, scores)
        if CAUSALITY:
            tril = jnp.tril(jnp.ones((Sq, Sk), jnp.float32))
            scores = jnp.where(tril[None] == 0.0, NEG, scores)
        attn = jax.nn.softmax(scores, axis=-1)
        query_mask = jnp.sign(jnp.abs(jnp.sum(queries, axis=-1)))
        query_mask = jnp.tile(query_mask, (H, 1))[:, :, None]
        attn = attn * query_mask
        out = jnp.einsum('bqk,bkd->bqd', attn, V_)
        out = _merge_heads(out, H)
        out = out + queries
        return _layer_norm(out, gamma, beta)

    def _L1_xattn_ref(tgt, src, sa_wqkv, sa_wproj, sa_bproj, ed_wkv, ed_wq, ed_wproj, ed_bproj, ff_w1, ff_b1, ff_w2, ff_b2, ln1_g, ln1_b, ln2_g, ln2_b, ln3_g, ln3_b, tgt_padding_mask):
        import jax, jax.numpy as jnp
        import numpy as np
        B, T, J, C, H = (16, 112, 112, 256, 16)
        HD = C // H
        NEG_INF = float('-inf')

        def _layernorm(x, g, b, eps=1e-05):
            mu = jnp.mean(x, axis=-1, keepdims=True)
            var = jnp.var(x, axis=-1, keepdims=True)
            return (x - mu) * jax.lax.rsqrt(var + eps) * g + b

        def _heads(x):
            Bv, S, _ = x.shape
            return x.reshape(Bv, S, H, HD).transpose(0, 2, 1, 3)

        def _merge(x):
            Bv, _, S, _ = x.shape
            return x.transpose(0, 2, 1, 3).reshape(Bv, S, C)

        def _forward(tgt, src, sa_wqkv, sa_wproj, sa_bproj, ed_wkv, ed_wq, ed_wproj, ed_bproj, ff_w1, ff_b1, ff_w2, ff_b2, ln1_g, ln1_b, ln2_g, ln2_b, ln3_g, ln3_b, tgt_padding_mask):
            scale = C ** (-0.5)
            x = _layernorm(tgt, ln1_g, ln1_b)
            qkv = x @ sa_wqkv
            q, k, v = (_heads(t) for t in jnp.split(qkv, 3, axis=-1))
            wei = jnp.einsum('bhtd,bhsd->bhts', q, k) * scale
            causal = jnp.tril(jnp.ones((T, T), bool))
            wei = jnp.where(causal[None, None], wei, NEG_INF)
            wei = jnp.where(tgt_padding_mask[:, None, None, :], NEG_INF, wei)
            wei = jax.nn.softmax(wei, axis=-1)
            sa_out = _merge(jnp.einsum('bhts,bhsd->bhtd', wei, v)) @ sa_wproj + sa_bproj
            result = tgt + sa_out
            xq = _layernorm(result, ln2_g, ln2_b)
            xs = _layernorm(src, ln2_g, ln2_b)
            kv = xs @ ed_wkv
            k2, v2 = (_heads(t) for t in jnp.split(kv, 2, axis=-1))
            q2 = _heads(xq @ ed_wq)
            wei2 = jnp.einsum('bhtd,bhjd->bhtj', q2, k2) * scale
            wei2 = jax.nn.softmax(wei2, axis=-1)
            ed_out = _merge(jnp.einsum('bhtj,bhjd->bhtd', wei2, v2)) @ ed_wproj + ed_bproj
            result = result + ed_out
            h = jax.nn.relu(_layernorm(tgt, ln3_g, ln3_b) @ ff_w1 + ff_b1)
            result = result + (h @ ff_w2 + ff_b2)
            return result
        return _forward(tgt, src, sa_wqkv, sa_wproj, sa_bproj, ed_wkv, ed_wq, ed_wproj, ed_bproj, ff_w1, ff_b1, ff_w2, ff_b2, ln1_g, ln1_b, ln2_g, ln2_b, ln3_g, ln3_b, tgt_padding_mask)
    x = _L0_xattn_ref(x, ctx_1024, ctx_1024, L0_xattn_Wq, L0_xattn_bq, L0_xattn_Wk, L0_xattn_bk, L0_xattn_Wv, L0_xattn_bv, L0_xattn_gamma, L0_xattn_beta)
    x = _L1_xattn_ref(x, ctx_1024, L1_xattn_sa_wqkv, L1_xattn_sa_wproj, L1_xattn_sa_bproj, L1_xattn_ed_wkv, L1_xattn_ed_wq, L1_xattn_ed_wproj, L1_xattn_ed_bproj, L1_xattn_ff_w1, L1_xattn_ff_b1, L1_xattn_ff_w2, L1_xattn_ff_b2, L1_xattn_ln1_g, L1_xattn_ln1_b, L1_xattn_ln2_g, L1_xattn_ln2_b, L1_xattn_ln3_g, L1_xattn_ln3_b, mask_BxS_bf0)
    return x

_drawn_inputs = setup_inputs


def setup_inputs(seed=0):
    import zlib

    import numpy as np

    out = dict(_drawn_inputs(seed))
    spreads = {'L0_xattn_gamma': (1.0, 0.2),
     'L0_xattn_beta': (0.0, 0.1),
     'L1_xattn_sa_bproj': (0.0, 0.1),
     'L1_xattn_ed_bproj': (0.0, 0.1),
     'L1_xattn_ff_b1': (0.0, 0.1),
     'L1_xattn_ff_b2': (0.0, 0.1),
     'L1_xattn_ln1_g': (1.0, 0.6),
     'L1_xattn_ln1_b': (0.0, 0.8),
     'L1_xattn_ln2_g': (1.0, 0.6),
     'L1_xattn_ln2_b': (0.0, 0.8),
     'L1_xattn_ln3_g': (1.0, 0.6),
     'L1_xattn_ln3_b': (0.0, 0.612)}
    factors = {'L0_xattn_bq': 8.0, 'L0_xattn_bk': 21.642, 'L1_xattn_ed_wq': 34.736}
    for name, (base, spread) in spreads.items():
        noise = np.random.default_rng([zlib.crc32(name.encode()), seed]).standard_normal(out[name].shape)
        drawn = base * np.exp(spread * noise) if base else spread * noise
        out[name] = jnp.asarray(drawn.astype(out[name].dtype))
    for name, factor in factors.items():
        out[name] = (out[name] * factor).astype(out[name].dtype)
    return out
```

```python
from contextlib import ExitStack

import numpy as np

import concourse.bass as bass
from concourse import mybir

F32 = mybir.dt.float32
F32R = mybir.dt.float32r
BF16 = mybir.dt.bfloat16
I32 = mybir.dt.int32
U8 = mybir.dt.uint8
ALU = mybir.AluOpType
ACT = mybir.ActivationFunctionType
AX = mybir.AxisListType

B, T, S, U, H = 8, 112, 375, 256, 16
D = U // H
C = U // 128
FF = 4 * U // 128
G = 2
NG = B // G
NCH, CH = 3, 125
SP = 376
DV = D + 1
BIG = -float(2 ** 100)
HI, LO = 0, 1


class Signal:

    def __init__(self, sem, per):
        self.sem, self.per, self.given = sem, per, 0
        self.start = 0

    def at(self, g, k):
        return g * self.per + (k + self.start)

    def done(self, g):
        return g * self.per + (self.per + self.start)

    def before(self, g):
        return g * self.per + self.start

    def step(self, instruction):
        self.given += 1
        instruction.then_inc(self.sem, 1)


def build(nc, x_nat_d, x_t_d, c_nat_d, c_t_d, c_first_d, mask_d, w_d, vec_d, row_d, const_d, out_d):
    ctx = ExitStack()
    with ctx:
        def sb(name, shape, dt=F32):
            return ctx.enter_context(nc.sbuf_tensor(name, shape, dt))

        def sem(name):
            return ctx.enter_context(nc.semaphore(name))

        wshape = {"wq0": (C, U), "wk0": (C, U), "wv0": (C, U), "wqkv1": (C, 3 * U), "wp1": (C, U),
                  "wq2": (C, U), "wkv2": (C, 2 * U), "wp2": (C, U), "w1": (C, 4 * U), "w2": (FF, U)}
        w = {n: sb(n, [128, 2, *s], F32R) for n, s in wshape.items()}
        late = ("w1", "w2")
        raw_cols = sum(a * b for n, (a, b) in wshape.items() if n not in late)
        w_raw = sb("w_raw", [128, raw_cols])
        w_raw_of, at = {}, 0
        for n, (a, b) in wshape.items():
            at = 0 if n == late[0] else at
            w_raw_of[n] = w_raw[:, at:at + a * b].rearrange("p (a b) -> p a b", a=a)
            at += a * b
        spare = [0]

        def over_raw(*shape):
            n = int(np.prod(shape))
            at_, spare[0] = spare[0], spare[0] + n
            assert spare[0] <= raw_cols
            names_ = "abcd"[:len(shape)]
            return w_raw[:, at_:at_ + n].rearrange(f"p ({' '.join(names_)}) -> p {' '.join(names_)}", **dict(zip(names_, shape)))

        NVEC = vec_d.shape[1]
        vec = sb("vec", [128, NVEC])
        names = ["bq0", "bk0", "g1", "b1", "g3", "b3", "g2", "b2"]
        VEC = {n: 2 * i for i, n in enumerate(names)}
        FB1 = 2 * len(names)
        EO = FB1 + FF
        rowv = {n: sb(n, [T if n != "bv0" else CH, U]) for n in ("bv0", "gamma0", "beta0", "bp1", "bp2")}
        ident = sb("ident", [128, 128])
        ident_b = sb("ident_b", [T, T], BF16)
        causal = sb("causal", [T, T], BF16)
        causal2 = sb("causal2", [T, T], BF16)
        tril = sb("tril", [T, T], BF16)
        select = sb("select", [48, H], BF16)
        mask_u8 = sb("mask_u8", [T, B], U8)
        pad1_all = sb("pad1_all", [T, B])
        eo_scale = sb("eo_scale", [128, 2, 2])
        bq0_eo = sb("bq0_eo", [128, C, 2])

        x_nat = sb("x_nat", [T, G, U])
        x_t = sb("x_t", [128, C, G, T])
        c_nat = sb("c_nat", [CH, G, NCH, U])
        c_t = sb("c_t", [128, C, G, T])
        xs = sb("xs", [128, 2, C, G, T], F32R)
        cs = sb("cs", [128, 2, C, G, T], F32R)
        q_tmp = over_raw(C, G, 2, T)
        q = sb("q", [128, 2, C, G, 2, T], F32R)
        o_n = over_raw(G, U)[0:T]
        k_tmp = w_raw[:, spare[0] - G * U:spare[0] - G * U + C * G * T].rearrange("p (c b t) -> p c b t", c=C, b=G)
        k = sb("k", [128, 2, C, G, T], F32R)
        v = [sb(f"v{i}", [T, G, H, DV]) for i in range(2)]
        n1_tmp, n3_tmp = x_t, c_t
        n1, n3 = xs, cs
        h_tmp = over_raw(FF, G, T)
        h = sb("h", [128, 2, FF, G, T], F32R)
        ct_tmp = over_raw(C, G, SP)
        ct = sb("ct", [128, 2, C, G, SP], F32R)
        k2 = sb("k2", [128, 2, C, G, SP], F32R)
        v2 = sb("v2", [CH, G, NCH, H, DV])
        o_t = sb("o_t", [128, 2, C, G, T], F32R)
        NP = 4
        probs = sb("probs", [CH, NP, 2, 4, T])
        negmax = sb("negmax", [T, G, H])
        negmax_t = sb("negmax_t", [48, G, T], BF16)

        first_keys = x_nat[0:B, 0, :]
        first_sum = sb("first_sum", [B, 1]); first_masked = sb("first_masked", [B, 1]); ones = sb("ones", [CH, 1])
        any_masked = sb("any_masked", [1, 1], I32)
        gen_c = x_t[:, :, :, :].rearrange("p c b t -> p (c b t)")[:, 0:C * CH].rearrange("p (c k) -> p c k", c=C)
        ksum = sb("ksum", [T, G]); keep0 = sb("keep0", [T, G]); keep0b = sb("keep0b", [T, G], BF16)
        pad0 = sb("pad0", [T, G]); pad1 = sb("pad1", [T, G]); keep1b = sb("keep1b", [T, G], BF16)
        qkeep = sb("qkeep", [T, G])
        add_mask = sb("add_mask", [T, 2, G, T], BF16)
        valid = sb("valid", [T, G]); rvalid = sb("rvalid", [T, G]); nanf = sb("nanf", [T, G])
        empty = sb("empty", [1, G, T])
        v_all_g = over_raw(G, H * DV)[0:1]
        stats = sb("stats", [CH, G * NCH, 6]); mv = sb("mv", [CH, G * NCH, 2])
        rstd = sb("rstd", [CH, G * NCH]); var_e = sb("var_e", [CH, G * NCH]); half = sb("half", [CH, 2 * G * NCH])
        rden = sb("rden", [T, G, H]); x1 = sb("x1", [T, G, U]); r1 = x1
        sd = sb("sd", [T, G]); sd_r = sb("sd_r", [T, G]); xh = sb("xh", [T, G, U])
        y = res = v_tmp = xh
        row = xh[0:1, :, :].rearrange("p b u -> p (b u)")[:, 0:H * DV]
        rowv["fb2"] = x1[:, 0, :]

        NR = 3
        ring = [ctx.enter_context(nc.psum_tensor(f"ring{i}", [128, 2, 512], F32)) for i in range(NR)]
        out_acc = [ctx.enter_context(nc.psum_tensor(f"out_acc{b}", [128, 512], F32)) for b in range(G)]

        x_loaded, c_loaded = sem("x_loaded"), sem("c_loaded")
        stored = sem("stored"); v_all_stored = sem("v_all_stored")
        first_loaded, first_counted, flag_made = sem("first_loaded"), sem("first_counted"), sem("flag_made")
        flag_steps = sem("flag_steps")
        gen_loaded, gen_values, gen_ready, gen_summed, gen_row = (sem(n) for n in ("gen_loaded", "gen_values", "gen_ready", "gen_summed", "gen_row"))
        v_all_d = nc.dram_tensor("v_all", [B, H * DV], F32).ap()
        const_loaded = [sem(f"const_loaded{i}") for i in range(3)]
        w_loaded = {n: sem("loaded_" + n) for n in wshape}
        PREP_DVE, PREP_POOL = 9 + len(wshape), 2 + len(wshape)
        prep_act = sem("prep_act"); prep_dve = sem("prep_dve"); prep_pool = sem("prep_pool")

        waited = {e.engine: sem(n) for n, e in (("waited_sp", nc.sync), ("waited_dve", nc.vector), ("waited_pool", nc.gpsimd))}
        sig = {}
        OUT0, OUT1, OUT2 = 17, 3, 2

        def signal(name, per):
            sig[name] = Signal(sem(name), per)
            return sig[name]

        JOBS = []
        filled = None
        a_q0 = signal("q0_biased", 4); a_k0 = signal("k0_biased", 2)
        a_q1 = signal("q1_scaled", 4); a_n = signal("norm13_scaled", 4); a_q2 = signal("q2_scaled", 4)
        a_k1 = signal("k1_hi", 1); a_k2 = signal("k2_hi", G); a_ct = signal("ctx_scaled", 2 * G)
        a_h = signal("hidden_biased", FF); a_exp = signal("exponentials", 20); a_ot = signal("out1_hi", 1)
        a_o2t = signal("out2_hi", 1); a_xq = signal("norm2_scaled", 2)
        v_mask = signal("masks_made", 8 + 2 * G)
        v_cnt = signal("counts_read", 4)
        v_ctxln = signal("ctx_normed", 3 * G * NCH + 1)
        v_xs_hi = signal("xs_hi", 2)
        v_q0_hi = signal("q0_hi", 1); v_k0_hi = signal("k0_hi", 1)
        v_q1_hi = signal("q1_hi", 1); v_q2_hi = signal("q2_hi", 1); v_k1_lo = signal("k1_lo", 1); v_k2_lo = signal("k2_lo", G)
        v_n_hi = signal("norm13_hi", 2); v_ct_hi = signal("ctx_hi", G); v_h_hi = signal("hidden_hi", 2)
        v_v0 = signal("values0", 1 + 2 * G); v_v1 = signal("values1", 1); v_v2 = signal("values2", 2)
        v_max = [signal(f"max{a}", n) for a, n in enumerate((4, 4, 16))]
        v_maxt = [signal(f"max_t{a}", 2 * G) for a in range(3)]
        v_post0 = signal("out0_steps", OUT0 * G); v_post1 = signal("out1_steps", 3 * G)
        v_ot_lo = signal("out1_lo", 1); v_o2t_lo = signal("out2_lo", 1); v_proj = signal("proj_steps", 2 + 5 * G)
        v_xq_hi = signal("norm2_hi", 1); v_post2 = signal("out2_steps", 2 * G); v_res = signal("result", 1)
        p_xs_lo = signal("xs_lo", 2); p_q0_lo = signal("q0_lo", 1); p_k0_lo = signal("k0_lo", 1)
        p_q1_lo = signal("q1_lo", 1); p_q2_lo = signal("q2_lo", 1); p_n_lo = signal("norm13_lo", 2)
        p_ct_lo = signal("ctx_lo", G); p_h_lo = signal("hidden_lo", 2);
        p_rstd = signal("rstd", 1 + 2 * G + G); p_xq_lo = signal("norm2_lo", 1)
        pv_done = signal("values_summed", 20)

        def job(name, by, step):
            JOBS.append((name, by, step))

        job("cnt", v_cnt, 2)
        job("q0", a_q0, 4); job("k0", a_k0, 2); job("v0", v_v0, 1)
        for b in range(G):
            job(f"ctxT{b}", a_ct, 2 * b + 2)
        for b in range(G):
            for m in range(2):
                job(f"max0_{b}_{m}", v_max[0], 2 * b + m + 1)
        job("k2_0", v_k2_lo, 1)
        job("maxT0_0", v_maxt[0], 2)
        job("exp0_0_0", a_exp, 1); job("exp0_0_1", a_exp, 2)
        job("k2_1", v_k2_lo, 2)
        job("maxT0_1", v_maxt[0], 4)
        job("exp0_1_0", a_exp, 3); job("exp0_1_1", a_exp, 4)
        job("v2_0", v_v2, 1); job("v2_1", v_v2, 2)
        job("xT1", a_n, 4); job("q1", a_q1, 4); job("k1", v_k1_lo, 1); job("v1", v_v1, 1)
        for b in range(G):
            for m in range(2):
                job(f"max1_{b}_{m}", v_max[1], 2 * b + m + 1)
        job("h0", a_h, 4)
        job("maxT1_0", v_maxt[1], 2)
        job("exp1_0_0", a_exp, 5); job("exp1_0_1", a_exp, 6)
        job("h1", a_h, 8)
        job("maxT1_1", v_maxt[1], 4)
        job("exp1_1_0", a_exp, 7); job("exp1_1_1", a_exp, 8)
        job("oT1", v_ot_lo, 1); job("proj", v_proj, 2); job("xqT", a_xq, 2); job("q2", a_q2, 4)
        for m in range(8):
            job(f"max2_0_{m}", v_max[2], m + 1)
        job("maxT2_0", v_maxt[2], 2)
        for i in range(6):
            job(f"exp2_0_{i}", a_exp, 9 + i)
            job(f"max2_1_{i}", v_max[2], 9 + i)
        job("max2_1_6", v_max[2], 15); job("max2_1_7", v_max[2], 16)
        job("maxT2_1", v_maxt[2], 4)
        for i in range(6):
            job(f"exp2_1_{i}", a_exp, 15 + i)
        job("oT2", v_o2t_lo, 1); job("y", v_res, 1)
        while len(JOBS) % NR:
            job(f"none{len(JOBS)}", None, 0)
        act_back, dve_back, pool_back = (a_ct, a_exp), (v_post0, v_post2, v_o2t_lo, v_res, v_cnt), (p_xq_lo, p_q2_lo, p_ct_lo)
        for s in (*act_back, *dve_back, *pool_back):
            s.start = 1
        NJ = len([j for j in JOBS if j[1]])
        filled = signal("psum_filled", NJ)
        number = {name: i for i, (name, _, _) in enumerate(JOBS)}

        def granule(name):
            return ring[number[name] % NR]

        def is_filled(eng, g, name):
            eng.wait_ge(filled.sem, filled.at(g, number[name] + 1))

        def claim(pe, g, name):
            i = number[name] - NR
            _, by, step = JOBS[i]
            while by is None:
                i -= NR
                _, by, step = JOBS[i]
            pe.wait_ge(by.sem, by.at(g, step) if i >= 0 else by.before(g))
            return granule(name)

        def alone(eng):
            eng.sem_inc(waited[eng.engine], 1)

        TERMS = ((HI, HI), (HI, LO), (LO, HI))

        block = ctx.enter_context(nc.Block())

        @block.sync
        def _(sp):
            sp.dma_start(vec[:, :], vec_d).then_inc(const_loaded[0], 16)
            sp.dma_start(mask_u8[:, :], mask_d).then_inc(const_loaded[0], 16)
            sp.dma_start(first_keys, c_first_d).then_inc(first_loaded, 16)
            for n in ("causal", "causal2", "tril", "ident_b", "select"):
                dst = {"causal": causal[:, :], "causal2": causal2[:, :], "tril": tril[:, :], "ident_b": ident_b[:, :], "select": select[:, :]}[n]
                sp.dma_start(dst, const_d[n]).then_inc(const_loaded[1], 16)
            sp.dma_start(ident[:, :], const_d["ident"]).then_inc(const_loaded[1], 16)
            for n in rowv:
                sp.dma_start(rowv[n][:, :], row_d[n].unsqueeze(0).to_broadcast([rowv[n].shape[0], U])).then_inc(const_loaded[2], 16)
            for n in wshape:
                if n == late[0]:
                    sp.wait_ge(prep_pool, 2 + len(wshape) - len(late))
                sp.dma_start(w_raw_of[n], w_d[n].rearrange("(a p) b -> p a b", p=128)).then_inc(w_loaded[n], 16)
            sp.wait_ge(prep_dve, 5)
            sp.dma_start(v_all_d.rearrange("b n -> (b n)").unsqueeze(0).rearrange("p (b n) -> p b n", b=B),
                         row.unsqueeze(1).to_broadcast([1, B, H * DV])).then_inc(v_all_stored, 16)
            sp.wait_ge(v_all_stored, 16)
            sp.wait_ge(flag_made, 2)
            with sp.If(sp.value_load(any_masked[0:1, 0:1]) > 0):
                with sp.Fori(0, B) as b:
                    for ch in range(NCH):
                        if ch:
                            sp.wait_ge(gen_values, b * NCH + ch)
                            alone(sp)
                        sp.dma_start(gen_c, c_t_d.rearrange("(c p) t -> p c t", p=128)[:, :, bass.ds(b * S + ch * CH, CH)]).then_inc(gen_loaded, 16)
                    sp.wait_ge(gen_row, b + 1)
                    alone(sp)
                    sp.dma_start(v_all_d[bass.ds(b, 1), :], row).then_inc(v_all_stored, 16)
                    sp.wait_ge(v_all_stored, b * 16 + 32)
                    alone(sp)
            sp.wait_ge(prep_pool, PREP_POOL)
            with sp.Fori(0, NG) as g:
                sp.wait_ge(p_xq_lo.sem, p_xq_lo.before(g))
                sp.wait_ge(v_post0.sem, v_post0.before(g))
                alone(sp)
                sp.dma_start(x_t[:, :, :, :].rearrange("p c b t -> p c (b t)"),
                             x_t_d.rearrange("(c p) t -> p c t", p=128)[:, :, bass.ds(g * (G * T), G * T)]).then_inc(x_loaded, 16)
                for b in range(G):
                    sp.dma_start(c_t[:, :, b, :], c_t_d.rearrange("(c p) t -> p c t", p=128)[:, :, bass.ds(g * (G * S) + b * S, T)]).then_inc(x_loaded, 16)
                sp.dma_start(x_nat[:, :, :], x_nat_d[bass.ds(g * G, G), :, :].rearrange("b t f -> t b f")).then_inc(x_loaded, 16)
                sp.wait_ge(a_ct.sem, a_ct.before(g))
                alone(sp)
                sp.dma_start(v_all_g[:, :, :], v_all_d[bass.ds(g * G, G), :].unsqueeze(0)).then_inc(x_loaded, 16)
                for b in range(G):
                    sp.dma_start(c_nat[:, b, :, :], c_nat_d.rearrange("b (c p) f -> b p c f", p=CH)[bass.ds(g * G + b, 1), :, :, :].rearrange("b p c f -> (b p) c f")).then_inc(c_loaded, 16)
            sp.wait_ge(stored, 16 * NG + 16)

        @block.tensor
        def _(pe):
            def tokens(t, part, c, b=None):
                return t[:, part, c, :, :].rearrange("p b t -> p (b t)") if b is None else t[:, part, c, b, :]

            def end(g, name, m):
                filled.step(m)

            def transposed_out(g, name, weights, col, act, tiles=C, first=0, per_bank=1):
                o = claim(pe, g, name)
                for i in range(tiles):
                    dst = o[:, i // per_bank, (i % per_bank) * G * T:(i % per_bank + 1) * G * T]
                    n = 0
                    for ci in range(C):
                        for wp, ap in TERMS:
                            m = nc.tensor.matmul(dst, weights[:, wp, ci, col + 128 * (first + i):col + 128 * (first + i + 1)],
                                                 tokens(act, ap, ci), start=n == 0, stop=n == 3 * C - 1)
                            n += 1
                end(g, name, m)

            def self_max(g, layer, b, m_, qs, ks):
                name = f"max{layer}_{b}_{m_}"
                o = claim(pe, g, name)
                for jj in range(2):
                    nc.tensor.matmul(o[0:T, jj, 0:4 * T], add_mask[:, layer, b, :], ident_b[:, :].unsqueeze(1).to_broadcast([T, 4, T]),
                                     start=True, stop=False, skip_group_check=True)
                for c in range(C):
                    for e in range(2):
                        for wp, ap in TERMS:
                            for jj in range(2):
                                r = 32 * (2 * m_ + jj)
                                m = nc.tensor.matmul(o[0:T, jj, (2 * c + e) * T:(2 * c + e + 1) * T],
                                                     qs[r:r + 32, wp, c, b, e, :], ks[r:r + 32, ap, c, b, :],
                                                     start=False, stop=True, skip_group_check=True)
                end(g, name, m)

            def max_transpose(g, layer, b):
                name = f"maxT{layer}_{b}"
                o = claim(pe, g, name)
                pe.wait_ge(v_max[layer].sem, v_max[layer].at(g, (b + 1) * v_max[layer].per // G))
                m = nc.tensor.transpose(o[0:H, 0, 0:T], negmax[:, b, :], ident[0:T, 0:T])
                end(g, name, m)

            def exp_scores(g, name, b, m_, ks, keys, n_keys, layer):
                o = claim(pe, g, name)
                if layer < 2:
                    for jj in range(2):
                        nc.tensor.matmul(o[0:T, jj, 0:4 * T], ident_b[:, :], causal2[:, :].unsqueeze(1).to_broadcast([T, 4, T]),
                                         start=True, stop=False, skip_group_check=True)
                for c in range(C):
                    for n, (kp, qp) in enumerate(TERMS):
                        for jj in range(2):
                            r = 32 * (2 * m_ + jj)
                            nc.tensor.matmul(o[0:n_keys, jj, 2 * c * T:2 * (c + 1) * T], ks(r, kp, c, b, keys),
                                             q[r:r + 32, qp, c, b, :, :].rearrange("p e t -> p (e t)"),
                                             start=(layer == 2 and c == 0 and n == 0), stop=False, skip_group_check=True)
                for jj in range(2):
                    for ce in range(4):
                        hh = 4 * (2 * m_ + jj) + ce
                        m = nc.tensor.matmul(o[0:n_keys, jj, ce * T:(ce + 1) * T], select[:, hh:hh + 1].to_broadcast([48, n_keys]),
                                             negmax_t[:, b, :], start=False, stop=True, skip_group_check=True)
                end(g, name, m)

            def ks_self(r, part, c, b, keys):
                return k[r:r + 32, part, c, b, :]

            def ks_cross(r, part, c, b, ch):
                return k2[r:r + 32, part, c, b, ch * CH:(ch + 1) * CH]

            def sum_values(g, e_no, b, m_, vals, n_keys, first, last, tail=None):
                slot = e_no % NP
                for jj in range(2):
                    for ce in range(4):
                        hd = 8 * (ce // 2) + 2 * (2 * m_ + jj) + ce % 2
                        m = nc.tensor.matmul(out_acc[b][0:T, hd * DV:(hd + 1) * DV], probs[0:n_keys, slot, jj, ce, :],
                                             vals(hd), start=first and jj == 0 and ce == 0, stop=True,
                                             skip_group_check=True)
                if tail is not None:
                    m = tail()
                pv_done.step(m)

            pe.wait_ge(flag_made, 1)
            nc.tensor.matmul(ring[0][0:1, 0, 0:1], first_masked[:, :], ones[0:B, :], start=True, stop=True).then_inc(first_counted, 1)
            pe.wait_ge(const_loaded[1], 96)
            pe.wait_ge(prep_dve, PREP_DVE)
            pe.wait_ge(prep_pool, PREP_POOL)
            pe.wait_ge(flag_made, 2)
            with pe.If(pe.value_load(any_masked[0:1, 0:1]) > 0):
                with pe.Fori(0, B) as b:
                    for ch in range(NCH):
                        pe.wait_ge(gen_loaded, b * (16 * NCH) + 16 * ch + 16)
                        n = 0
                        for ci in range(C):
                            for part in (HI, LO):
                                m = nc.tensor.matmul(ring[1][0:CH, 0, 0:U], gen_c[:, ci, :], w["wv0"][:, part, ci, :].bitcast(F32),
                                                     start=n == 0, stop=n == 2 * C - 1)
                                n += 1
                        m.then_inc(gen_values, 1)
                        pe.wait_ge(gen_ready, b * (2 * NCH) + 2 * ch + 2)
                        m = nc.tensor.matmul(ring[2][0:1, 0, 0:H * DV], ones[:, :], v2[:, 0, ch, :, :].rearrange("p h d -> p (h d)"), start=ch == 0, stop=ch == NCH - 1)
                    m.then_inc(gen_summed, 1)
                    pe.wait_ge(gen_row, b + 1)
            with pe.Fori(0, NG) as g:
                o = claim(pe, g, "cnt")
                pe.wait_ge(v_mask.sem, v_mask.done(g))
                for b in range(G):
                    nc.tensor.matmul(o[0:1, 1, b * T:(b + 1) * T], keep0b[:, b:b + 1], tril[:, :], start=b == 0, stop=True, skip_group_check=True)
                m = nc.tensor.matmul(o[0:T, 0, 0:G], tril[:, :], keep1b[:, :], start=True, stop=True)
                end(g, "cnt", m)
                pe.wait_ge(p_xs_lo.sem, p_xs_lo.done(g))
                transposed_out(g, "q0", w["wq0"], 0, xs)
                transposed_out(g, "k0", w["wk0"], 0, cs)

                def natural(g, name, act, weights, col, rows=T, more=()):
                    o = claim(pe, g, name)
                    for b in range(G):
                        prods = [(act[:, ap, c, b, :], weights[:, wp, c, col:col + U]) for c in range(C) for wp, ap in TERMS]
                        for a2, w2_, n2 in more:
                            prods += [(a2[:, ap, c, b, :], w2_[:, wp, c, 0:U]) for c in range(n2) for wp, ap in TERMS]
                        for n, (l, r) in enumerate(prods):
                            m = nc.tensor.matmul(o[0:rows, b, 0:U], l, r, start=n == 0, stop=n == len(prods) - 1)
                    end(g, name, m)

                natural(g, "v0", cs, w["wv0"], 0)
                for b in range(G):
                    name = f"ctxT{b}"
                    o = claim(pe, g, name)
                    pe.wait_ge(v_ctxln.sem, v_ctxln.done(g))
                    for c in range(C):
                        for ch in range(NCH):
                            m = nc.tensor.transpose(o[:, c, ch * CH:(ch + 1) * CH], c_nat[0:CH, b, ch, c * 128:(c + 1) * 128],
                                                    ident[0:CH, 0:CH])
                    end(g, name, m)
                pe.wait_ge(p_q0_lo.sem, p_q0_lo.done(g))
                pe.wait_ge(p_k0_lo.sem, p_k0_lo.done(g))
                for b in range(G):
                    for m_ in range(2):
                        self_max(g, 0, b, m_, q, k)

                def project_k2(g, b):
                    name = f"k2_{b}"
                    o = claim(pe, g, name)
                    pe.wait_ge(p_ct_lo.sem, p_ct_lo.at(g, b + 1))
                    for i in range(C):
                        n = 0
                        for ci in range(C):
                            for wp, ap in TERMS:
                                m = nc.tensor.matmul(o[:, i, 0:SP], w["wkv2"][:, wp, ci, 128 * i:128 * (i + 1)], ct[:, ap, ci, b, :],
                                                     start=n == 0, stop=n == 3 * C - 1)
                                n += 1
                    end(g, name, m)

                def project_v2(g, b):
                    name = f"v2_{b}"
                    o = claim(pe, g, name)
                    for ch in range(NCH):
                        n = 0
                        for ci in range(C):
                            for wp, ap in TERMS:
                                m = nc.tensor.matmul(o[0:CH, ch // 2, (ch % 2) * U:(ch % 2 + 1) * U],
                                                     ct[:, ap, ci, b, ch * CH:(ch + 1) * CH], w["wkv2"][:, wp, ci, U:2 * U],
                                                     start=n == 0 and ch % 2 == 0, stop=n == 3 * C - 1, skip_group_check=True)
                                n += 1
                    end(g, name, m)

                def attend(g, layer, b):
                    max_transpose(g, layer, b)
                    pe.wait_ge(v_maxt[layer].sem, v_maxt[layer].at(g, 2 * b + 2))
                    for m_ in range(2):
                        exp_scores(g, f"exp{layer}_{b}_{m_}", b, m_, ks_self, None, T, layer)

                def sum_self(g, layer, b):
                    for m_ in range(2):
                        e_no = 4 * layer + 2 * b + m_
                        pe.wait_ge(a_exp.sem, a_exp.at(g, e_no + 1))

                        def no_keys_at_all():
                            return nc.tensor.matmul(out_acc[b][0:T, 0:H * DV], empty[:, b, :], v_all_g[:, b, :],
                                                    start=False, stop=True, skip_group_check=True)

                        sum_values(g, e_no, b, m_, lambda hd: v[layer][:, b, hd, :], T, m_ == 0, m_ == 1,
                                   no_keys_at_all if layer == 0 and m_ == 1 else None)

                project_k2(g, 0)
                attend(g, 0, 0)
                project_k2(g, 1)
                attend(g, 0, 1)
                project_v2(g, 0)
                project_v2(g, 1)
                pe.wait_ge(v_v0.sem, v_v0.done(g))
                pe.wait_ge(v_cnt.sem, v_cnt.done(g))
                pe.wait_ge(v_post2.sem, v_post2.before(g))
                sum_self(g, 0, 0)
                sum_self(g, 0, 1)
                o = claim(pe, g, "xT1")
                for b in range(G):
                    pe.wait_ge(v_post0.sem, v_post0.at(g, OUT0 * (b + 1) - 1))
                    for c in range(C):
                        m = nc.tensor.transpose(o[:, c, b * T:(b + 1) * T], xh[:, b, c * 128:(c + 1) * 128], ident[0:T, 0:T])
                end(g, "xT1", m)
                pe.wait_ge(p_n_lo.sem, p_n_lo.at(g, 1))
                transposed_out(g, "q1", w["wqkv1"], 0, n1)
                transposed_out(g, "k1", w["wqkv1"], U, n1)
                natural(g, "v1", n1, w["wqkv1"], 2 * U)
                pe.wait_ge(p_q1_lo.sem, p_q1_lo.done(g))
                pe.wait_ge(v_k1_lo.sem, v_k1_lo.done(g))
                for b in range(G):
                    for m_ in range(2):
                        self_max(g, 1, b, m_, q, k)
                pe.wait_ge(p_n_lo.sem, p_n_lo.done(g))
                transposed_out(g, "h0", w["w1"], 0, n3, tiles=4, per_bank=2)
                attend(g, 1, 0)
                transposed_out(g, "h1", w["w1"], 0, n3, tiles=4, first=4, per_bank=2)
                attend(g, 1, 1)
                pe.wait_ge(v_v1.sem, v_v1.done(g))
                sum_self(g, 1, 0)
                sum_self(g, 1, 1)

                def out_transposed(g, name, post, per_b):
                    o = claim(pe, g, name)
                    for b in range(G):
                        pe.wait_ge(post.sem, post.at(g, per_b * (b + 1)))
                        for c in range(C):
                            m = nc.tensor.transpose(o[:, 0, (2 * c + b) * T:(2 * c + b + 1) * T], o_n[:, b, c * 128:(c + 1) * 128], ident[0:T, 0:T])
                    end(g, name, m)

                out_transposed(g, "oT1", v_post1, 3)
                pe.wait_ge(v_ot_lo.sem, v_ot_lo.done(g))
                natural(g, "proj", o_t, w["wp1"], 0)
                o = claim(pe, g, "xqT")
                for b in range(G):
                    pe.wait_ge(v_proj.sem, v_proj.at(g, 2 + 5 * b + 4))
                    for c in range(C):
                        m = nc.tensor.transpose(o[:, c, b * T:(b + 1) * T], xh[:, b, c * 128:(c + 1) * 128], ident[0:T, 0:T])
                end(g, "xqT", m)
                pe.wait_ge(p_xq_lo.sem, p_xq_lo.done(g))
                transposed_out(g, "q2", w["wq2"], 0, xs)
                pe.wait_ge(p_q2_lo.sem, p_q2_lo.done(g))
                pe.wait_ge(v_k2_lo.sem, v_k2_lo.done(g))

                def cross_max(g, b, i):
                    name = f"max2_{b}_{i}"
                    o = claim(pe, g, name)
                    c, e = (i % 4) // 2, i % 2
                    for n, (wp, ap) in enumerate(TERMS):
                        for jj in range(2):
                            r = 32 * (2 * (i // 4) + jj)
                            m = nc.tensor.matmul(o[0:T, jj, 0:SP], q[r:r + 32, wp, c, b, e, :], k2[r:r + 32, ap, c, b, :],
                                                 start=n == 0, stop=n == 2)
                    end(g, name, m)

                def cross_exp(g, b, i):
                    exp_scores(g, f"exp2_{b}_{i}", b, i % 2, ks_cross, i // 2, CH, 2)

                def cross_sum(g, b, i):
                    e_no = 8 + 6 * b + i
                    pe.wait_ge(a_exp.sem, a_exp.at(g, e_no + 1))
                    sum_values(g, e_no, b, i % 2, lambda hd: v2[:, b, i // 2, hd, :], CH, i == 0, i == 5)

                for i in range(8):
                    cross_max(g, 0, i)
                max_transpose(g, 2, 0)
                pe.wait_ge(v_maxt[2].sem, v_maxt[2].at(g, 2))
                pe.wait_ge(v_v2.sem, v_v2.done(g))
                for i in range(6):
                    cross_exp(g, 0, i)
                    cross_max(g, 1, i)
                    cross_sum(g, 0, i)
                cross_max(g, 1, 6)
                cross_max(g, 1, 7)
                max_transpose(g, 2, 1)
                pe.wait_ge(v_maxt[2].sem, v_maxt[2].at(g, 4))
                for i in range(6):
                    cross_exp(g, 1, i)
                    if i:
                        cross_sum(g, 1, i - 1)
                cross_sum(g, 1, 5)
                out_transposed(g, "oT2", v_post2, 2)
                pe.wait_ge(v_o2t_lo.sem, v_o2t_lo.done(g))
                pe.wait_ge(p_h_lo.sem, p_h_lo.done(g))
                natural(g, "y", o_t, w["wp2"], 0, more=[(h, w["w2"], FF)])

        @block.scalar
        def _(act):
            def two_heads(g, name, s, scale, bias):
                is_filled(act, g, name)
                o = granule(name)
                for c in range(C):
                    for e in range(2):
                        dst = q_tmp[:, c, :, e, :]
                        src = o[:, c, 0:G * T].rearrange("p (b t) -> p b t", b=G)
                        f = ACT.Identity if bias is None else ACT.Relu
                        bb = 0.0 if bias is None else bias[:, c, e:e + 1]
                        s.step(nc.scalar.activation(dst, src, f, bias=bb, scale=eo_scale[:, scale, e:e + 1]))

            def affine(g, name, s, dst, c, scale, bias, func=ACT.Identity):
                o = granule(name)
                s.step(nc.scalar.activation(dst, o[:, c, 0:G * T], func, bias=bias, scale=scale))

            def col(name, c):
                return vec[:, VEC[name] + c:VEC[name] + c + 1]

            def exponentials(g, name, e_no, bias, n_keys):
                is_filled(act, g, name)
                if e_no >= NP:
                    act.wait_ge(pv_done.sem, pv_done.at(g, e_no - NP + 1))
                o = granule(name)
                a_exp.step(nc.scalar.activation(
                    probs[0:n_keys, e_no % NP, :, :, :].rearrange("p j a t -> p j (a t)"),
                    o[0:n_keys, :, 0:4 * T], ACT.Exp, **({} if bias is None else {"bias": bias})))

            for s in act_back:
                act.sem_inc(s.sem, 1)
            act.wait_ge(const_loaded[0], 32)
            for i in range(2):
                nc.scalar.activation(eo_scale[:, i, :], vec[:, EO:EO + 2], ACT.Copy, scale=(0.25, 0.0625)[i]).then_inc(prep_act, 1)
            act.wait_ge(prep_act, 2)
            act.wait_ge(prep_dve, PREP_DVE)
            act.sem_inc(stored, 16)
            with act.Fori(0, NG) as g:
                act.wait_ge(p_q2_lo.sem, p_q2_lo.before(g))
                two_heads(g, "q0", a_q0, 0, bq0_eo)
                is_filled(act, g, "k0")
                for c in range(C):
                    affine(g, "k0", a_k0, k_tmp[:, c, :, :].rearrange("p b t -> p (b t)"), c, 1.0, col("bk0", c), ACT.Relu)
                act.wait_ge(p_ct_lo.sem, p_ct_lo.before(g))
                for b in range(G):
                    is_filled(act, g, f"ctxT{b}")
                    for c in range(C):
                        o = granule(f"ctxT{b}")
                        a_ct.step(nc.scalar.activation(ct_tmp[:, c, b, 0:S], o[:, c, 0:S], ACT.Identity, bias=col("b2", c), scale=col("g2", c)))

                def k2_hi(b):
                    is_filled(act, g, f"k2_{b}")
                    a_k2.step(nc.scalar.activation(k2[:, HI, :, b, :], granule(f"k2_{b}")[:, :, 0:SP], ACT.Copy))

                k2_hi(0)
                for m_ in range(2):
                    exponentials(g, f"exp0_0_{m_}", m_, pad0[:, 0:1], T)
                k2_hi(1)
                for m_ in range(2):
                    exponentials(g, f"exp0_1_{m_}", 2 + m_, pad0[:, 1:2], T)
                is_filled(act, g, "xT1")
                for dst, s_, b_ in ((n1_tmp, "g1", "b1"), (n3_tmp, "g3", "b3")):
                    for c in range(C):
                        affine(g, "xT1", a_n, dst[:, c, :, :].rearrange("p b t -> p (b t)"), c, col(s_, c), col(b_, c))
                act.wait_ge(p_q0_lo.sem, p_q0_lo.done(g))
                two_heads(g, "q1", a_q1, 1, None)
                is_filled(act, g, "k1")
                a_k1.step(nc.scalar.activation(k[:, HI, :, :, :].rearrange("p c b t -> p c (b t)"), granule("k1")[:, :, 0:G * T], ACT.Copy))

                def hidden(i0):
                    name = f"h{i0 // 4}"
                    is_filled(act, g, name)
                    for i in range(4):
                        a_h.step(nc.scalar.activation(h_tmp[:, i0 + i, :, :].rearrange("p b t -> p (b t)"),
                                                      granule(name)[:, i // 2, (i % 2) * G * T:(i % 2 + 1) * G * T], ACT.Relu,
                                                      bias=vec[:, FB1 + i0 + i:FB1 + i0 + i + 1]))

                hidden(0)
                for m_ in range(2):
                    exponentials(g, f"exp1_0_{m_}", 4 + m_, pad1[:, 0:1], T)
                hidden(4)
                for m_ in range(2):
                    exponentials(g, f"exp1_1_{m_}", 6 + m_, pad1[:, 1:2], T)

                def out_hi(name, s):
                    is_filled(act, g, name)
                    s.step(nc.scalar.activation(o_t[:, HI, :, :, :].rearrange("p c b t -> p (c b t)"), granule(name)[:, 0, 0:C * G * T], ACT.Copy))

                out_hi("oT1", a_ot)
                is_filled(act, g, "xqT")
                for c in range(C):
                    affine(g, "xqT", a_xq, n1_tmp[:, c, :, :].rearrange("p b t -> p (b t)"), c, col("g2", c), col("b2", c))
                act.wait_ge(p_q1_lo.sem, p_q1_lo.done(g))
                two_heads(g, "q2", a_q2, 1, None)
                for b in range(G):
                    for i in range(6):
                        exponentials(g, f"exp2_{b}_{i}", 8 + 6 * b + i, None, CH)
                out_hi("oT2", a_o2t)
                act.wait_ge(v_res.sem, v_res.done(g))
                act.dma_start(out_d[bass.ds(g * G, G), :, :].rearrange("b t f -> t b f"), res[:, :, :]).then_inc(stored, 16)

        @block.vector
        def _(dve):
            def after(s, g):
                dve.wait_ge(s.sem, s.at(g, s.given))

            def step(s, ins):
                s.step(ins)

            for s in dve_back:
                dve.sem_inc(s.sem, 1)
            dve.wait_ge(const_loaded[0], 32)
            nc.vector.tensor_scalar(pad1_all[:, :], mask_u8[:, :], BIG, None, ALU.mult).then_inc(prep_dve, 1)
            nc.vector.memset(v[1][:, :, :, :], 1.0).then_inc(prep_dve, 1)
            nc.vector.memset(v2[:, :, :, :, :], 1.0).then_inc(prep_dve, 1)
            nc.vector.memset(negmax_t[:, :, :], 0.0).then_inc(prep_dve, 1)
            nc.vector.memset(row, 0.0).then_inc(prep_dve, 1)
            nc.vector.memset(ones[:, :], 1.0).then_inc(flag_steps, 1)
            dve.wait_ge(first_loaded, 16)
            nc.vector.reduce_sum(first_sum[:, :], first_keys, AX.X).then_inc(flag_steps, 1)
            dve.wait_ge(flag_steps, 2)
            nc.vector.tensor_scalar(first_masked[:, :], first_sum[:, :], 0.0, None, ALU.is_equal).then_inc(flag_made, 1)
            dve.wait_ge(first_counted, 1)
            nc.vector.tensor_copy(any_masked[:, :], ring[0][0:1, 0, 0:1]).then_inc(flag_made, 1)
            dve.wait_ge(prep_act, 2)
            for e in range(2):
                nc.vector.tensor_scalar(bq0_eo[:, :, e], vec[:, VEC["bq0"]:VEC["bq0"] + C], eo_scale[:, 0, e:e + 1], None, ALU.mult).then_inc(prep_dve, 1)
            dve.wait_ge(const_loaded[2], 16 * len(rowv))
            nc.vector.tensor_tensor(rowv["bp2"][:, :], rowv["bp2"][:, :], rowv["fb2"][:, :], ALU.add).then_inc(prep_dve, 1)
            for n in wshape:
                dve.wait_ge(w_loaded[n], 16)
                nc.vector.tensor_copy(w[n][:, HI, :, :], w_raw_of[n]).then_inc(prep_dve, 1)
            dve.wait_ge(prep_pool, PREP_POOL)
            nc.vector.memset(ct_tmp[:, :, :, S:SP], 0.0).then_inc(prep_dve, 1)
            dve.wait_ge(prep_dve, PREP_DVE)
            dve.wait_ge(flag_made, 2)
            with dve.If(dve.value_load(any_masked[0:1, 0:1]) > 0):
                with dve.Fori(0, B) as b:
                    for ch in range(NCH):
                        dve.wait_ge(gen_values, b * NCH + ch + 1)
                        nc.vector.tensor_tensor(v2[:, 0, ch, :, 0:D], ring[1][0:CH, 0, 0:U].rearrange("p (h d) -> p h d", h=H),
                                                rowv["bv0"][:, :].rearrange("p (h d) -> p h d", h=H), ALU.add).then_inc(gen_ready, 1)
                        dve.wait_ge(gen_ready, b * (2 * NCH) + 2 * ch + 1)
                        nc.vector.tensor_scalar(v2[:, 0, ch, :, 0:D], v2[:, 0, ch, :, 0:D], 0.0, None, ALU.max).then_inc(gen_ready, 1)
                    dve.wait_ge(gen_summed, b + 1)
                    dve.wait_ge(v_all_stored, b * 16 + 16)
                    nc.vector.tensor_copy(row, ring[2][0:1, 0, 0:H * DV]).then_inc(gen_row, 1)
            with dve.Fori(0, NG) as g:
                dve.wait_ge(c_loaded, g * 32 + 32)
                dve.wait_ge(x_loaded, g * 80 + 80)
                mk = v_mask
                dve.wait_ge(a_exp.sem, a_exp.before(g))
                step(mk, nc.vector.reduce_sum(ksum[:, :], c_nat[0:T, :, 0, :], AX.X))
                step(mk, nc.vector.reduce_sum(qkeep[:, :], x_nat[:, :, :], AX.X))
                after(mk, g)
                step(mk, nc.vector.tensor_scalar(keep0[:, :], ksum[:, :], 0.0, None, ALU.not_equal))
                step(mk, nc.vector.tensor_scalar(keep0b[:, :], ksum[:, :], 0.0, None, ALU.not_equal))
                step(mk, nc.vector.tensor_scalar(pad0[:, :], ksum[:, :], 0.0, BIG, ALU.is_equal, ALU.mult))
                step(mk, nc.vector.tensor_scalar(qkeep[:, :], qkeep[:, :], 0.0, None, ALU.not_equal))
                step(mk, nc.vector.tensor_copy(pad1[:, :], pad1_all[:, bass.ds(g * G, G)]))
                after(mk, g)
                step(mk, nc.vector.tensor_scalar(keep1b[:, :], pad1[:, :], 0.0, None, ALU.is_equal))
                for b in range(G):
                    step(mk, nc.vector.tensor_scalar(add_mask[:, 0, b, :], causal[:, :], pad0[:, b:b + 1], None, ALU.min))
                    step(mk, nc.vector.tensor_scalar(add_mask[:, 1, b, :], causal[:, :], pad1[:, b:b + 1], None, ALU.min))
                xt2, ct2 = (t[:, :, :, :].rearrange("p c b t -> p (c b t)") for t in (x_t, c_t))
                step(v_xs_hi, nc.vector.tensor_copy(xs[:, HI].rearrange("p c b t -> p (c b t)"), xt2))
                step(v_xs_hi, nc.vector.tensor_copy(cs[:, HI].rearrange("p c b t -> p (c b t)"), ct2))
                cl = v_ctxln
                for i in range(G * NCH):
                    step(cl, nc.vector.bn_stats(stats[:, i, :], c_nat[:, i // NCH, i % NCH, :]))
                after(cl, g)
                alone(dve)
                for i in range(G * NCH):
                    step(cl, nc.vector.bn_aggr(mv[:, i, :], stats[:, i, :]))
                after(cl, g)
                step(cl, nc.vector.tensor_scalar(var_e[:, :], mv[:, :, 1], 1e-5, None, ALU.add))
                is_filled(dve, g, "cnt")
                o = granule("cnt")
                step(v_cnt, nc.vector.tensor_scalar(valid[:, :], o[0:T, 0, 0:G], 1.0, None, ALU.min))
                step(v_cnt, nc.vector.tensor_scalar(empty[:, :, :].rearrange("p b t -> p (b t)"), o[0:1, 1, 0:G * T], 0.0, None, ALU.is_equal))
                after(v_cnt, g)
                step(v_cnt, nc.vector.reciprocal(rvalid[:, :], valid[:, :]))
                after(v_cnt, g)
                step(v_cnt, nc.vector.tensor_tensor(nanf[:, :], valid[:, :], rvalid[:, :], ALU.mult))
                dve.wait_ge(p_rstd.sem, p_rstd.at(g, 1))
                for i in range(G * NCH):
                    step(cl, nc.vector.tensor_scalar(c_nat[0:CH, i // NCH, i % NCH, :], c_nat[:, i // NCH, i % NCH, :],
                                                     mv[:, i, 0:1], rstd[:, i:i + 1], ALU.subtract, ALU.mult))

                def high(s, a_s, dst, src, k_=None):
                    dve.wait_ge(a_s.sem, a_s.done(g) if k_ is None else a_s.at(g, k_))
                    step(s, nc.vector.tensor_copy(dst, src))

                def flat(t):
                    return t.rearrange("p c b t -> p (c b t)")

                qf = "p c b e t -> p (c b e t)"
                high(v_q0_hi, a_q0, q[:, HI].rearrange(qf), q_tmp[:, :, :, :, :].rearrange(qf))
                high(v_k0_hi, a_k0, flat(k[:, HI]), flat(k_tmp[:, :, :, :]))
                dve.wait_ge(stored, g * 16 + 16)
                is_filled(dve, g, "v0")
                o = granule("v0")
                step(v_v0, nc.vector.tensor_tensor(v_tmp[:, :, :], o[0:T, :, 0:U], rowv["bv0"][0:T, :].unsqueeze(1).to_broadcast([T, G, U]), ALU.add))
                after(v_v0, g)
                for b in range(G):
                    step(v_v0, nc.vector.tensor_copy(v[0][:, b, :, D], keep0[:, b:b + 1].to_broadcast([T, H])))
                    step(v_v0, nc.vector.tensor_scalar(v[0][:, b, :, 0:D], v_tmp[:, b, :].rearrange("p (h d) -> p h d", h=H), 0.0, keep0[:, b:b + 1], ALU.max, ALU.mult))
                for b in range(G):
                    high(v_ct_hi, a_ct, ct[:, HI, :, b, :], ct_tmp[:, :, b, :], 2 * b + 2)

                def self_maxima(layer, b):
                    for m_ in range(2):
                        name = f"max{layer}_{b}_{m_}"
                        is_filled(dve, g, name)
                        step(v_max[layer], nc.vector.tensor_reduce(
                            negmax[:, b, 8 * m_:8 * m_ + 8], granule(name)[0:T, :, 0:4 * T].rearrange("p j (a t) -> p j a t", a=4),
                            AX.X, ALU.max, negate=True))

                def max_rows(layer, b):
                    name = f"maxT{layer}_{b}"
                    is_filled(dve, g, name)
                    o = granule(name)
                    step(v_maxt[layer], nc.vector.tensor_copy(negmax_t[0:H, b, :], o[0:H, 0, 0:T]))
                    after(v_maxt[layer], g)
                    step(v_maxt[layer], nc.vector.tensor_tensor(negmax_t[32:32 + H, b, :], o[0:H, 0, 0:T], negmax_t[0:H, b, :], ALU.subtract))

                def k2_lo(b):
                    is_filled(dve, g, f"k2_{b}")
                    dve.wait_ge(a_k2.sem, a_k2.at(g, b + 1))
                    step(v_k2_lo, nc.vector.tensor_tensor(k2[:, LO, :, b, :], granule(f"k2_{b}")[:, :, 0:SP], k2[:, HI, :, b, :].bitcast(F32), ALU.subtract))

                self_maxima(0, 0)
                self_maxima(0, 1)
                k2_lo(0)
                max_rows(0, 0)
                k2_lo(1)
                max_rows(0, 1)
                for b in range(G):
                    is_filled(dve, g, f"v2_{b}")
                    step(v_v2, nc.vector.tensor_copy(v2[:, b, :, :, 0:D].rearrange("p n h d -> p n h d"),
                                                     granule(f"v2_{b}")[0:CH, :, :].rearrange("p j n -> p (j n)")[:, 0:NCH * U].rearrange("p (n h d) -> p n h d", n=NCH, h=H)))

                def statistics(s, src, b):
                    step(s, nc.vector.bn_stats(stats[0:T, b, :], src))
                    after(s, g)
                    alone(dve)
                    step(s, nc.vector.bn_aggr(mv[0:T, b, :], stats[0:T, b, :]))
                    after(s, g)

                def heads_out(s, b, flag):
                    acc = out_acc[b][0:T, 0:H * DV].rearrange("p (h d) -> p h d", h=H)
                    step(s, nc.vector.reciprocal(rden[:, b, :], acc[:, :, D]))
                    after(s, g)
                    if flag is not None:
                        step(s, nc.vector.tensor_scalar(rden[:, b, :], rden[:, b, :], flag[:, b:b + 1], None, ALU.mult))
                        after(s, g)
                    step(s, nc.vector.tensor_tensor(o_n[:, b, :].rearrange("p (h d) -> p h d", h=H), acc[:, :, 0:D],
                                                    rden[:, b, :].unsqueeze(2).to_broadcast([T, H, D]), ALU.mult))

                s = v_post0
                for b in range(G):
                    dve.wait_ge(pv_done.sem, pv_done.at(g, 2 * b + 2))
                    heads_out(s, b, qkeep)
                    after(s, g)
                    step(s, nc.vector.tensor_tensor(x1[:, b, :], o_n[:, b, :], x_nat[:, b, :], ALU.add))
                    after(s, g)
                    statistics(s, x1[:, b, :], b)
                    step(s, nc.vector.tensor_scalar(sd[:, b:b + 1], mv[0:T, b, 1:2], U / (U - 1), None, ALU.mult))
                    dve.wait_ge(p_rstd.sem, p_rstd.at(g, 2 + 2 * b))
                    step(s, nc.vector.tensor_scalar(sd[:, b:b + 1], sd_r[:, b:b + 1], 1e-8, None, ALU.add))
                    after(s, g)
                    step(s, nc.vector.reciprocal(sd_r[:, b:b + 1], sd[:, b:b + 1]))
                    after(s, g)
                    step(s, nc.vector.tensor_scalar(y[:, b, :], x1[:, b, :], mv[0:T, b, 0:1], sd_r[:, b:b + 1], ALU.subtract, ALU.mult))
                    after(s, g)
                    step(s, nc.vector.tensor_tensor(y[:, b, :], y[:, b, :], rowv["gamma0"][:, :], ALU.mult))
                    after(s, g)
                    step(s, nc.vector.tensor_tensor(x1[:, b, :], y[:, b, :], rowv["beta0"][:, :], ALU.add))
                    after(s, g)
                    statistics(s, x1[:, b, :], b)
                    step(s, nc.vector.tensor_scalar(var_e[0:T, b:b + 1], mv[0:T, b, 1:2], 1e-5, None, ALU.add))
                    dve.wait_ge(p_rstd.sem, p_rstd.at(g, 3 + 2 * b))
                    step(s, nc.vector.tensor_scalar(xh[:, b, :], x1[:, b, :], mv[0:T, b, 0:1], rstd[0:T, b:b + 1], ALU.subtract, ALU.mult))
                    step(s, nc.vector.tensor_tensor(x1[:, b, :], x1[:, b, :], rowv["bp1"][:, :], ALU.add))
                high(v_n_hi, a_n, flat(n1[:, HI]), flat(n1_tmp[:, :, :, :]), 2)
                high(v_n_hi, a_n, flat(n3[:, HI]), flat(n3_tmp[:, :, :, :]), 4)
                high(v_q1_hi, a_q1, q[:, HI].rearrange(qf), q_tmp[:, :, :, :, :].rearrange(qf))
                dve.wait_ge(a_k1.sem, a_k1.done(g))
                step(v_k1_lo, nc.vector.tensor_tensor(k[:, LO].rearrange("p c b t -> p c (b t)"), granule("k1")[:, :, 0:G * T], k[:, HI].bitcast(F32).rearrange("p c b t -> p c (b t)"), ALU.subtract))
                is_filled(dve, g, "v1")
                step(v_v1, nc.vector.tensor_copy(v[1][:, :, :, 0:D], granule("v1")[0:T, :, 0:U].rearrange("p b (h d) -> p b h d", h=H)))
                self_maxima(1, 0)
                self_maxima(1, 1)
                high(v_h_hi, a_h, h[:, HI, 0:4].rearrange("p c b t -> p (c b t)"), h_tmp[:, 0:4].rearrange("p c b t -> p (c b t)"), 4)
                max_rows(1, 0)
                high(v_h_hi, a_h, h[:, HI, 4:8].rearrange("p c b t -> p (c b t)"), h_tmp[:, 4:8].rearrange("p c b t -> p (c b t)"), 8)
                max_rows(1, 1)
                for b in range(G):
                    dve.wait_ge(pv_done.sem, pv_done.at(g, 4 + 2 * b + 2))
                    heads_out(v_post1, b, nanf)

                def out_lo(s, a_s, name):
                    dve.wait_ge(a_s.sem, a_s.done(g))
                    step(s, nc.vector.tensor_tensor(o_t[:, LO].rearrange("p c b t -> p (c b t)"), granule(name)[:, 0, 0:C * G * T],
                                                    o_t[:, HI].bitcast(F32).rearrange("p c b t -> p (c b t)"), ALU.subtract))

                out_lo(v_ot_lo, a_ot, "oT1")
                is_filled(dve, g, "proj")
                s = v_proj
                for b in range(G):
                    step(s, nc.vector.tensor_tensor(r1[:, b, :], granule("proj")[0:T, b, 0:U], x1[:, b, :], ALU.add))
                after(s, g)
                for b in range(G):
                    statistics(s, r1[:, b, :], b)
                    step(s, nc.vector.tensor_scalar(var_e[0:T, b:b + 1], mv[0:T, b, 1:2], 1e-5, None, ALU.add))
                    dve.wait_ge(p_rstd.sem, p_rstd.at(g, 2 + 2 * G + b))
                    step(s, nc.vector.tensor_scalar(xh[:, b, :], r1[:, b, :], mv[0:T, b, 0:1], rstd[0:T, b:b + 1], ALU.subtract, ALU.mult))
                    step(s, nc.vector.tensor_tensor(r1[:, b, :], r1[:, b, :], rowv["bp2"][:, :], ALU.add))
                high(v_xq_hi, a_xq, flat(xs[:, HI]), flat(n1_tmp[:, :, :, :]))
                high(v_q2_hi, a_q2, q[:, HI].rearrange(qf), q_tmp[:, :, :, :, :].rearrange(qf))
                for b in range(G):
                    for i in range(8):
                        name = f"max2_{b}_{i}"
                        is_filled(dve, g, name)
                        first = 8 * (i // 4) + i % 4
                        step(v_max[2], nc.vector.tensor_reduce(negmax[:, b, first:first + 5:4], granule(name)[0:T, :, 0:S], AX.X, ALU.max, negate=True))
                    max_rows(2, b)
                for b in range(G):
                    dve.wait_ge(pv_done.sem, pv_done.at(g, 8 + 6 * b + 6))
                    heads_out(v_post2, b, None)
                out_lo(v_o2t_lo, a_o2t, "oT2")
                is_filled(dve, g, "y")
                step(v_res, nc.vector.tensor_tensor(res[:, :, :], granule("y")[0:T, :, 0:U], r1[:, :, :], ALU.add))

        @block.gpsimd
        def _(pool):
            def low(s, v_s, dst, src, hi, g, k_=None):
                pool.wait_ge(v_s.sem, v_s.done(g) if k_ is None else v_s.at(g, k_))
                s.step(nc.gpsimd.tensor_tensor(dst, src, hi.bitcast(F32), ALU.subtract))

            for s in pool_back:
                pool.sem_inc(s.sem, 1)
            nc.gpsimd.memset(half[:, 0:G * NCH], -0.5).then_inc(prep_pool, 1)
            nc.gpsimd.memset(half[:, G * NCH:2 * G * NCH], 0.5).then_inc(prep_pool, 1)
            for i, n in enumerate(wshape):
                pool.wait_ge(prep_dve, 8 + i + 1)
                nc.gpsimd.tensor_tensor(w[n][:, LO, :, :], w_raw_of[n], w[n][:, HI, :, :].bitcast(F32), ALU.subtract).then_inc(prep_pool, 1)
            with pool.Fori(0, NG) as g:
                def power(out, in_, neg, n):
                    base = 0 if neg else G * NCH
                    p_rstd.step(nc.gpsimd.tensor_tensor(out, in_, half[0:out.shape[0], base:base + n], ALU.pow))

                def f4(t):
                    return t.rearrange("p c b t -> p (c b t)")

                qf = "p c b e t -> p (c b e t)"
                low(p_xs_lo, v_xs_hi, f4(xs[:, LO]), f4(x_t[:, :, :, :]), f4(xs[:, HI]), g, 1)
                low(p_xs_lo, v_xs_hi, f4(cs[:, LO]), f4(c_t[:, :, :, :]), f4(cs[:, HI]), g, 2)
                pool.wait_ge(v_ctxln.sem, v_ctxln.at(g, 2 * G * NCH + 1))
                power(rstd[:, :], var_e[:, :], True, G * NCH)
                low(p_q0_lo, v_q0_hi, q[:, LO].rearrange(qf), q_tmp[:, :, :, :, :].rearrange(qf), q[:, HI].rearrange(qf), g)
                low(p_k0_lo, v_k0_hi, f4(k[:, LO]), f4(k_tmp[:, :, :, :]), f4(k[:, HI]), g)
                for b in range(G):
                    low(p_ct_lo, v_ct_hi, ct[:, LO, :, b, :], ct_tmp[:, :, b, :], ct[:, HI, :, b, :], g, b + 1)

                for b in range(G):
                    pool.wait_ge(v_post0.sem, v_post0.at(g, OUT0 * b + 7))
                    power(sd_r[:, b:b + 1], sd[:, b:b + 1], False, 1)
                    pool.wait_ge(v_post0.sem, v_post0.at(g, OUT0 * b + 15))
                    power(rstd[0:T, b:b + 1], var_e[0:T, b:b + 1], True, 1)
                low(p_n_lo, v_n_hi, f4(n1[:, LO]), f4(n1_tmp[:, :, :, :]), f4(n1[:, HI]), g, 1)
                low(p_n_lo, v_n_hi, f4(n3[:, LO]), f4(n3_tmp[:, :, :, :]), f4(n3[:, HI]), g, 2)
                low(p_q1_lo, v_q1_hi, q[:, LO].rearrange(qf), q_tmp[:, :, :, :, :].rearrange(qf), q[:, HI].rearrange(qf), g)
                low(p_h_lo, v_h_hi, f4(h[:, LO, 0:4]), f4(h_tmp[:, 0:4]), f4(h[:, HI, 0:4]), g, 1)
                low(p_h_lo, v_h_hi, f4(h[:, LO, 4:8]), f4(h_tmp[:, 4:8]), f4(h[:, HI, 4:8]), g, 2)
                for b in range(G):
                    pool.wait_ge(v_proj.sem, v_proj.at(g, 2 + 5 * b + 3))
                    power(rstd[0:T, b:b + 1], var_e[0:T, b:b + 1], True, 1)
                low(p_xq_lo, v_xq_hi, f4(xs[:, LO]), f4(n1_tmp[:, :, :, :]), f4(xs[:, HI]), g)
                low(p_q2_lo, v_q2_hi, q[:, LO].rearrange(qf), q_tmp[:, :, :, :, :].rearrange(qf), q[:, HI].rearrange(qf), g)

        for name, s in sig.items():
            assert s.given == s.per, (name, s.given, s.per)


def kernel(**inputs):
    import concourse.bacc as bacc
    from concourse.bass_utils import run_bass_kernel_spmd

    a = {n: np.asarray(x) for n, x in inputs.items()}

    def layer(prefix, n):
        return a[prefix + n]

    cols = lambda x: np.ascontiguousarray(x.reshape(-1, 128).T)
    t = np.ascontiguousarray
    rows = np.arange(128)
    even = ((rows // D) % 2 == 0).astype(np.float32)[:, None]
    vec = np.concatenate([cols(a[n]) for n in (
        "L0_xattn_bq", "L0_xattn_bk", "L1_xattn_ln1_g", "L1_xattn_ln1_b", "L1_xattn_ln3_g", "L1_xattn_ln3_b",
        "L1_xattn_ln2_g", "L1_xattn_ln2_b", "L1_xattn_ff_b1")] + [even, 1 - even], axis=1)
    sel = np.zeros((48, H), np.float32)
    for r in range(H):
        sel[[r, 32 + r], r] = 1.0
    kq = np.arange(T)[:, None] <= np.arange(T)[None, :]
    bf = mybir.dt.np(BF16)
    data = {
        "x": t(a["x"]), "x_t": t(a["x"].reshape(B * T, U).T),
        "ctx": t(a["ctx_1024"]), "ctx_t": t(a["ctx_1024"].reshape(B * S, U).T),
        "mask": t(a["mask_BxS_bf0"].T), "vec": t(vec),
        "w_wq0": t(a["L0_xattn_Wq"].T), "w_wk0": t(a["L0_xattn_Wk"].T), "w_wv0": t(a["L0_xattn_Wv"].T),
        "w_wqkv1": t(a["L1_xattn_sa_wqkv"]), "w_wp1": t(a["L1_xattn_sa_wproj"]), "w_wq2": t(a["L1_xattn_ed_wq"]),
        "w_wkv2": t(a["L1_xattn_ed_wkv"]), "w_wp2": t(a["L1_xattn_ed_wproj"]), "w_w1": t(a["L1_xattn_ff_w1"]),
        "w_w2": t(a["L1_xattn_ff_w2"]),
        "r_bv0": t(a["L0_xattn_bv"]), "r_gamma0": t(a["L0_xattn_gamma"]), "r_beta0": t(a["L0_xattn_beta"]),
        "r_bp1": t(a["L1_xattn_sa_bproj"]), "r_bp2": t(a["L1_xattn_ed_bproj"]), "r_fb2": t(a["L1_xattn_ff_b2"]),
        "c_ident": np.eye(128, dtype=np.float32), "c_ident_b": np.eye(T).astype(bf),
        "c_causal": np.where(kq, 0.0, BIG).astype(bf), "c_causal2": np.where(kq, 0.0, 2 * BIG).astype(bf), "c_tril": kq.astype(bf), "c_select": sel.astype(bf),
    }
    nc = bacc.Bacc("TRN2", target_bir_lowering=False, num_devices=1)
    d = {n: nc.dram_tensor("in_" + n, x.shape, mybir.dt.from_np(x.dtype), kind="ExternalInput").ap() for n, x in data.items()}
    out = nc.dram_tensor("out", [B, T, U], F32, kind="ExternalOutput").ap()

    def group(prefix):
        return {n[len(prefix):]: ap for n, ap in d.items() if n.startswith(prefix)}

    build(nc, d["x"], d["x_t"], d["ctx"], d["ctx_t"], d["ctx"][:, 0, :], d["mask"], group("w_"), d["vec"], group("r_"), group("c_"), out)
    r = run_bass_kernel_spmd(nc, [{"in_" + n: x for n, x in data.items()}], core_ids=[0])
    return r.results[0]["out"]
```

```python
from contextlib import ExitStack

import numpy as np

import concourse.bass as bass
from concourse import mybir

F32 = mybir.dt.float32
F32R = mybir.dt.float32r
BF16 = mybir.dt.bfloat16
I32 = mybir.dt.int32
U8 = mybir.dt.uint8
ALU = mybir.AluOpType
ACT = mybir.ActivationFunctionType
AX = mybir.AxisListType

B, T, S, U, H = 8, 112, 375, 256, 16
D = U // H
C = U // 128
FF = 4 * U // 128
G = 2
NG = B // G
NCH, CH = 3, 125
SP = 376
DV = D + 1
BIG = -float(2 ** 100)
HI, LO = 0, 1


class Signal:

    def __init__(self, sem, per, owner, order):
        self.sem, self.per, self.given, self.owner, self.order = sem, per, 0, owner, order
        self.start = 0

    def at(self, g, k):
        return g * self.per + (k + self.start)

    def done(self, g):
        return self.at(g, self.per)

    def before(self, g):
        return self.at(g, 0)

    def step(self, instruction):
        self.given += 1
        instruction.then_inc(self.sem, 1)


class Part:

    def __init__(self, order, first_job, per_turn=0):
        self.order, self.first_job, self.per_turn = order, first_job, per_turn
        self.jobs = [j for step in order for j in JOBS_OF.get(step, ())]
        self.number = {name: i for i, name in enumerate(self.jobs)}


A_STEPS = (["A.masks", "A.q0", "A.k0", "A.v0"] + [f"A.max0_{b}" for b in range(G)]
           + [f"A.{s}" for s in ("top0_0", "exp0_0", "top0_1", "sum0_0", "exp0_1", "out0_0", "sum0_1", "out0_1")]
           + ["A.xT", "A.q1", "A.k1", "A.v1"] + [f"A.max1_{b}" for b in range(G)]
           + [f"A.{s}" for s in ("top1_0", "exp1_0", "top1_1", "sum1_0", "exp1_1", "out1_0", "sum1_1", "out1_1")]
           + ["A.oT", "A.proj", "A.xqT"])
B_STEPS = (["B.q2", "B.norm", "B.h0", "B.scale", "B.h1"] + [f"B.cT_{b}" for b in range(G)] + [f"B.k2_{b}" for b in range(G)]
           + [f"B.v2_{b}" for b in range(G)] + [f"B.max_0_{i}" for i in range(8)] + ["B.top_0"]
           + [s for i in range(6) for s in (f"B.exp_0_{i}", f"B.max_1_{i}", f"B.sum_0_{i}")]
           + ["B.out_0", "B.max_1_6", "B.max_1_7", "B.top_1"]
           + [s for i in range(6) for s in (f"B.exp_1_{i}", f"B.sum_1_{i - 1}") if "-" not in s]
           + ["B.sum_1_5", "B.out_1", "B.oT", "B.y"])
COST = {"A.masks": 1, "A.q0": 15, "A.k0": 15, "A.v0": 17, "A.max": 38, "A.top": 2, "A.exp": 45, "A.sum": 30, "A.out": 20,
        "A.xT": 10, "A.q1": 13, "A.k1": 13, "A.v1": 13, "A.oT": 8, "A.proj": 13, "A.xqT": 8,
        "B.q2": 13, "B.h": 26, "B.norm": 0, "B.scale": 0, "B.cT": 12, "B.k2": 19, "B.v2": 19, "B.max": 10, "B.top": 2, "B.exp": 17,
        "B.sum": 15, "B.out": 8, "B.oT": 8, "B.y": 64}


def cost(step):
    return max((len(k), v) for k, v in COST.items() if step.startswith(k))[1]


def mixed(a_steps, b_steps, lead):
    def placed(steps, off, span):
        total, at, out = sum(map(cost, steps)), 0, []
        for s in steps:
            out.append((off + span * at / total, s))
            at += cost(s)
        return out
    return [s for _, s in sorted(placed(a_steps, lead, 1 - lead) + placed(b_steps, 0, 1.0), key=lambda x: x[0])]


JOBS_OF = {"A.masks": ("counts",), "A.q0": ("q0",), "A.k0": ("k0",), "A.v0": ("v0",), "A.xT": ("xT",), "A.q1": ("q1",),
           "A.k1": ("k1",), "A.v1": ("v1",), "A.oT": ("oT1",), "A.proj": ("proj",), "A.xqT": ("xqT",), "B.q2": ("q2",),
           "B.h0": ("h0",), "B.h1": ("h1",), "B.oT": ("oT2",), "B.y": ("y",)}
for b_ in range(G):
    for l_ in range(2):
        JOBS_OF[f"A.max{l_}_{b_}"] = tuple(f"max{l_}_{b_}_{m}" for m in range(2))
        JOBS_OF[f"A.exp{l_}_{b_}"] = tuple(f"exp{l_}_{b_}_{m}" for m in range(2))
        JOBS_OF[f"A.top{l_}_{b_}"] = (f"top{l_}_{b_}",)
        JOBS_OF[f"A.out{l_}_{b_}"] = (f"out{l_}_{b_}",)
    JOBS_OF[f"B.top_{b_}"] = (f"top2_{b_}",)
    JOBS_OF[f"B.out_{b_}"] = (f"out2_{b_}",)
    for n_ in ("cT", "k2", "v2"):
        JOBS_OF[f"B.{n_}_{b_}"] = (f"{n_}_{b_}",)
    for i_ in range(8):
        JOBS_OF[f"B.max_{b_}_{i_}"] = (f"max2_{b_}_{i_}",)
    for i_ in range(6):
        JOBS_OF[f"B.exp_{b_}_{i_}"] = (f"exp2_{b_}_{i_}",)
LEAD = 0.04


def build(nc, x_nat_d, x_t_d, c_nat_d, c_t_d, c_first_d, mask_d, w_d, vec_d, row_d, const_d, out_d):
    ctx = ExitStack()
    with ctx:
        def sb(name, shape, dt=F32):
            return ctx.enter_context(nc.sbuf_tensor(name, shape, dt))

        def sem(name):
            return ctx.enter_context(nc.semaphore(name))

        w0 = {n: sb(n, [128, C, U]) for n in ("wq0", "wk0", "wv0")}
        wshape = {"wqkv1": (C, 3 * U), "wp1": (C, U), "wq2": (C, U), "wkv2": (C, 2 * U), "wp2": (C, U),
                  "w1": (C, 4 * U), "w2": (FF, U)}
        w = {n: sb(n, [128, 2, *s], F32R) for n, s in wshape.items()}
        late = ("w1", "w2")
        raw_cols = max(sum(a * b for n, (a, b) in wshape.items() if (n in late) == l) for l in (False, True))
        w_raw = sb("w_raw", [128, raw_cols])
        w_raw_of, at = {}, 0
        for n, (a, b) in wshape.items():
            at = 0 if n == late[0] else at
            w_raw_of[n] = w_raw[:, at:at + a * b].rearrange("p (a b) -> p a b", a=a)
            at += a * b
        spare = [0]

        def over_raw(*shape):
            n = int(np.prod(shape))
            at_, spare[0] = spare[0], spare[0] + n
            assert spare[0] <= raw_cols
            names_ = "abcde"[:len(shape)]
            return w_raw[:, at_:at_ + n].rearrange(f"p ({' '.join(names_)}) -> p {' '.join(names_)}", **dict(zip(names_, shape)))

        vec = sb("vec", [128, vec_d.shape[1]])
        names = ["bq0", "bk0", "g1", "b1", "g3", "b3", "g2", "b2"]
        VEC = {n: 2 * i for i, n in enumerate(names)}
        FB1 = 2 * len(names)
        EO = FB1 + FF
        rowv = {n: sb(n, [T if n != "bv0" else CH, U]) for n in ("bv0", "gamma0", "beta0", "bp1", "bp2")}
        ident = sb("ident", [128, 128])
        ident_b = sb("ident_b", [T, T], BF16)
        causal = sb("causal", [T, T], BF16)
        causal2 = sb("causal2", [T, T], BF16)
        tril = sb("tril", [T, T], BF16)
        select = sb("select", [48, H], BF16)
        mask_u8 = sb("mask_u8", [T, B], U8)
        pad1_all = sb("pad1_all", [T, B])
        eo_scale = sb("eo_scale", [128, 2, 2])
        bq0_eo = sb("bq0_eo", [128, C, 2])
        ones = sb("ones", [128, 1])

        x_nat = sb("x_nat", [T, G, U])
        x_t = sb("x_t", [128, C, G, T])
        c_nat = sb("c_nat", [CH, G, NCH, U])
        c_t = sb("c_t", [128, C, G, T])
        qf = over_raw(C, G, 2, T)
        kf = over_raw(C, G, T)
        v = [sb(f"v{i}", [T, G, H, DV]) for i in range(2)]
        n1 = sb("n1", [128, 2, C, G, T], F32R)
        n3 = sb("n3", [128, 2, C, G, T], F32R)
        n_tmp = over_raw(2, C, G, T)
        o_t = [sb(f"o_t{i}", [128, 2, C, G, T], F32R) for i in range(2)]
        q2_tmp = n_tmp.rearrange("p a c b t -> p (a c b t)").rearrange("p (c b e t) -> p c b e t", c=C, b=G, e=2)
        q2 = sb("q2", [128, 2, C, G, 2, T], F32R)
        ct_tmp = over_raw(C, SP)
        ct = sb("ct", [128, 2, C, G, SP], F32R)
        k2 = sb("k2", [128, 2, C, G, SP], F32R)
        v2 = sb("v2", [CH, G, NCH, H, DV])
        h_tmp = over_raw(4, G, T)
        h = sb("h", [128, 2, FF, G, T], F32R)
        NP = 2
        probs = [sb(f"probs{i}", [T if i == 0 else CH, NP, 2, 4, T]) for i in range(2)]
        negmax = [sb(f"negmax{i}", [T, G, H]) for i in range(2)]
        negmax_t = [sb(f"negmax_t{i}", [48, G, T], BF16) for i in range(2)]
        acc_sb = [sb(f"acc_sb{i}", [128, 4, T]) for i in range(2)]

        keep0 = sb("keep0", [T, G]); keep0b = sb("keep0b", [T, G], BF16)
        pad0 = sb("pad0", [T, G]); pad1 = sb("pad1", [T, G]); keep1b = sb("keep1b", [T, G], BF16)
        qkeep = sb("qkeep", [T, G]); ksum = sb("ksum", [T, G]); qsum = sb("qsum", [T, G])
        add_mask = sb("add_mask", [T, 2, G, T], BF16)
        valid = sb("valid", [T, G]); rvalid = sb("rvalid", [T, G]); nanf = sb("nanf", [T, G])
        empty = sb("empty", [1, G, T])
        v_all_g = sb("v_all_g", [1, G, H * DV])
        first_keys = x_nat[0:B, 0, :]
        first_sum = sb("first_sum", [B, 1]); first_masked = sb("first_masked", [B, 1])
        any_masked = sb("any_masked", [1, 1], I32)
        gen_c = x_t[:, :, :, :].rearrange("p c b t -> p (c b t)")[:, 0:C * CH].rearrange("p (c k) -> p c k", c=C)
        c_stats = sb("c_stats", [CH, G * NCH, 6]); c_mv = sb("c_mv", [CH, G * NCH, 2])
        c_rstd = sb("c_rstd", [CH, G * NCH]); c_var = sb("c_var", [CH, G * NCH]); half = sb("half", [CH, 2 * G * NCH])
        stats = sb("stats", [T, G, 6]); mv = sb("mv", [T, G, 2]); rstd = sb("rstd", [T, G]); var_e = sb("var_e", [T, G])
        rden = [sb(f"rden{i}", [T, G, H]) for i in range(2)]
        o_n = [sb(f"o_n{i}", [T, G, U]) for i in range(2)]
        key_nat = o_n[0]
        x1 = sb("x1", [T, G, U]); r1 = sb("r1", [T, G, U])
        sd = sb("sd", [T, G]); sd_r = sb("sd_r", [T, G]); xh = sb("xh", [T, G, U])
        y = v_tmp = xh
        res = o_n[1]
        row = xh[0:1, :, :].rearrange("p b u -> p (b u)")[:, 0:H * DV]
        rowv["fb2"] = x1[:, 0, :]

        NR = 3
        ring = [ctx.enter_context(nc.psum_tensor(f"ring{i}", [128, 2, 512], F32)) for i in range(NR)]
        acc = [ctx.enter_context(nc.psum_tensor(f"acc{i}", [128, 4, 128], F32)) for i in range(2)]

        PREP_SPLIT = 11
        PREP_DVE, PREP_POOL = PREP_SPLIT + len(wshape) + 1, 2 + len(wshape)
        prep_act = sem("prep_act"); prep_dve = sem("prep_dve"); prep_pool = sem("prep_pool")
        x_loaded, c_loaded, stored = sem("x_loaded"), sem("c_loaded"), sem("stored")
        v_all_stored, first_loaded, first_counted, flag_made = sem("v_all_stored"), sem("first_loaded"), sem("first_counted"), sem("flag_made")
        flag_steps = sem("flag_steps")
        gen_loaded, gen_values, gen_ready, gen_summed, gen_row = (sem(n) for n in ("gen_loaded", "gen_values", "gen_ready", "gen_summed", "gen_row"))
        v_all_d = nc.dram_tensor("v_all", [B, H * DV], F32).ap()
        const_loaded = [sem(f"const_loaded{i}") for i in range(3)]
        w_loaded = {n: sem("loaded_" + n) for n in wshape}
        w0_loaded = sem("w0_loaded")
        waited = {e.engine: sem(n) for n, e in (("waited_sp", nc.sync), ("waited_dve", nc.vector), ("waited_pool", nc.gpsimd))}
        sig = {}
        OUT0 = 17

        def signal(name, per):
            sig[name] = Signal(sem(name), per, owner[0], len(sig))
            return sig[name]

        owner = [None]

        owner[0] = "scalar"
        a_q0 = signal("q0_biased", 4); a_k0 = signal("k0_biased", 2); a_q1 = signal("q1_scaled", 4); a_k1 = signal("k1_copied", 1)
        a_n = signal("norm13_scaled", 4); a_expA = signal("exponentialsA", 8); a_accA = signal("outputsA_copied", 2 * G)
        a_ot = signal("out1_hi", 1); a_xq = signal("norm2_scaled", 2)
        a_q2 = signal("q2_scaled", 4); a_h = signal("hidden_biased", FF); a_ct = signal("ctx_scaled", 2 * G)
        a_k2 = signal("k2_hi", G); a_expB = signal("exponentialsB", 6 * G); a_accB = signal("outputsB_copied", G); a_o2t = signal("out2_hi", 1)
        owner[0] = "vector"
        v_mask = signal("masks_made", 8 + 2 * G); v_cnt = signal("counts_read", 4); v_v0 = signal("values0", 1 + 2 * G)
        v_max = [signal(f"max{a}", n) for a, n in enumerate((2 * G, 2 * G, 8 * G))]
        v_top = [signal(f"max_t{a}", 2 * G) for a in range(3)]
        v_post0 = signal("out0_steps", OUT0 * G); v_n_hi = signal("norm13_hi", 2); v_v1 = signal("values1", 1)
        v_post1 = signal("out1_steps", 3 * G); v_ot_lo = signal("out1_lo", 1)
        v_proj = signal("proj_steps", G + 4 * G); v_xq_hi = signal("norm2_hi", 1); v_r1 = signal("residual_made", 1)
        v_q2_hi = signal("q2_hi", 1); v_h_hi = signal("hidden_hi", 2)
        v_ctxln = signal("ctx_normed", 3 * G * NCH + 1); v_ct_hi = signal("ctx_hi", G); v_k2_lo = signal("k2_lo", G); v_v2 = signal("values2", G)
        v_post2 = signal("out2_steps", 2 * G); v_o2t_lo = signal("out2_lo", 1); v_res = signal("result", 1)
        owner[0] = "gpsimd"
        p_rstd = signal("rstd", 3 * G); p_n_lo = signal("norm13_lo", 2); p_xq_lo = signal("norm2_lo", 1)
        p_q2_lo = signal("q2_lo", 1); p_h_lo = signal("hidden_lo", 2); p_crstd = signal("ctx_rstd", 1); p_ct_lo = signal("ctx_lo", G)
        owner[0] = "tensor"
        t_pvA = signal("values_summedA", 8); t_pvB = signal("values_summedB", 6 * G)
        psum_filled = sem("psum_filled")

        READER = {"counts": (v_cnt, 2), "q0": (a_q0, 4), "k0": (a_k0, 2), "v0": (v_v0, 1), "xT": (a_n, 4),
                  "q1": (a_q1, 4), "k1": (a_k1, 1), "v1": (v_v1, 1), "oT1": (v_ot_lo, 1), "proj": (v_proj, G), "xqT": (a_xq, 2),
                  "q2": (a_q2, 4), "h0": (a_h, 4), "h1": (a_h, 8), "oT2": (v_o2t_lo, 1), "y": (v_res, 1)}
        for b in range(G):
            for l in range(2):
                for m in range(2):
                    READER[f"max{l}_{b}_{m}"] = (v_max[l], 2 * b + m + 1)
                    READER[f"exp{l}_{b}_{m}"] = (a_expA, 4 * l + 2 * b + m + 1)
            for l in range(3):
                READER[f"top{l}_{b}"] = (v_top[l], 2 * b + 2)
            READER[f"out0_{b}"] = (v_post0, OUT0 * b + 3)
            READER[f"out1_{b}"] = (v_post1, 3 * b + 3)
            READER[f"out2_{b}"] = (v_post2, 2 * b + 2)
            READER[f"cT_{b}"] = (a_ct, 2 * b + 2)
            READER[f"k2_{b}"] = (v_k2_lo, b + 1)
            READER[f"v2_{b}"] = (v_v2, b + 1)
            for i in range(8):
                READER[f"max2_{b}_{i}"] = (v_max[2], 8 * b + i + 1)
            for i in range(6):
                READER[f"exp2_{b}_{i}"] = (a_expB, 6 * b + i + 1)
        B_JOBS = {j for s in B_STEPS for j in JOBS_OF.get(s, ())}

        first = Part(A_STEPS, 0)
        order = mixed(A_STEPS, B_STEPS, LEAD)
        body = Part(order, len(first.jobs), sum(len(JOBS_OF.get(s, ())) for s in order))
        last = Part(B_STEPS, len(first.jobs) + (NG - 1) * len(body.jobs))
        assert max(order.index(s) for s in ("B.q2", "B.h0", "B.h1")) < order.index("A.xT")
        assert order.index("B.q2") < order.index("A.out0_0")

        def home(part, name):
            return ring[part.number[name] % NR]

        def filled_at(part, i, name):
            return i * part.per_turn + (part.first_job + part.number[name] + 1)

        class At:

            def __init__(self, part, i, a, b):
                self.part, self.i, self.a, self.b = part, i, a, b

            def pair(self, name):
                return self.b if name in B_JOBS else self.a

        def is_filled(eng, at, name):
            eng.wait_ge(psum_filled, filled_at(at.part, at.i, name))
            return home(at.part, name)

        def claim(pe, at, name):
            n = at.part.number[name]
            if n >= NR:
                before = at.part.jobs[n - NR]
                s, k = READER[before]
                pe.wait_ge(s.sem, s.at(at.pair(before), k))
                return home(at.part, name)
            for part in {first: (), body: (first, body), last: (body,)}[at.part]:
                before = [j for j in part.jobs if part.number[j] % NR == n][-1]
                s, k = READER[before]
                if before in B_JOBS:
                    pe.wait_ge(s.sem, s.before(at.b))
                else:
                    pe.wait_ge(s.sem, s.done(at.a - 1) if at.part is not last else s.done(NG - 1))
            return home(at.part, name)

        def alone(eng):
            eng.sem_inc(waited[eng.engine], 1)

        made = set()

        def run(eng, steps):
            def go(at):
                for s in sig.values():
                    s.given = 0
                for name in at.part.order:
                    stage, rest = name.split(".")
                    kind, *idx = rest.split("_")
                    if f"{stage}.{kind}" in steps:
                        steps[f"{stage}.{kind}"](at, at.a if stage == "A" else at.b, *map(int, idx))
                for name, s in sig.items():
                    assert s.given in (0, s.per), (name, s.given, s.per)
                    made.update([name] if s.given else [])

            go(At(first, 0, 0, None))
            with eng.Fori(0, NG - 1) as i:
                go(At(body, i, i + 1, i))
            go(At(last, 0, None, NG - 1))

        back = {READER[body.jobs[-1 - n]][0] for n in range(NR) if body.jobs[-1 - n] in B_JOBS}
        back |= {a_expA, a_accA, a_xq, p_h_lo, p_ct_lo, a_accB}
        for s in back:
            s.start = 1

        def start_signals(eng, letter):
            for s in sorted((s for s in back if s.owner == letter), key=lambda s: s.order):
                eng.sem_inc(s.sem, 1)

        TERMS = ((HI, HI), (HI, LO), (LO, HI))
        block = ctx.enter_context(nc.Block())

        @block.sync
        def _(sp):
            sp.dma_start(vec[:, :], vec_d).then_inc(const_loaded[0], 16)
            sp.dma_start(mask_u8[:, :], mask_d).then_inc(const_loaded[0], 16)
            sp.dma_start(first_keys, c_first_d).then_inc(first_loaded, 16)
            for n, dst in (("causal", causal), ("causal2", causal2), ("tril", tril), ("ident_b", ident_b), ("select", select), ("ident", ident)):
                sp.dma_start(dst[:, :], const_d[n]).then_inc(const_loaded[1], 16)
            for n in w0:
                sp.dma_start(w0[n][:, :, :], w_d[n].rearrange("(a p) b -> p a b", p=128)).then_inc(w0_loaded, 16)
            for n in rowv:
                sp.dma_start(rowv[n][:, :], row_d[n].unsqueeze(0).to_broadcast([rowv[n].shape[0], U])).then_inc(const_loaded[2], 16)
            for n in wshape:
                if n == late[0]:
                    sp.wait_ge(prep_pool, 2 + len(wshape) - len(late))
                sp.dma_start(w_raw_of[n], w_d[n].rearrange("(a p) b -> p a b", p=128)).then_inc(w_loaded[n], 16)
            sp.wait_ge(prep_dve, 6)
            sp.dma_start(v_all_d.rearrange("b n -> (b n)").unsqueeze(0).rearrange("p (b n) -> p b n", b=B),
                         row.unsqueeze(1).to_broadcast([1, B, H * DV])).then_inc(v_all_stored, 16)
            sp.wait_ge(v_all_stored, 16)
            sp.wait_ge(flag_made, 2)
            with sp.If(sp.value_load(any_masked[0:1, 0:1]) > 0):
                with sp.Fori(0, B) as b:
                    for ch in range(NCH):
                        if ch:
                            sp.wait_ge(gen_values, b * NCH + ch)
                            alone(sp)
                        sp.dma_start(gen_c, c_t_d.rearrange("(c p) t -> p c t", p=128)[:, :, bass.ds(b * S + ch * CH, CH)]).then_inc(gen_loaded, 16)
                    sp.wait_ge(gen_row, b + 1)
                    alone(sp)
                    sp.dma_start(v_all_d[bass.ds(b, 1), :], row).then_inc(v_all_stored, 16)
                    sp.wait_ge(v_all_stored, b * 16 + 32)
                    alone(sp)

            def load_x(g, look_back):
                if look_back:
                    sp.wait_ge(a_q0.sem, a_q0.done(g - 1))
                    alone(sp)
                    sp.wait_ge(a_k0.sem, a_k0.done(g - 1))
                    alone(sp)
                    sp.wait_ge(v_v0.sem, v_v0.done(g - 1))
                    alone(sp)
                    sp.wait_ge(v_post0.sem, v_post0.done(g - 1))
                    alone(sp)
                sp.dma_start(x_t[:, :, :, :].rearrange("p c b t -> p c (b t)"),
                             x_t_d.rearrange("(c p) t -> p c t", p=128)[:, :, bass.ds(g * (G * T), G * T)]).then_inc(x_loaded, 16)
                for b in range(G):
                    sp.dma_start(c_t[:, :, b, :], c_t_d.rearrange("(c p) t -> p c t", p=128)[:, :, bass.ds(g * (G * S) + b * S, T)]).then_inc(x_loaded, 16)
                sp.dma_start(x_nat[:, :, :], x_nat_d[bass.ds(g * G, G), :, :].rearrange("b t f -> t b f")).then_inc(x_loaded, 16)
                sp.dma_start(v_all_g[:, :, :], v_all_d[bass.ds(g * G, G), :].unsqueeze(0)).then_inc(x_loaded, 16)
                if look_back:
                    sp.wait_ge(a_ot.sem, a_ot.done(g - 1))
                    alone(sp)
                sp.dma_start(key_nat[:, :, :], c_nat_d[bass.ds(g * G, G), 0:T, :].rearrange("b t f -> t b f")).then_inc(x_loaded, 16)

            def load_context(g, look_back):
                if look_back:
                    sp.wait_ge(a_ct.sem, a_ct.done(g - 1))
                    alone(sp)
                for b in range(G):
                    sp.dma_start(c_nat[:, b, :, :], c_nat_d.rearrange("b (c p) f -> b p c f", p=CH)[bass.ds(g * G + b, 1), :, :, :].rearrange("b p c f -> (b p) c f")).then_inc(c_loaded, 16)

            def store(g):
                sp.wait_ge(v_res.sem, v_res.done(g))
                alone(sp)
                sp.dma_start(out_d[bass.ds(g * G, G), :, :].rearrange("b t f -> t b f"), res[:, :, :]).then_inc(stored, 16)

            sp.sem_inc(stored, 16)
            load_x(0, False)
            load_context(0, False)
            load_x(1, True)
            with sp.Fori(0, NG - 2) as i:
                load_context(i + 1, True)
                load_x(i + 2, True)
                store(i)
            load_context(NG - 1, True)
            store(NG - 2)
            store(NG - 1)
            sp.wait_ge(stored, 16 * NG + 16)

        @block.tensor
        def _(pe):
            def end(m):
                m.then_inc(psum_filled, 1)

            def products(pairs, dst, start=True):
                for n, (lhs, rhs) in enumerate(pairs):
                    m = nc.tensor.matmul(dst, lhs, rhs, start=start and n == 0, stop=n == len(pairs) - 1, skip_group_check=True)
                return m

            def flat(t):
                return t.rearrange("p b t -> p (b t)")

            def features_out(at, name, weights, col, act_, tiles=C, per_bank=1, split=True):
                o = claim(pe, at, name)
                for i in range(tiles):
                    cols = slice(col + 128 * i, col + 128 * (i + 1))
                    if split:
                        pairs = [(weights[:, wp, ci, cols], flat(act_[:, ap, ci, :, :])) for ci in range(C) for wp, ap in TERMS]
                    else:
                        pairs = [(weights[:, ci, cols], flat(act_[:, ci, :, :])) for ci in range(C)]
                    m = products(pairs, o[:, i // per_bank, (i % per_bank) * G * T:(i % per_bank + 1) * G * T])
                end(m)

            def tokens_out(at, name, operands):
                o = claim(pe, at, name)
                for b in range(G):
                    m = products(operands(b), o[0:T, b, 0:U])
                end(m)

            def split_pairs(act_, b, weights, col=0, tiles=C):
                return [(act_[:, ap, c, b, :], weights[:, wp, c, col:col + U]) for c in range(tiles) for wp, ap in TERMS]

            def rows_transposed(o, src, post, at_b):
                for b in range(G):
                    pe.wait_ge(post.sem, at_b(b))
                    for c in range(C):
                        m = nc.tensor.transpose(o(c, b), src[:, b, c * 128:(c + 1) * 128], ident[0:T, 0:T])
                end(m)

            def masks(at, g):
                o = claim(pe, at, "counts")
                pe.wait_ge(v_mask.sem, v_mask.done(g))
                for b in range(G):
                    nc.tensor.matmul(o[0:1, 1, b * T:(b + 1) * T], keep0b[:, b:b + 1], tril[:, :], start=b == 0, stop=True, skip_group_check=True)
                end(nc.tensor.matmul(o[0:T, 0, 0:G], tril[:, :], keep1b[:, :], start=True, stop=True))

            def project_q0(at, g):
                pe.wait_ge(x_loaded, g * 96 + 96)
                features_out(at, "q0", w0["wq0"], 0, x_t, split=False)

            def project_k0(at, g):
                features_out(at, "k0", w0["wk0"], 0, c_t, split=False)

            def project_v0(at, g):
                tokens_out(at, "v0", lambda b: [(c_t[:, c, b, :], w0["wv0"][:, c, :]) for c in range(C)])

            def self_max(at, g, layer, b):
                for s in ((a_q0, a_k0), (a_q1, a_k1))[layer]:
                    pe.wait_ge(s.sem, s.done(g))
                pe.wait_ge(v_mask.sem, v_mask.done(g))
                for m_ in range(2):
                    o = claim(pe, at, f"max{layer}_{b}_{m_}")
                    for jj in range(2):
                        nc.tensor.matmul(o[0:T, jj, 0:4 * T], add_mask[:, layer, b, :], ident_b[:, :].unsqueeze(1).to_broadcast([T, 4, T]),
                                         start=True, stop=False, skip_group_check=True)
                    for c in range(C):
                        for e in range(2):
                            for jj in range(2):
                                r = 32 * (2 * m_ + jj)
                                m = nc.tensor.matmul(o[0:T, jj, (2 * c + e) * T:(2 * c + e + 1) * T], qf[r:r + 32, c, b, e, :],
                                                     kf[r:r + 32, c, b, :], start=False, stop=True, skip_group_check=True)
                    end(m)

            def top(at, g, layer, b):
                o = claim(pe, at, f"top{layer}_{b}")
                pe.wait_ge(v_max[layer].sem, v_max[layer].at(g, (b + 1) * v_max[layer].per // G))
                end(nc.tensor.transpose(o[0:H, 0, 0:T], negmax[layer // 2][:, b, :], ident[0:T, 0:T]))

            def minus_max(o, n_keys, stage, b, m_):
                for jj in range(2):
                    for ce in range(4):
                        row_ = 4 * (2 * m_ + jj) + ce
                        m = nc.tensor.matmul(o[0:n_keys, jj, ce * T:(ce + 1) * T], select[:, row_:row_ + 1].to_broadcast([48, n_keys]),
                                             negmax_t[stage][:, b, :], start=False, stop=True, skip_group_check=True)
                end(m)

            def self_exp(at, g, layer, b):
                pe.wait_ge(v_top[layer].sem, v_top[layer].at(g, 2 * b + 2))
                for m_ in range(2):
                    o = claim(pe, at, f"exp{layer}_{b}_{m_}")
                    for jj in range(2):
                        nc.tensor.matmul(o[0:T, jj, 0:4 * T], ident_b[:, :], causal2[:, :].unsqueeze(1).to_broadcast([T, 4, T]),
                                         start=True, stop=False, skip_group_check=True)
                    for c in range(C):
                        for jj in range(2):
                            r = 32 * (2 * m_ + jj)
                            nc.tensor.matmul(o[0:T, jj, 2 * c * T:2 * (c + 1) * T], kf[r:r + 32, c, b, :],
                                             qf[r:r + 32, c, b, :, :].rearrange("p e t -> p (e t)"), start=False, stop=False, skip_group_check=True)
                    minus_max(o, T, 0, b, m_)

            def add_values(stage, n_keys, slot, m_, vals, opens):
                for jj in range(2):
                    for ce in range(4):
                        hd = 8 * (ce // 2) + 2 * (2 * m_ + jj) + ce % 2
                        s, p = hd // 4, hd % 4
                        m = nc.tensor.matmul(acc[stage][32 * p:32 * p + DV, s, 0:T], vals(hd), probs[stage][0:n_keys, slot, jj, ce, :],
                                             start=opens and s == 0, stop=True, skip_group_check=True, tile_position=(0, 32 * p))
                return m

            def self_sum(at, g, layer, b):
                s = (v_v0, v_v1)[layer]
                pe.wait_ge(s.sem, s.done(g))
                pe.wait_ge(a_accA.sem, a_accA.at(g, 2 * layer + b))
                for m_ in range(2):
                    e_no = 4 * layer + 2 * b + m_
                    pe.wait_ge(a_expA.sem, a_expA.at(g, e_no + 1))
                    t_pvA.step(add_values(0, T, e_no % NP, m_, lambda hd: v[layer][:, b, hd, :], m_ == 0))

            def out_back(at, g, layer, b):
                stage = layer // 2
                o = claim(pe, at, f"out{layer}_{b}")
                if layer == 0:
                    pe.wait_ge(v_cnt.sem, v_cnt.done(g))
                    nc.tensor.matmul(o[0:T, 0, :].rearrange("q (h d) -> q h d", h=H)[:, :, 0:DV], empty[:, b, :],
                                     v_all_g[:, b, :].rearrange("p (h d) -> p h d", h=H), start=True, stop=False, skip_group_check=True)
                s = (a_accA, a_accB)[stage]
                pe.wait_ge(s.sem, s.at(g, 2 * layer + b + 1 if stage == 0 else b + 1))
                for i in range(4):
                    dst = o[0:T, 0, 128 * i:128 * (i + 1)]
                    if layer == 0:
                        m = nc.tensor.matmul(dst, acc_sb[stage][:, i, :], ident[:, :], start=False, stop=True, skip_group_check=True)
                    else:
                        m = nc.tensor.transpose(dst, acc_sb[stage][:, i, :], ident[:, :])
                end(m)

            def x_transposed(at, g):
                o = claim(pe, at, "xT")
                rows_transposed(lambda c, b: o[:, c, b * T:(b + 1) * T], xh, v_post0, lambda b: v_post0.at(g, OUT0 * (b + 1) - 1))

            def project_q1(at, g):
                pe.wait_ge(p_n_lo.sem, p_n_lo.at(g, 1))
                features_out(at, "q1", w["wqkv1"], 0, n1)

            def out_transposed(at, g, stage):
                o = claim(pe, at, ("oT1", "oT2")[stage])
                post = (v_post1, v_post2)[stage]
                rows_transposed(lambda c, b: o[:, 0, (2 * c + b) * T:(2 * c + b + 1) * T], o_n[stage], post, lambda b: post.at(g, post.per // G * (b + 1)))

            def project_out1(at, g):
                pe.wait_ge(v_ot_lo.sem, v_ot_lo.done(g))
                tokens_out(at, "proj", lambda b: split_pairs(o_t[0], b, w["wp1"]))

            def xq_transposed(at, g):
                o = claim(pe, at, "xqT")
                rows_transposed(lambda c, b: o[:, c, b * T:(b + 1) * T], xh, v_proj, lambda b: v_proj.at(g, G + 4 * (b + 1)))

            def project_q2(at, g):
                pe.wait_ge(p_xq_lo.sem, p_xq_lo.done(g))
                features_out(at, "q2", w["wq2"], 0, n1)

            def hidden(at, g, i):
                pe.wait_ge(p_n_lo.sem, p_n_lo.done(g))
                features_out(at, f"h{i}", w["w1"], 512 * i, n3, tiles=4, per_bank=2)

            def context_transposed(at, g, b):
                o = claim(pe, at, f"cT_{b}")
                pe.wait_ge(v_ctxln.sem, v_ctxln.done(g))
                for c in range(C):
                    for ch in range(NCH):
                        m = nc.tensor.transpose(o[:, c, ch * CH:(ch + 1) * CH], c_nat[0:CH, b, ch, c * 128:(c + 1) * 128], ident[0:CH, 0:CH])
                end(m)

            def project_k2(at, g, b):
                o = claim(pe, at, f"k2_{b}")
                pe.wait_ge(p_ct_lo.sem, p_ct_lo.at(g, b + 1))
                for i in range(C):
                    m = products([(w["wkv2"][:, wp, ci, 128 * i:128 * (i + 1)], ct[:, ap, ci, b, :]) for ci in range(C) for wp, ap in TERMS], o[:, i, 0:SP])
                end(m)

            def project_v2(at, g, b):
                o = claim(pe, at, f"v2_{b}")
                for ch in range(NCH):
                    m = products([(ct[:, ap, ci, b, ch * CH:(ch + 1) * CH], w["wkv2"][:, wp, ci, U:2 * U]) for ci in range(C) for wp, ap in TERMS],
                                 o[0:CH, ch // 2, (ch % 2) * U:(ch % 2 + 1) * U], start=ch % 2 == 0)
                end(m)

            def cross_max(at, g, b, i):
                o = claim(pe, at, f"max2_{b}_{i}")
                if i == 0:
                    pe.wait_ge(p_q2_lo.sem, p_q2_lo.done(g))
                    pe.wait_ge(v_k2_lo.sem, v_k2_lo.at(g, b + 1))
                c, e = (i % 4) // 2, i % 2
                for n, (qp, kp) in enumerate(TERMS):
                    for jj in range(2):
                        r = 32 * (2 * (i // 4) + jj)
                        m = nc.tensor.matmul(o[0:T, jj, 0:SP], q2[r:r + 32, qp, c, b, e, :], k2[r:r + 32, kp, c, b, :], start=n == 0, stop=n == 2)
                end(m)

            def cross_exp(at, g, b, i):
                o = claim(pe, at, f"exp2_{b}_{i}")
                pe.wait_ge(v_top[2].sem, v_top[2].at(g, 2 * b + 2))
                keys = slice(i // 2 * CH, (i // 2 + 1) * CH)
                for c in range(C):
                    for n, (kp, qp) in enumerate(TERMS):
                        for jj in range(2):
                            r = 32 * (2 * (i % 2) + jj)
                            nc.tensor.matmul(o[0:CH, jj, 2 * c * T:2 * (c + 1) * T], k2[r:r + 32, kp, c, b, keys],
                                             q2[r:r + 32, qp, c, b, :, :].rearrange("p e t -> p (e t)"),
                                             start=c == 0 and n == 0, stop=False, skip_group_check=True)
                minus_max(o, CH, 1, b, i % 2)

            def cross_sum(at, g, b, i):
                if i == 0:
                    pe.wait_ge(v_v2.sem, v_v2.at(g, b + 1))
                    pe.wait_ge(a_accB.sem, a_accB.at(g, b))
                e_no = 6 * b + i
                pe.wait_ge(a_expB.sem, a_expB.at(g, e_no + 1))
                t_pvB.step(add_values(1, CH, e_no % NP, i % 2, lambda hd: v2[:, b, i // 2, hd, :], i == 0))

            def project_y(at, g):
                pe.wait_ge(v_o2t_lo.sem, v_o2t_lo.done(g))
                pe.wait_ge(p_h_lo.sem, p_h_lo.done(g))
                tokens_out(at, "y", lambda b: split_pairs(h, b, w["w2"], tiles=FF) + split_pairs(o_t[1], b, w["wp2"]))

            pe.wait_ge(flag_made, 1)
            nc.tensor.matmul(ring[0][0:1, 0, 0:1], first_masked[:, :], ones[0:B, :], start=True, stop=True).then_inc(first_counted, 1)
            pe.wait_ge(const_loaded[1], 96)
            pe.wait_ge(w0_loaded, 16 * len(w0))
            pe.wait_ge(prep_dve, PREP_DVE)
            pe.wait_ge(prep_pool, PREP_POOL)
            pe.wait_ge(flag_made, 2)
            with pe.If(pe.value_load(any_masked[0:1, 0:1]) > 0):
                with pe.Fori(0, B) as b:
                    for ch in range(NCH):
                        pe.wait_ge(gen_loaded, b * (16 * NCH) + 16 * ch + 16)
                        for ci in range(C):
                            m = nc.tensor.matmul(ring[1][0:CH, 0, 0:U], gen_c[:, ci, :], w0["wv0"][:, ci, :], start=ci == 0, stop=ci == C - 1)
                        m.then_inc(gen_values, 1)
                        pe.wait_ge(gen_ready, b * (2 * NCH) + 2 * ch + 2)
                        m = nc.tensor.matmul(ring[2][0:1, 0, 0:H * DV], ones[0:CH, :], v2[:, 0, ch, :, :].rearrange("p h d -> p (h d)"), start=ch == 0, stop=ch == NCH - 1)
                    m.then_inc(gen_summed, 1)
                    pe.wait_ge(gen_row, b + 1)
            run(pe, {
                "A.masks": masks, "A.q0": project_q0, "A.k0": project_k0, "A.v0": project_v0,
                "A.max0": lambda at, g, b: self_max(at, g, 0, b), "A.top0": lambda at, g, b: top(at, g, 0, b),
                "A.exp0": lambda at, g, b: self_exp(at, g, 0, b), "A.sum0": lambda at, g, b: self_sum(at, g, 0, b),
                "A.out0": lambda at, g, b: out_back(at, g, 0, b), "A.xT": x_transposed, "A.q1": project_q1,
                "A.k1": lambda at, g: features_out(at, "k1", w["wqkv1"], U, n1),
                "A.v1": lambda at, g: tokens_out(at, "v1", lambda b: split_pairs(n1, b, w["wqkv1"], 2 * U)),
                "A.max1": lambda at, g, b: self_max(at, g, 1, b), "A.top1": lambda at, g, b: top(at, g, 1, b),
                "A.exp1": lambda at, g, b: self_exp(at, g, 1, b), "A.sum1": lambda at, g, b: self_sum(at, g, 1, b),
                "A.out1": lambda at, g, b: out_back(at, g, 1, b), "A.oT": lambda at, g: out_transposed(at, g, 0),
                "A.proj": project_out1, "A.xqT": xq_transposed,
                "B.q2": project_q2, "B.h0": lambda at, g: hidden(at, g, 0), "B.h1": lambda at, g: hidden(at, g, 1),
                "B.cT": context_transposed, "B.k2": project_k2, "B.v2": project_v2, "B.max": cross_max,
                "B.top": lambda at, g, b: top(at, g, 2, b), "B.exp": cross_exp, "B.sum": cross_sum,
                "B.out": lambda at, g, b: out_back(at, g, 2, b), "B.oT": lambda at, g: out_transposed(at, g, 1), "B.y": project_y})

        @block.scalar
        def _(act):
            def two_heads(at, name, s, dst, scale, bias):
                o = is_filled(act, at, name)
                for c in range(C):
                    for e in range(2):
                        src = o[:, c, 0:G * T].rearrange("p (b t) -> p b t", b=G)
                        f = ACT.Identity if bias is None else ACT.Relu
                        s.step(nc.scalar.activation(dst[:, c, :, e, :], src, f, bias=0.0 if bias is None else bias[:, c, e:e + 1],
                                                    scale=eo_scale[:, scale, e:e + 1]))

            def affine(at, name, s, dst, scale, bias, func=ACT.Identity):
                o = is_filled(act, at, name)
                for c in range(C):
                    s.step(nc.scalar.activation(dst[:, c, :, :].rearrange("p b t -> p (b t)"), o[:, c, 0:G * T], func, bias=bias(c), scale=scale(c)))

            def col(name):
                return lambda c: vec[:, VEC[name] + c:VEC[name] + c + 1]

            def exponentials(at, g, name, stage, e_no, bias, n_keys):
                o = is_filled(act, at, name)
                s, used = ((a_expA, t_pvA), (a_expB, t_pvB))[stage]
                if e_no >= NP:
                    act.wait_ge(used.sem, used.at(g, e_no - NP + 1))
                s.step(nc.scalar.activation(probs[stage][0:n_keys, e_no % NP, :, :, :].rearrange("p j a t -> p j (a t)"),
                                            o[0:n_keys, :, 0:4 * T], ACT.Exp, **({} if bias is None else {"bias": bias})))

            def self_exp(at, g, layer, b):
                pad = (pad0, pad1)[layer]
                for m_ in range(2):
                    exponentials(at, g, f"exp{layer}_{b}_{m_}", 0, 4 * layer + 2 * b + m_, pad[:, b:b + 1], T)

            def copy_out(s, used, stage):
                act.wait_ge(used[0].sem, used[1])
                s.step(nc.scalar.activation(acc_sb[stage][:, :, :], acc[stage][:, :, 0:T], ACT.Copy))

            def self_out(at, g, layer, b):
                copy_out(a_accA, (t_pvA, t_pvA.at(g, 4 * layer + 2 * b + 2)), 0)

            def cross_out(at, g, b):
                copy_out(a_accB, (t_pvB, t_pvB.at(g, 6 * b + 6)), 1)

            def normed(at, g):
                if at.b is not None:
                    act.wait_ge(p_q2_lo.sem, p_q2_lo.done(at.b))
                affine(at, "xT", a_n, n_tmp[:, 0], col("g1"), col("b1"))
                affine(at, "xT", a_n, n_tmp[:, 1], col("g3"), col("b3"))

            def copy_k1(at, g):
                a_k1.step(nc.scalar.activation(kf[:, :, :, :].rearrange("p c b t -> p c (b t)"), is_filled(act, at, "k1")[:, :, 0:G * T], ACT.Copy))

            def out_hi(at, name, s, stage):
                s.step(nc.scalar.activation(o_t[stage][:, HI, :, :, :].rearrange("p c b t -> p (c b t)"), is_filled(act, at, name)[:, 0, 0:C * G * T], ACT.Copy))

            def scale_q2(at, g):
                act.wait_ge(p_n_lo.sem, p_n_lo.done(g))
                two_heads(at, "q2", a_q2, q2_tmp, 1, None)

            def hidden(at, g, i0):
                act.wait_ge(p_h_lo.sem, p_h_lo.at(g, i0))
                o = is_filled(act, at, f"h{i0}")
                for i in range(4):
                    a_h.step(nc.scalar.activation(h_tmp[:, i, :, :].rearrange("p b t -> p (b t)"), o[:, i // 2, (i % 2) * G * T:(i % 2 + 1) * G * T],
                                                  ACT.Relu, bias=vec[:, FB1 + 4 * i0 + i:FB1 + 4 * i0 + i + 1]))

            def context(at, g, b):
                act.wait_ge(p_ct_lo.sem, p_ct_lo.at(g, b))
                o = is_filled(act, at, f"cT_{b}")
                for c in range(C):
                    a_ct.step(nc.scalar.activation(ct_tmp[:, c, 0:S], o[:, c, 0:S], ACT.Identity, bias=col("b2")(c), scale=col("g2")(c)))

            def k2_hi(at, g, b):
                a_k2.step(nc.scalar.activation(k2[:, HI, :, b, :], is_filled(act, at, f"k2_{b}")[:, :, 0:SP], ACT.Copy))

            start_signals(act, "scalar")
            act.wait_ge(const_loaded[0], 32)
            for i in range(2):
                nc.scalar.activation(eo_scale[:, i, :], vec[:, EO:EO + 2], ACT.Copy, scale=(0.25, 0.0625)[i]).then_inc(prep_act, 1)
            act.wait_ge(prep_act, 2)
            act.wait_ge(prep_dve, PREP_DVE)
            act.wait_ge(prep_pool, PREP_POOL)
            run(act, {
                "A.q0": lambda at, g: two_heads(at, "q0", a_q0, qf, 0, bq0_eo),
                "A.k0": lambda at, g: affine(at, "k0", a_k0, kf, lambda c: 1.0, col("bk0"), ACT.Relu),
                "A.exp0": lambda at, g, b: self_exp(at, g, 0, b), "A.out0": lambda at, g, b: self_out(at, g, 0, b), "A.xT": normed,
                "A.q1": lambda at, g: two_heads(at, "q1", a_q1, qf, 1, None), "A.k1": copy_k1,
                "A.exp1": lambda at, g, b: self_exp(at, g, 1, b), "A.out1": lambda at, g, b: self_out(at, g, 1, b),
                "A.oT": lambda at, g: out_hi(at, "oT1", a_ot, 0),
                "A.xqT": lambda at, g: affine(at, "xqT", a_xq, n_tmp[:, 0], col("g2"), col("b2")),
                "B.q2": scale_q2, "B.h0": lambda at, g: hidden(at, g, 0), "B.h1": lambda at, g: hidden(at, g, 1),
                "B.cT": context, "B.k2": k2_hi,
                "B.exp": lambda at, g, b, i: exponentials(at, g, f"exp2_{b}_{i}", 1, 6 * b + i, None, CH),
                "B.out": cross_out, "B.oT": lambda at, g: out_hi(at, "oT2", a_o2t, 1)})

        @block.vector
        def _(dve):
            def after(s, g):
                dve.wait_ge(s.sem, s.at(g, s.given))

            def flat(t):
                return t.rearrange("p c b t -> p (c b t)")

            def high(s, g, a_s, k_, dst, src):
                dve.wait_ge(a_s.sem, a_s.at(g, k_))
                s.step(nc.vector.tensor_copy(dst, src))

            def masks(at, g):
                s = v_mask
                dve.wait_ge(x_loaded, g * 96 + 96)
                dve.wait_ge(a_expA.sem, a_expA.before(g))
                s.step(nc.vector.reduce_sum(ksum[:, :], key_nat[:, :, :], AX.X))
                s.step(nc.vector.reduce_sum(qsum[:, :], x_nat[:, :, :], AX.X))
                s.step(nc.vector.tensor_copy(pad1[:, :], pad1_all[:, bass.ds(g * G, G)]))
                after(s, g)
                s.step(nc.vector.tensor_scalar(keep0[:, :], ksum[:, :], 0.0, None, ALU.not_equal))
                s.step(nc.vector.tensor_scalar(keep0b[:, :], ksum[:, :], 0.0, None, ALU.not_equal))
                s.step(nc.vector.tensor_scalar(pad0[:, :], ksum[:, :], 0.0, BIG, ALU.is_equal, ALU.mult))
                s.step(nc.vector.tensor_scalar(qkeep[:, :], qsum[:, :], 0.0, None, ALU.not_equal))
                s.step(nc.vector.tensor_scalar(keep1b[:, :], pad1[:, :], 0.0, None, ALU.is_equal))
                after(s, g)
                for b in range(G):
                    s.step(nc.vector.tensor_scalar(add_mask[:, 0, b, :], causal[:, :], pad0[:, b:b + 1], None, ALU.min))
                    s.step(nc.vector.tensor_scalar(add_mask[:, 1, b, :], causal[:, :], pad1[:, b:b + 1], None, ALU.min))
                o = is_filled(dve, at, "counts")
                s = v_cnt
                s.step(nc.vector.tensor_scalar(valid[:, :], o[0:T, 0, 0:G], 1.0, None, ALU.min))
                s.step(nc.vector.tensor_scalar(empty[:, :, :].rearrange("p b t -> p (b t)"), o[0:1, 1, 0:G * T], 0.0, None, ALU.is_equal))
                after(s, g)
                s.step(nc.vector.reciprocal(rvalid[:, :], valid[:, :]))
                after(s, g)
                s.step(nc.vector.tensor_tensor(nanf[:, :], valid[:, :], rvalid[:, :], ALU.mult))

            def values0(at, g):
                o = is_filled(dve, at, "v0")
                dve.wait_ge(a_xq.sem, a_xq.before(g))
                v_v0.step(nc.vector.tensor_tensor(v_tmp[:, :, :], o[0:T, :, 0:U], rowv["bv0"][0:T, :].unsqueeze(1).to_broadcast([T, G, U]), ALU.add))
                after(v_v0, g)
                for b in range(G):
                    v_v0.step(nc.vector.tensor_copy(v[0][:, b, :, D], keep0[:, b:b + 1].to_broadcast([T, H])))
                    v_v0.step(nc.vector.tensor_scalar(v[0][:, b, :, 0:D], v_tmp[:, b, :].rearrange("p (h d) -> p h d", h=H), 0.0, keep0[:, b:b + 1], ALU.max, ALU.mult))

            def self_maxima(at, g, layer, b):
                for m_ in range(2):
                    o = is_filled(dve, at, f"max{layer}_{b}_{m_}")
                    v_max[layer].step(nc.vector.tensor_reduce(negmax[0][:, b, 8 * m_:8 * m_ + 8],
                                                              o[0:T, :, 0:4 * T].rearrange("p j (a t) -> p j a t", a=4), AX.X, ALU.max, negate=True))

            def max_rows(at, g, layer, b):
                o, s, to = is_filled(dve, at, f"top{layer}_{b}"), v_top[layer], negmax_t[layer // 2]
                s.step(nc.vector.tensor_copy(to[0:H, b, :], o[0:H, 0, 0:T]))
                after(s, g)
                s.step(nc.vector.tensor_tensor(to[32:32 + H, b, :], o[0:H, 0, 0:T], to[0:H, b, :], ALU.subtract))

            def statistics(s, g, src, b):
                s.step(nc.vector.bn_stats(stats[0:T, b, :], src))
                after(s, g)
                alone(dve)
                s.step(nc.vector.bn_aggr(mv[0:T, b, :], stats[0:T, b, :]))
                after(s, g)

            def heads_out(at, s, g, layer, b, flag):
                stage = layer // 2
                o = is_filled(dve, at, f"out{layer}_{b}")[0:T, 0, :].rearrange("q (h d) -> q h d", h=H)
                s.step(nc.vector.reciprocal(rden[stage][:, b, :], o[:, :, D]))
                after(s, g)
                if flag is not None:
                    s.step(nc.vector.tensor_scalar(rden[stage][:, b, :], rden[stage][:, b, :], flag[:, b:b + 1], None, ALU.mult))
                    after(s, g)
                s.step(nc.vector.tensor_tensor(o_n[stage][:, b, :].rearrange("q (h d) -> q h d", h=H), o[:, :, 0:D],
                                               rden[stage][:, b, :].unsqueeze(2).to_broadcast([T, H, D]), ALU.mult))

            def out0(at, g, b):
                s = v_post0
                heads_out(at, s, g, 0, b, qkeep)
                after(s, g)
                s.step(nc.vector.tensor_tensor(x1[:, b, :], o_n[0][:, b, :], x_nat[:, b, :], ALU.add))
                after(s, g)
                statistics(s, g, x1[:, b, :], b)
                s.step(nc.vector.tensor_scalar(sd[:, b:b + 1], mv[0:T, b, 1:2], U / (U - 1), None, ALU.mult))
                dve.wait_ge(p_rstd.sem, p_rstd.at(g, 2 * b + 1))
                s.step(nc.vector.tensor_scalar(sd[:, b:b + 1], sd_r[:, b:b + 1], 1e-8, None, ALU.add))
                after(s, g)
                s.step(nc.vector.reciprocal(sd_r[:, b:b + 1], sd[:, b:b + 1]))
                after(s, g)
                s.step(nc.vector.tensor_scalar(y[:, b, :], x1[:, b, :], mv[0:T, b, 0:1], sd_r[:, b:b + 1], ALU.subtract, ALU.mult))
                after(s, g)
                s.step(nc.vector.tensor_tensor(y[:, b, :], y[:, b, :], rowv["gamma0"][:, :], ALU.mult))
                after(s, g)
                s.step(nc.vector.tensor_tensor(x1[:, b, :], y[:, b, :], rowv["beta0"][:, :], ALU.add))
                after(s, g)
                statistics(s, g, x1[:, b, :], b)
                s.step(nc.vector.tensor_scalar(var_e[0:T, b:b + 1], mv[0:T, b, 1:2], 1e-5, None, ALU.add))
                dve.wait_ge(p_rstd.sem, p_rstd.at(g, 2 * b + 2))
                s.step(nc.vector.tensor_scalar(xh[:, b, :], x1[:, b, :], mv[0:T, b, 0:1], rstd[0:T, b:b + 1], ALU.subtract, ALU.mult))
                s.step(nc.vector.tensor_tensor(x1[:, b, :], x1[:, b, :], rowv["bp1"][:, :], ALU.add))

            def norm_hi(at, g):
                high(v_n_hi, g, a_n, 2, flat(n1[:, HI]), flat(n_tmp[:, 0]))
                high(v_n_hi, g, a_n, 4, flat(n3[:, HI]), flat(n_tmp[:, 1]))

            def values1(at, g):
                v_v1.step(nc.vector.tensor_copy(v[1][:, :, :, 0:D], is_filled(dve, at, "v1")[0:T, :, 0:U].rearrange("p b (h d) -> p b h d", h=H)))

            def out_lo(at, g, s, a_s, name, stage):
                dve.wait_ge(a_s.sem, a_s.done(g))
                s.step(nc.vector.tensor_tensor(flat(o_t[stage][:, LO]), is_filled(dve, at, name)[:, 0, 0:C * G * T],
                                               flat(o_t[stage][:, HI].bitcast(F32)), ALU.subtract))

            def residual1(at, g):
                s = v_proj
                o = is_filled(dve, at, "proj")
                dve.wait_ge(v_post0.sem, v_post0.done(g))
                for b in range(G):
                    s.step(nc.vector.tensor_tensor(x1[:, b, :], o[0:T, b, 0:U], x1[:, b, :], ALU.add))
                after(s, g)
                for b in range(G):
                    statistics(s, g, x1[:, b, :], b)
                    s.step(nc.vector.tensor_scalar(var_e[0:T, b:b + 1], mv[0:T, b, 1:2], 1e-5, None, ALU.add))
                    dve.wait_ge(p_rstd.sem, p_rstd.at(g, 2 * G + b + 1))
                    s.step(nc.vector.tensor_scalar(xh[:, b, :], x1[:, b, :], mv[0:T, b, 0:1], rstd[0:T, b:b + 1], ALU.subtract, ALU.mult))

            def query2_hi(at, g):
                dve.wait_ge(v_proj.sem, v_proj.done(g))
                v_r1.step(nc.vector.tensor_tensor(r1[:, :, :], x1[:, :, :], rowv["bp2"][:, :].unsqueeze(1).to_broadcast([T, G, U]), ALU.add))
                high(v_q2_hi, g, a_q2, 4, q2[:, HI].rearrange("p c b e t -> p (c b e t)"), q2_tmp[:, :, :, :, :].rearrange("p c b e t -> p (c b e t)"))

            def hidden_hi(at, g, i):
                high(v_h_hi, g, a_h, 4 * (i + 1), flat(h[:, HI, 4 * i:4 * (i + 1)]), flat(h_tmp[:, :, :, :]))

            def context_statistics(at, g):
                s = v_ctxln
                dve.wait_ge(c_loaded, g * 32 + 32)
                for i in range(G * NCH):
                    s.step(nc.vector.bn_stats(c_stats[:, i, :], c_nat[:, i // NCH, i % NCH, :]))
                after(s, g)
                alone(dve)
                for i in range(G * NCH):
                    s.step(nc.vector.bn_aggr(c_mv[:, i, :], c_stats[:, i, :]))
                after(s, g)
                s.step(nc.vector.tensor_scalar(c_var[:, :], c_mv[:, :, 1], 1e-5, None, ALU.add))

            def context_normed(at, g):
                dve.wait_ge(p_crstd.sem, p_crstd.done(g))
                for i in range(G * NCH):
                    v_ctxln.step(nc.vector.tensor_scalar(c_nat[0:CH, i // NCH, i % NCH, :], c_nat[:, i // NCH, i % NCH, :],
                                                         c_mv[:, i, 0:1], c_rstd[:, i:i + 1], ALU.subtract, ALU.mult))

            def context_hi(at, g, b):
                high(v_ct_hi, g, a_ct, 2 * b + 2, ct[:, HI, :, b, :], ct_tmp[:, :, :])

            def k2_lo(at, g, b):
                dve.wait_ge(a_k2.sem, a_k2.at(g, b + 1))
                v_k2_lo.step(nc.vector.tensor_tensor(k2[:, LO, :, b, :], is_filled(dve, at, f"k2_{b}")[:, :, 0:SP], k2[:, HI, :, b, :].bitcast(F32), ALU.subtract))

            def values2(at, g, b):
                o = is_filled(dve, at, f"v2_{b}")
                v_v2.step(nc.vector.tensor_copy(v2[:, b, :, :, 0:D], o[0:CH, :, :].rearrange("p j n -> p (j n)")[:, 0:NCH * U].rearrange("p (n h d) -> p n h d", n=NCH, h=H)))

            def cross_maxima(at, g, b, i):
                o = is_filled(dve, at, f"max2_{b}_{i}")
                r = 8 * (i // 4) + i % 4
                v_max[2].step(nc.vector.tensor_reduce(negmax[1][:, b, r:r + 5:4], o[0:T, :, 0:S], AX.X, ALU.max, negate=True))

            def out2(at, g, b):
                dve.wait_ge(stored, g * 16 + 16)
                heads_out(at, v_post2, g, 2, b, None)

            def result(at, g):
                o = is_filled(dve, at, "y")
                dve.wait_ge(v_r1.sem, v_r1.done(g))
                v_res.step(nc.vector.tensor_tensor(res[:, :, :], o[0:T, :, 0:U], r1[:, :, :], ALU.add))

            start_signals(dve, "vector")
            dve.wait_ge(const_loaded[0], 32)
            nc.vector.tensor_scalar(pad1_all[:, :], mask_u8[:, :], BIG, None, ALU.mult).then_inc(prep_dve, 1)
            nc.vector.memset(v[1][:, :, :, :], 1.0).then_inc(prep_dve, 1)
            nc.vector.memset(v2[:, :, :, :, :], 1.0).then_inc(prep_dve, 1)
            for i in range(2):
                nc.vector.memset(negmax_t[i][:, :, :], 0.0).then_inc(prep_dve, 1)
            nc.vector.memset(row, 0.0).then_inc(prep_dve, 1)
            for i in range(2):
                nc.vector.memset(acc[i][:, :, :], 0.0).then_inc(prep_dve, 1)
            nc.vector.memset(ones[:, :], 1.0).then_inc(flag_steps, 1)
            dve.wait_ge(first_loaded, 16)
            nc.vector.reduce_sum(first_sum[:, :], first_keys, AX.X).then_inc(flag_steps, 1)
            dve.wait_ge(flag_steps, 2)
            nc.vector.tensor_scalar(first_masked[:, :], first_sum[:, :], 0.0, None, ALU.is_equal).then_inc(flag_made, 1)
            dve.wait_ge(first_counted, 1)
            nc.vector.tensor_copy(any_masked[:, :], ring[0][0:1, 0, 0:1]).then_inc(flag_made, 1)
            dve.wait_ge(prep_act, 2)
            for e in range(2):
                nc.vector.tensor_scalar(bq0_eo[:, :, e], vec[:, VEC["bq0"]:VEC["bq0"] + C], eo_scale[:, 0, e:e + 1], None, ALU.mult).then_inc(prep_dve, 1)
            dve.wait_ge(const_loaded[2], 16 * len(rowv))
            nc.vector.tensor_tensor(rowv["bp2"][:, :], rowv["bp2"][:, :], rowv["fb2"][:, :], ALU.add).then_inc(prep_dve, 1)
            for n in wshape:
                dve.wait_ge(w_loaded[n], 16)
                nc.vector.tensor_copy(w[n][:, HI, :, :], w_raw_of[n]).then_inc(prep_dve, 1)
            dve.wait_ge(prep_pool, PREP_POOL)
            nc.vector.memset(ct_tmp[:, :, S:SP], 0.0).then_inc(prep_dve, 1)
            dve.wait_ge(prep_dve, PREP_DVE)
            dve.wait_ge(const_loaded[1], 96)
            dve.wait_ge(flag_made, 2)
            with dve.If(dve.value_load(any_masked[0:1, 0:1]) > 0):
                with dve.Fori(0, B) as b:
                    for ch in range(NCH):
                        dve.wait_ge(gen_values, b * NCH + ch + 1)
                        nc.vector.tensor_tensor(v2[:, 0, ch, :, 0:D], ring[1][0:CH, 0, 0:U].rearrange("p (h d) -> p h d", h=H),
                                                rowv["bv0"][:, :].rearrange("p (h d) -> p h d", h=H), ALU.add).then_inc(gen_ready, 1)
                        dve.wait_ge(gen_ready, b * (2 * NCH) + 2 * ch + 1)
                        nc.vector.tensor_scalar(v2[:, 0, ch, :, 0:D], v2[:, 0, ch, :, 0:D], 0.0, None, ALU.max).then_inc(gen_ready, 1)
                    dve.wait_ge(gen_summed, b + 1)
                    dve.wait_ge(v_all_stored, b * 16 + 16)
                    nc.vector.tensor_copy(row, ring[2][0:1, 0, 0:H * DV]).then_inc(gen_row, 1)
            run(dve, {
                "A.masks": masks, "A.v0": values0, "A.max0": lambda at, g, b: self_maxima(at, g, 0, b), "A.top0": lambda at, g, b: max_rows(at, g, 0, b),
                "A.out0": out0, "A.xT": norm_hi, "A.v1": values1, "A.max1": lambda at, g, b: self_maxima(at, g, 1, b),
                "A.top1": lambda at, g, b: max_rows(at, g, 1, b), "A.out1": lambda at, g, b: heads_out(at, v_post1, g, 1, b, nanf),
                "A.oT": lambda at, g: out_lo(at, g, v_ot_lo, a_ot, "oT1", 0), "A.proj": residual1,
                "A.xqT": lambda at, g: high(v_xq_hi, g, a_xq, 2, flat(n1[:, HI]), flat(n_tmp[:, 0])),
                "B.q2": query2_hi, "B.norm": context_statistics, "B.scale": context_normed,
                "B.h0": lambda at, g: hidden_hi(at, g, 0), "B.h1": lambda at, g: hidden_hi(at, g, 1), "B.cT": context_hi,
                "B.k2": k2_lo, "B.v2": values2, "B.max": cross_maxima, "B.top": lambda at, g, b: max_rows(at, g, 2, b), "B.out": out2,
                "B.oT": lambda at, g: out_lo(at, g, v_o2t_lo, a_o2t, "oT2", 1), "B.y": result})

        @block.gpsimd
        def _(pool):
            def flat(t):
                return t.rearrange("p c b t -> p (c b t)")

            def low(s, g, v_s, k_, dst, src, hi):
                pool.wait_ge(v_s.sem, v_s.at(g, k_))
                s.step(nc.gpsimd.tensor_tensor(dst, src, hi.bitcast(F32), ALU.subtract))

            def power(s, out, in_, neg, n):
                base = 0 if neg else G * NCH
                s.step(nc.gpsimd.tensor_tensor(out, in_, half[0:out.shape[0], base:base + n], ALU.pow))

            def deviations(at, g, b):
                pool.wait_ge(v_post0.sem, v_post0.at(g, OUT0 * b + 7))
                power(p_rstd, sd_r[:, b:b + 1], sd[:, b:b + 1], False, 1)
                pool.wait_ge(v_post0.sem, v_post0.at(g, OUT0 * b + 15))
                power(p_rstd, rstd[0:T, b:b + 1], var_e[0:T, b:b + 1], True, 1)

            def norm_lo(at, g):
                low(p_n_lo, g, v_n_hi, 1, flat(n1[:, LO]), flat(n_tmp[:, 0]), flat(n1[:, HI]))
                low(p_n_lo, g, v_n_hi, 2, flat(n3[:, LO]), flat(n_tmp[:, 1]), flat(n3[:, HI]))

            def deviations1(at, g):
                for b in range(G):
                    pool.wait_ge(v_proj.sem, v_proj.at(g, G + 4 * b + 3))
                    power(p_rstd, rstd[0:T, b:b + 1], var_e[0:T, b:b + 1], True, 1)

            def context_deviations(at, g):
                pool.wait_ge(v_ctxln.sem, v_ctxln.at(g, 2 * G * NCH + 1))
                power(p_crstd, c_rstd[:, :], c_var[:, :], True, G * NCH)

            def query2_lo(at, g):
                low(p_q2_lo, g, v_q2_hi, 1, q2[:, LO].rearrange("p c b e t -> p (c b e t)"), q2_tmp[:, :, :, :, :].rearrange("p c b e t -> p (c b e t)"),
                    q2[:, HI].rearrange("p c b e t -> p (c b e t)"))

            def hidden_lo(at, g, i):
                low(p_h_lo, g, v_h_hi, i + 1, flat(h[:, LO, 4 * i:4 * (i + 1)]), flat(h_tmp[:, :, :, :]), flat(h[:, HI, 4 * i:4 * (i + 1)]))

            start_signals(pool, "gpsimd")
            nc.gpsimd.memset(half[:, 0:G * NCH], -0.5).then_inc(prep_pool, 1)
            nc.gpsimd.memset(half[:, G * NCH:2 * G * NCH], 0.5).then_inc(prep_pool, 1)
            for i, n in enumerate(wshape):
                pool.wait_ge(prep_dve, PREP_SPLIT + i + 1)
                nc.gpsimd.tensor_tensor(w[n][:, LO, :, :], w_raw_of[n], w[n][:, HI, :, :].bitcast(F32), ALU.subtract).then_inc(prep_pool, 1)
            run(pool, {
                "A.out0": deviations, "A.xT": norm_lo, "A.proj": deviations1,
                "A.xqT": lambda at, g: low(p_xq_lo, g, v_xq_hi, 1, flat(n1[:, LO]), flat(n_tmp[:, 0]), flat(n1[:, HI])),
                "B.q2": query2_lo, "B.norm": context_deviations, "B.h0": lambda at, g: hidden_lo(at, g, 0), "B.h1": lambda at, g: hidden_lo(at, g, 1),
                "B.cT": lambda at, g, b: low(p_ct_lo, g, v_ct_hi, b + 1, ct[:, LO, :, b, :], ct_tmp[:, :, :], ct[:, HI, :, b, :])})

        assert made == set(sig), set(sig) - made


def kernel(**inputs):
    import concourse.bacc as bacc
    from concourse.bass_utils import run_bass_kernel_spmd

    a = {n: np.asarray(x) for n, x in inputs.items()}

    def layer(prefix, n):
        return a[prefix + n]

    cols = lambda x: np.ascontiguousarray(x.reshape(-1, 128).T)
    t = np.ascontiguousarray
    rows = np.arange(128)
    even = ((rows // D) % 2 == 0).astype(np.float32)[:, None]
    vec = np.concatenate([cols(a[n]) for n in (
        "L0_xattn_bq", "L0_xattn_bk", "L1_xattn_ln1_g", "L1_xattn_ln1_b", "L1_xattn_ln3_g", "L1_xattn_ln3_b",
        "L1_xattn_ln2_g", "L1_xattn_ln2_b", "L1_xattn_ff_b1")] + [even, 1 - even], axis=1)
    sel = np.zeros((48, H), np.float32)
    for r in range(H):
        sel[[r, 32 + r], r] = 1.0
    kq = np.arange(T)[:, None] <= np.arange(T)[None, :]
    bf = mybir.dt.np(BF16)
    data = {
        "x": t(a["x"]), "x_t": t(a["x"].reshape(B * T, U).T),
        "ctx": t(a["ctx_1024"]), "ctx_t": t(a["ctx_1024"].reshape(B * S, U).T),
        "mask": t(a["mask_BxS_bf0"].T), "vec": t(vec),
        "w_wq0": t(a["L0_xattn_Wq"].T), "w_wk0": t(a["L0_xattn_Wk"].T), "w_wv0": t(a["L0_xattn_Wv"].T),
        "w_wqkv1": t(a["L1_xattn_sa_wqkv"]), "w_wp1": t(a["L1_xattn_sa_wproj"]), "w_wq2": t(a["L1_xattn_ed_wq"]),
        "w_wkv2": t(a["L1_xattn_ed_wkv"]), "w_wp2": t(a["L1_xattn_ed_wproj"]), "w_w1": t(a["L1_xattn_ff_w1"]),
        "w_w2": t(a["L1_xattn_ff_w2"]),
        "r_bv0": t(a["L0_xattn_bv"]), "r_gamma0": t(a["L0_xattn_gamma"]), "r_beta0": t(a["L0_xattn_beta"]),
        "r_bp1": t(a["L1_xattn_sa_bproj"]), "r_bp2": t(a["L1_xattn_ed_bproj"]), "r_fb2": t(a["L1_xattn_ff_b2"]),
        "c_ident": np.eye(128, dtype=np.float32), "c_ident_b": np.eye(T).astype(bf),
        "c_causal": np.where(kq, 0.0, BIG).astype(bf), "c_causal2": np.where(kq, 0.0, 2 * BIG).astype(bf), "c_tril": kq.astype(bf), "c_select": sel.astype(bf),
    }
    nc = bacc.Bacc("TRN2", target_bir_lowering=False, num_devices=1)
    d = {n: nc.dram_tensor("in_" + n, x.shape, mybir.dt.from_np(x.dtype), kind="ExternalInput").ap() for n, x in data.items()}
    out = nc.dram_tensor("out", [B, T, U], F32, kind="ExternalOutput").ap()

    def group(prefix):
        return {n[len(prefix):]: ap for n, ap in d.items() if n.startswith(prefix)}

    build(nc, d["x"], d["x_t"], d["ctx"], d["ctx_t"], d["ctx"][:, 0, :], d["mask"], group("w_"), d["vec"], group("r_"), group("c_"), out)
    r = run_bass_kernel_spmd(nc, [{"in_" + n: x for n, x in data.items()}], core_ids=[0])
    return r.results[0]["out"]
```

```python
from contextlib import ExitStack

import numpy as np

import concourse.bass as bass
from concourse import mybir

F32 = mybir.dt.float32
F32R = mybir.dt.float32r
BF16 = mybir.dt.bfloat16
I32 = mybir.dt.int32
U8 = mybir.dt.uint8
ALU = mybir.AluOpType
ACT = mybir.ActivationFunctionType
AX = mybir.AxisListType

B, T, S, U, H = 8, 112, 375, 256, 16
D = U // H
C = U // 128
FF = 4 * U // 128
G = 2
NG = B // G
NCH, CH = 3, 125
SP = 376
BIG = -float(2 ** 100)
HI, LO = 0, 1


class Signal:

    def __init__(self, sem, per, owner, order):
        self.sem, self.per, self.given, self.owner, self.order = sem, per, 0, owner, order
        self.start = 0

    def at(self, g, k):
        return g * self.per + (k + self.start)

    def done(self, g):
        return self.at(g, self.per)

    def before(self, g):
        return self.at(g, 0)

    def step(self, instruction):
        self.given += 1
        instruction.then_inc(self.sem, 1)


class Part:

    def __init__(self, order, first_job, per_turn=0):
        self.order, self.first_job, self.per_turn = order, first_job, per_turn
        self.jobs = [j for step in order for j in JOBS_OF.get(step, ())]
        self.number = {name: i for i, name in enumerate(self.jobs)}


def attention(step, jobs, around):
    out = []
    for n in range(0, len(jobs) + 2, 2):
        for kind, i in (("tr", n - 2), ("sc", n), ("tr", n - 1), ("sc", n + 1), ("pv", n - 2), ("pv", n - 1), ("nm", n), ("nm", n + 1)):
            if 0 <= i < len(jobs):
                before, after = around.get((kind, i), ([], []))
                out += before + [step.format(kind, *jobs[i])] + after
    return out


def self_attention(l):
    norms = [[f"A.dev_{b}", f"A.norm_{b}"] if l == 0 else [] for b in range(G)]
    return attention(f"A.{{}}{l}_{{}}_{{}}", [(b, m) for b in range(G) for m in range(2)],
                     {("pv", 1): ([], [f"A.out{l}_0"]), ("tr", 3): (norms[0], []), ("pv", 3): ([], [f"A.out{l}_1"] + norms[1])})


def cross_attention():
    return attention("B.{}_{}_{}", [(b, i) for b in range(G) for i in range(8)],
                     {("tr", 6): (["B.k2_1", "B.v2_1"], []), ("pv", 7): ([], ["B.out_0"]), ("pv", 15): ([], ["B.out_1"])})


A_STEPS = (["A.masks", "A.q0", "A.k0", "A.v0"] + self_attention(0) + ["A.xT", "A.q1", "A.k1", "A.v1"] + self_attention(1)
           + ["A.proj", "A.norm2", "A.xqT"])
B_STEPS = (["B.norm", "B.q2", "B.scale", "B.h0", "B.cT_0", "B.h1", "B.k2_0", "B.v2_0", "B.cT_1"]
           + cross_attention() + ["B.y"])

SPLIT_AFTER = ("A.nm0", "A.tr0", "A.nm1", "A.tr1", "A.pv1")
PIECES = ([("wqkv1", c, c + 1, 0, 3 * U) for c in range(C)] + [(n, 0, C, 0, U) for n in ("wp1", "wq2")]
          + [("w1", c, c + 1, 2 * U * i, 2 * U * (i + 1)) for i in range(2) for c in range(C)] + [("wkv2", c, c + 1, 0, 2 * U) for c in range(C)]
          + [("w2", i, min(i + 3, FF), 0, U) for i in range(0, FF, 3)] + [("wp2", 0, C, 0, U)])
FIRST_STEPS, _next = [], 0
for _step in A_STEPS:
    FIRST_STEPS += {"A.q1": ["W.ready_1"], "A.proj": ["W.ready_2"]}.get(_step, []) + [_step]
    if _step[:5] in SPLIT_AFTER and _next < len(PIECES):
        FIRST_STEPS.append(f"W.split_{_next}")
        _next += 1
assert _next == len(PIECES)
FIRST_STEPS.append(f"W.ready_{_next - 1}")


MIX = ("ABBBABABAAAABBABBABBABAAABBBABAABBBBBAABBBBABABAAABBABBBBBBABBABABBBBBBBBBABABABBABABBBABBABAAAAABBB"
       "BABBBAABABBBBAABBBBAABBABAABA")


def mixed(a_steps, b_steps):
    stages = {"A": iter(a_steps), "B": iter(b_steps)}
    assert (MIX.count("A"), MIX.count("B")) == (len(a_steps), len(b_steps))
    return [next(stages[letter]) for letter in MIX]


JOBS_OF = {"A.masks": ("counts",), "A.q0": ("q0",), "A.k0": ("k0",), "A.v0": ("v0",), "A.xT": ("xT",), "A.q1": ("q1",),
           "A.k1": ("k1",), "A.v1": ("v1",), "A.proj": ("proj",), "A.xqT": ("xqT",), "B.q2": ("q2",),
           "B.h0": ("h0",), "B.h1": ("h1",), "B.y": ("y",)}
for b_ in range(G):
    for l_ in range(2):
        JOBS_OF[f"A.out{l_}_{b_}"] = (f"out{l_}_{b_}",)
        for m_ in range(2):
            JOBS_OF[f"A.sc{l_}_{b_}_{m_}"] = (f"sc{l_}_{b_}_{m_}",)
            JOBS_OF[f"A.tr{l_}_{b_}_{m_}"] = (f"pT{l_}_{b_}_{m_}",)
    JOBS_OF[f"B.out_{b_}"] = (f"out2_{b_}",)
    for n_ in ("cT", "k2", "v2"):
        JOBS_OF[f"B.{n_}_{b_}"] = (f"{n_}_{b_}",)
    for i_ in range(8):
        JOBS_OF[f"B.sc_{b_}_{i_}"] = (f"sc2_{b_}_{i_}",)
        JOBS_OF[f"B.tr_{b_}_{i_}"] = (f"pT2_{b_}_{i_}",)


def build(nc, x_nat_d, x_t_d, c_nat_d, c_t_d, c_first_d, mask_d, w_d, vec_d, row_d, const_d, out_d):
    ctx = ExitStack()
    with ctx:
        def sb(name, shape, dt=F32):
            return ctx.enter_context(nc.sbuf_tensor(name, shape, dt))

        def sem(name):
            return ctx.enter_context(nc.semaphore(name))

        w0 = {n: sb(n, [128, C, U]) for n in ("wq0", "wk0", "wv0")}
        wshape = {"wqkv1": (C, 3 * U), "wp1": (C, U), "wq2": (C, U), "wkv2": (C, 2 * U), "wp2": (C, U),
                  "w1": (C, 4 * U), "w2": (FF, U)}
        w = {n: sb(n, [128, 2, *s], F32R) for n, s in wshape.items()}
        temps, spare = sb("temps", [128, 4096]), [0]

        def temp(*shape):
            n = int(np.prod(shape))
            at_, spare[0] = spare[0], spare[0] + n
            assert spare[0] <= temps.shape[1]
            names_ = "abcde"[:len(shape)]
            return temps[:, at_:at_ + n].rearrange(f"p ({' '.join(names_)}) -> p {' '.join(names_)}", **dict(zip(names_, shape)))

        vec = sb("vec", [128, vec_d.shape[1]])
        names = ["bq0", "bk0", "g1", "b1", "g3", "b3", "g2", "b2"]
        VEC = {n: 2 * i for i, n in enumerate(names)}
        FB1 = 2 * len(names)
        EO = FB1 + FF
        rowv = {n: sb(n, [T if n != "bv0" else CH, U]) for n in ("bv0", "gamma0", "beta0", "bp1", "bp2")}
        ident = sb("ident", [128, 128])
        ident_b = sb("ident_b", [T, T], BF16)
        causal = sb("causal", [T, T], BF16)
        tril = sb("tril", [T, T], BF16)
        fold = sb("fold", [128, 4 * D])
        mask_u8 = sb("mask_u8", [T, B], U8)
        pad1_all = sb("pad1_all", [T, B])
        eo_scale = sb("eo_scale", [128, 2, 2])
        bq0_eo = sb("bq0_eo", [128, C, 2])
        ones = sb("ones", [128, 1])

        x_nat = sb("x_nat", [T, G, U])
        x_t = sb("x_t", [128, C, G, T])
        c_nat = sb("c_nat", [CH, G, NCH, U])
        c_t = sb("c_t", [128, C, G, T])
        h_tmp = temp(4, G, T)
        ct_tmp = temp(C, SP)
        piece_at = [h_tmp.rearrange("p c b t -> p (c b t)"), temps[:, 4 * G * T:4 * G * T + 3 * U]]
        temp(3 * U - C * SP)
        qf = temp(C, G, 2, T)
        kf = temp(C, G, T)
        v = sb("v", [T, G, H, D])
        n1 = sb("n1", [128, 2, C, G, T], F32R)
        n3 = sb("n3", [128, 2, C, G, T], F32R)
        n_tmp = temp(2, C, G, T)
        o_t = [sb(f"o_t{i}", [128, 2, C, G, T], F32R) for i in range(2)]
        q2_tmp = n_tmp.rearrange("p a c b t -> p (a c b t)").rearrange("p (c b e t) -> p c b e t", c=C, b=G, e=2)
        q2 = sb("q2", [128, 2, C, G, 2, T], F32R)
        ct = sb("ct", [128, 2, C, SP], F32R)
        k2 = sb("k2", [128, 2, C, SP], F32R)
        v2 = sb("v2", [CH, G, NCH, H, D])
        h = sb("h", [128, 2, FF, G, T], F32R)
        NP = 2
        NT = (2, 2)
        probs = [sb("probs0", [T, NP, 2, 4 * T]), sb("probs1", [T, NP, 2, SP])]
        probs_t = [sb("probs_t0", [T, NT[0], 2, 4 * T]),
                   sb("probs_t1", [CH, NT[1], 2, NCH * T])]
        negmax = [temp(G, H)[0:T] for i in range(2)]
        sums = [temp(G, H)[0:T] for i in range(2)]
        acc_sb = [sb(f"acc_sb{i}", [128, 4, T]) for i in range(2)]

        keep0 = sb("keep0", [T, G]); keep0b = sb("keep0b", [T, G], BF16)
        pad0 = sb("pad0", [T, G]); pad1 = sb("pad1", [T, G]); keep1b = sb("keep1b", [T, G], BF16)
        qkeep = sb("qkeep", [T, G]); ksum = sb("ksum", [T, G]); qsum = sb("qsum", [T, G]); seen0 = sb("seen0", [T, G])
        add_mask = sb("add_mask", [T, 2, G, T], BF16)
        valid = sb("valid", [T, G]); rvalid = sb("rvalid", [T, G]); nanf = sb("nanf", [T, G])
        empty = sb("empty", [1, G, T])
        v_all_g = sb("v_all_g", [1, G, U])
        first_keys = x_nat[0:B, 0, :]
        first_sum = sb("first_sum", [B, 1]); first_masked = sb("first_masked", [B, 1])
        any_masked = sb("any_masked", [1, 1], I32)
        gen_v = c_nat[:, 0, 0, :]
        gen_c = x_t[:, :, :, :].rearrange("p c b t -> p (c b t)")[:, 0:C * CH].rearrange("p (c k) -> p c k", c=C)
        c_stats = temp(G * NCH, 6)[0:CH]; c_mv = temp(G * NCH, 2)[0:CH]
        c_rstd = temp(G * NCH)[0:CH]; c_var = temp(G * NCH)[0:CH]; half = sb("half", [CH, 2 * G * NCH])
        stats = sb("stats", [T, G, 6]); mv = sb("mv", [T, G, 2]); rstd = sb("rstd", [T, G]); var_e = sb("var_e", [T, G])
        x1 = sb("x1", [T, G, U]); r1 = sb("r1", [T, G, U])
        sd = sb("sd", [T, G]); sd_r = sb("sd_r", [T, G]); xh = sb("xh", [T, G, U])
        y = v_tmp = xh
        key_nat = sb("key_nat", [T, G, U])
        res = r1
        row = xh[0:1, :, :].rearrange("p b u -> p (b u)")[:, 0:U]
        rowv["fb2"] = x1[:, 0, :]

        def unsplit(i):
            n, t0, t1, c0, c1 = PIECES[i]
            return piece_at[i % 2][:, 0:(t1 - t0) * (c1 - c0)].rearrange("p (a b) -> p a b", a=t1 - t0)

        def weight(i, part):
            n, t0, t1, c0, c1 = PIECES[i]
            return w[n][:, part, t0:t1, c0:c1]

        NR = 3
        ring = [ctx.enter_context(nc.psum_tensor(f"ring{i}", [128, 2, 512], F32)) for i in range(NR)]
        acc = [ctx.enter_context(nc.psum_tensor(f"acc{i}", [128, 4, 128], F32)) for i in range(2)]

        PREP_DVE = 7
        split_hi, split_lo = sem("weights_hi"), sem("weights_lo")
        prep_act = sem("prep_act"); prep_dve = sem("prep_dve"); prep_pool = sem("prep_pool")
        x_loaded, c_loaded, stored = sem("x_loaded"), sem("c_loaded"), sem("stored")
        v_all_stored, first_loaded, first_counted, flag_made = sem("v_all_stored"), sem("first_loaded"), sem("first_counted"), sem("flag_made")
        flag_steps = sem("flag_steps")
        gen_loaded, gen_values, gen_ready, gen_summed, gen_row = (sem(n) for n in ("gen_loaded", "gen_values", "gen_ready", "gen_summed", "gen_row"))
        v_all_d = nc.dram_tensor("v_all", [B, U], F32).ap()
        const_loaded = [sem(f"const_loaded{i}") for i in range(3)]
        w_loaded = [sem(f"loaded_{i}_{p[0]}") for i, p in enumerate(PIECES)]
        w0_loaded = sem("w0_loaded")
        waited = {e.engine: sem(n) for n, e in (("waited_sp", nc.sync), ("waited_dve", nc.vector), ("waited_pool", nc.gpsimd))}
        sig = {}
        OUT0 = 14

        def signal(name, per):
            sig[name] = Signal(sem(name), per, owner[0], len(sig))
            return sig[name]

        owner = [None]

        owner[0] = "scalar"
        a_q0 = signal("q0_biased", 4); a_k0 = signal("k0_biased", 2); a_q1 = signal("q1_scaled", 4); a_k1 = signal("k1_copied", 1)
        a_n = signal("norm13_scaled", 4); a_expA = signal("exponentialsA", 8); a_accA = signal("outputsA_copied", 2 * G)
        a_pt = signal("probs_copiedA", 8); a_ot = signal("out1_hi", G); a_xq = signal("norm2_scaled", 2)
        a_q2 = signal("q2_scaled", 4); a_h = signal("hidden_biased", FF); a_ct = signal("ctx_scaled", 2 * G)
        a_k2 = signal("k2_hi", G); a_expB = signal("exponentialsB", 8 * G)
        a_accB = signal("outputsB_copied", G); a_o2t = signal("out2_hi", G)
        owner[0] = "vector"
        v_mask = signal("masks_made", 8 + 2 * G); v_cnt = signal("counts_read", 5); v_v0 = signal("values0", 2)
        v_max = [signal(f"max{a}", n) for a, n in enumerate((4 * G, 2 * G, 8 * G))]
        v_sum = [signal(f"sums_inverted{a}", n) for a, n in enumerate((4 * G, 2 * G, 8 * G))]
        v_pt = signal("probs_copiedB", 8 * G)
        v_post0 = signal("out0_steps", OUT0 * G); v_n_hi = signal("norm13_hi", 2); v_v1 = signal("values1", 1)
        v_ot_lo = signal("out1_lo", G)
        v_proj = signal("proj_steps", G + 5 * G); v_xq_hi = signal("norm2_hi", 1)
        v_q2_hi = signal("q2_hi", 1); v_h_hi = signal("hidden_hi", 2)
        v_ctxln = signal("ctx_normed", 3 * G * NCH + 1); v_ct_hi = signal("ctx_hi", G); v_k2_lo = signal("k2_lo", G); v_v2 = signal("values2", G)
        v_o2t_lo = signal("out2_lo", G); v_res = signal("result", 1)
        owner[0] = "gpsimd"
        p_rstd = signal("rstd", 3 * G); p_n_lo = signal("norm13_lo", 2); p_xq_lo = signal("norm2_lo", 1)
        p_q2_lo = signal("q2_lo", 1); p_h_lo = signal("hidden_lo", 2); p_crstd = signal("ctx_rstd", 1); p_ct_lo = signal("ctx_lo", G)
        p_normA = signal("probs_normedA", 8); p_normB = signal("probs_normedB", 8 * G); p_r1 = signal("residual_copied", 1)
        owner[0] = "tensor"
        t_pvA = signal("values_summedA", 8); t_pvB = signal("values_summedB", 8 * G)
        psum_filled = sem("psum_filled")

        READER = {"counts": (v_cnt, 3), "q0": (a_q0, 4), "k0": (a_k0, 2), "v0": (v_v0, 1), "xT": (a_n, 4),
                  "q1": (a_q1, 4), "k1": (a_k1, 1), "v1": (v_v1, 1), "proj": (v_proj, G), "xqT": (a_xq, 2),
                  "q2": (a_q2, 4), "h0": (a_h, 4), "h1": (a_h, 8), "y": (v_res, 1)}
        for b in range(G):
            for l in range(2):
                for m in range(2):
                    READER[f"sc{l}_{b}_{m}"] = (a_expA, 4 * l + 2 * b + m + 1)
                    READER[f"pT{l}_{b}_{m}"] = (a_pt, 4 * l + 2 * b + m + 1)
            READER[f"out0_{b}"] = (v_post0, OUT0 * b + 1)
            READER[f"out1_{b}"] = (v_ot_lo, b + 1)
            READER[f"out2_{b}"] = (v_o2t_lo, b + 1)
            READER[f"cT_{b}"] = (a_ct, 2 * b + 2)
            READER[f"k2_{b}"] = (v_k2_lo, b + 1)
            READER[f"v2_{b}"] = (v_v2, b + 1)
            for i in range(8):
                READER[f"sc2_{b}_{i}"] = (a_expB, 8 * b + i + 1)
                READER[f"pT2_{b}_{i}"] = (v_pt, 8 * b + i + 1)
        B_JOBS = {j for s in B_STEPS for j in JOBS_OF.get(s, ())}

        first = Part(FIRST_STEPS, 0)
        order = mixed(A_STEPS, B_STEPS)
        body = Part(order, len(first.jobs), sum(len(JOBS_OF.get(s, ())) for s in order))
        last = Part(B_STEPS, len(first.jobs) + (NG - 1) * len(body.jobs))
        assert max(order.index(s) for s in ("B.q2", "B.h0", "B.h1")) < order.index("A.xT")
        assert order.index("B.q2") < order.index("A.out0_0")

        def home(part, name):
            return ring[part.number[name] % NR]

        def filled_at(part, i, name):
            return i * part.per_turn + (part.first_job + part.number[name] + 1)

        class At:

            def __init__(self, part, i, a, b):
                self.part, self.i, self.a, self.b = part, i, a, b

            def pair(self, name):
                return self.b if name in B_JOBS else self.a

        def is_filled(eng, at, name):
            eng.wait_ge(psum_filled, filled_at(at.part, at.i, name))
            return home(at.part, name)

        def claim(pe, at, name):
            n = at.part.number[name]
            if n >= NR:
                before = at.part.jobs[n - NR]
                s, k = READER[before]
                pe.wait_ge(s.sem, s.at(at.pair(before), k))
                return home(at.part, name)
            for part in {first: (), body: (first, body), last: (body,)}[at.part]:
                before = [j for j in part.jobs if part.number[j] % NR == n][-1]
                s, k = READER[before]
                if before in B_JOBS:
                    pe.wait_ge(s.sem, s.before(at.b))
                else:
                    pe.wait_ge(s.sem, s.done(at.a - 1) if at.part is not last else s.done(NG - 1))
            return home(at.part, name)

        def alone(eng):
            eng.sem_inc(waited[eng.engine], 1)

        made = set()

        def run(eng, steps):
            def go(at):
                for s in sig.values():
                    s.given = 0
                for name in at.part.order:
                    stage, rest = name.split(".")
                    kind, *idx = rest.split("_")
                    if f"{stage}.{kind}" in steps:
                        steps[f"{stage}.{kind}"](at, at.a if stage == "A" else at.b, *map(int, idx))
                for name, s in sig.items():
                    assert s.given in (0, s.per), (name, s.given, s.per)
                    made.update([name] if s.given else [])

            go(At(first, 0, 0, None))
            with eng.Fori(0, NG - 1) as i:
                go(At(body, i, i + 1, i))
            go(At(last, 0, None, NG - 1))

        back = {READER[body.jobs[-1 - n]][0] for n in range(NR) if body.jobs[-1 - n] in B_JOBS}
        back |= {a_expA, a_accA, a_xq, p_h_lo, p_ct_lo, a_accB, v_res}
        for s in back:
            s.start = 1

        def start_signals(eng, letter):
            for s in sorted((s for s in back if s.owner == letter), key=lambda s: s.order):
                eng.sem_inc(s.sem, 1)

        TERMS = ((HI, HI), (HI, LO), (LO, HI))
        block = ctx.enter_context(nc.Block())

        @block.sync
        def _(sp):
            sp.dma_start(vec[:, :], vec_d).then_inc(const_loaded[0], 16)
            sp.dma_start(mask_u8[:, :], mask_d).then_inc(const_loaded[0], 16)
            sp.dma_start(first_keys, c_first_d).then_inc(first_loaded, 16)
            for n, dst in (("causal", causal), ("tril", tril), ("ident_b", ident_b), ("ident", ident), ("fold", fold)):
                sp.dma_start(dst[:, :], const_d[n]).then_inc(const_loaded[1], 16)
            for n in w0:
                sp.dma_start(w0[n][:, :, :], w_d[n].rearrange("(a p) b -> p a b", p=128)).then_inc(w0_loaded, 16)
            for n in rowv:
                sp.dma_start(rowv[n][:, :], row_d[n].unsqueeze(0).to_broadcast([rowv[n].shape[0], U])).then_inc(const_loaded[2], 16)
            sp.wait_ge(prep_dve, 2)
            sp.dma_start(v_all_d.rearrange("b n -> (b n)").unsqueeze(0).rearrange("p (b n) -> p b n", b=B),
                         row.unsqueeze(1).to_broadcast([1, B, U])).then_inc(v_all_stored, 16)
            sp.wait_ge(v_all_stored, 16)
            sp.wait_ge(flag_made, 2)
            with sp.If(sp.value_load(any_masked[0:1, 0:1]) > 0):
                with sp.Fori(0, B) as b:
                    for ch in range(NCH):
                        if ch:
                            sp.wait_ge(gen_values, b * NCH + ch)
                            alone(sp)
                        sp.dma_start(gen_c, c_t_d.rearrange("(c p) t -> p c t", p=128)[:, :, bass.ds(b * S + ch * CH, CH)]).then_inc(gen_loaded, 16)
                    sp.wait_ge(gen_row, b + 1)
                    alone(sp)
                    sp.dma_start(v_all_d[bass.ds(b, 1), :], row).then_inc(v_all_stored, 16)
                    sp.wait_ge(v_all_stored, b * 16 + 32)
                    alone(sp)

            def load_x(g, look_back):
                if look_back:
                    sp.wait_ge(a_q0.sem, a_q0.done(g - 1))
                    alone(sp)
                    sp.wait_ge(a_k0.sem, a_k0.done(g - 1))
                    alone(sp)
                    sp.wait_ge(v_v0.sem, v_v0.done(g - 1))
                    alone(sp)
                    sp.wait_ge(v_post0.sem, v_post0.done(g - 1))
                    alone(sp)
                sp.dma_start(x_t[:, :, :, :].rearrange("p c b t -> p c (b t)"),
                             x_t_d.rearrange("(c p) t -> p c t", p=128)[:, :, bass.ds(g * (G * T), G * T)]).then_inc(x_loaded, 16)
                for b in range(G):
                    sp.dma_start(c_t[:, :, b, :], c_t_d.rearrange("(c p) t -> p c t", p=128)[:, :, bass.ds(g * (G * S) + b * S, T)]).then_inc(x_loaded, 16)
                sp.dma_start(x_nat[:, :, :], x_nat_d[bass.ds(g * G, G), :, :].rearrange("b t f -> t b f")).then_inc(x_loaded, 16)
                sp.dma_start(v_all_g[:, :, :], v_all_d[bass.ds(g * G, G), :].unsqueeze(0)).then_inc(x_loaded, 16)
                sp.dma_start(key_nat[:, :, :], c_nat_d[bass.ds(g * G, G), 0:T, :].rearrange("b t f -> t b f")).then_inc(x_loaded, 16)

            def load_context(g, look_back):
                if look_back:
                    sp.wait_ge(a_ct.sem, a_ct.done(g - 1))
                    alone(sp)
                for b in range(G):
                    sp.dma_start(c_nat[:, b, :, :], c_nat_d.rearrange("b (c p) f -> b p c f", p=CH)[bass.ds(g * G + b, 1), :, :, :].rearrange("b p c f -> (b p) c f")).then_inc(c_loaded, 16)

            def store(g):
                sp.wait_ge(v_res.sem, v_res.done(g))
                alone(sp)
                sp.dma_start(out_d[bass.ds(g * G, G), :, :].rearrange("b t f -> t b f"), res[:, :, :]).then_inc(stored, 16)

            def load_weights(i):
                n, t0, t1, c0, c1 = PIECES[i]
                if i >= 2:
                    sp.wait_ge(split_lo, i - 1)
                sp.dma_start(unsplit(i), w_d[n].rearrange("(a p) b -> p a b", p=128)[:, t0:t1, c0:c1]).then_inc(w_loaded[i], 16)

            sp.sem_inc(stored, 16)
            load_x(0, False)
            for i in range(2):
                load_weights(i)
            load_context(0, False)
            for i in range(2, len(PIECES)):
                load_weights(i)
            load_x(1, True)
            with sp.Fori(0, NG - 2) as i:
                load_context(i + 1, True)
                load_x(i + 2, True)
                store(i)
            load_context(NG - 1, True)
            store(NG - 2)
            store(NG - 1)
            sp.wait_ge(stored, 16 * NG + 16)

        @block.tensor
        def _(pe):
            def end(m):
                m.then_inc(psum_filled, 1)

            def products(pairs, dst, start=True):
                for n, (lhs, rhs) in enumerate(pairs):
                    m = nc.tensor.matmul(dst, lhs, rhs, start=start and n == 0, stop=n == len(pairs) - 1, skip_group_check=True)
                return m

            def flat(t):
                return t.rearrange("p b t -> p (b t)")

            def features_out(at, name, weights, col, act_, tiles=C, per_bank=1, split=True):
                o = claim(pe, at, name)
                for i in range(tiles):
                    cols = slice(col + 128 * i, col + 128 * (i + 1))
                    if split:
                        pairs = [(weights[:, wp, ci, cols], flat(act_[:, ap, ci, :, :])) for ci in range(C) for wp, ap in TERMS]
                    else:
                        pairs = [(weights[:, ci, cols], flat(act_[:, ci, :, :])) for ci in range(C)]
                    m = products(pairs, o[:, i // per_bank, (i % per_bank) * G * T:(i % per_bank + 1) * G * T])
                end(m)

            def tokens_out(at, name, operands):
                o = claim(pe, at, name)
                for b in range(G):
                    m = products(operands(b), o[0:T, b, 0:U])
                end(m)

            def split_pairs(act_, b, weights, col=0, tiles=C):
                return [(act_[:, ap, c, b, :], weights[:, wp, c, col:col + U]) for c in range(tiles) for wp, ap in TERMS]

            def rows_transposed(o, src, post, at_b):
                for b in range(G):
                    pe.wait_ge(post.sem, at_b(b))
                    for c in range(C):
                        m = nc.tensor.transpose(o(c, b), src[:, b, c * 128:(c + 1) * 128], ident[0:T, 0:T])
                end(m)

            def masks(at, g):
                o = claim(pe, at, "counts")
                pe.wait_ge(v_mask.sem, v_mask.done(g))
                for b in range(G):
                    nc.tensor.matmul(o[0:1, 1, b * T:(b + 1) * T], keep0b[:, b:b + 1], tril[:, :], start=b == 0, stop=True, skip_group_check=True)
                nc.tensor.matmul(o[0:T, 0, 0:G], tril[:, :], keep1b[:, :], start=True, stop=True, skip_group_check=True)
                end(nc.tensor.matmul(o[0:T, 0, G:2 * G], tril[:, :], keep0b[:, :], start=False, stop=True, skip_group_check=True))

            def project_q0(at, g):
                pe.wait_ge(x_loaded, g * 96 + 96)
                features_out(at, "q0", w0["wq0"], 0, x_t, split=False)

            def project_k0(at, g):
                features_out(at, "k0", w0["wk0"], 0, c_t, split=False)

            def project_v0(at, g):
                tokens_out(at, "v0", lambda b: [(c_t[:, c, b, :], w0["wv0"][:, c, :]) for c in range(C)])

            def self_scores(at, g, layer, b, m_):
                for s in ((a_q0, a_k0), (a_q1, a_k1))[layer]:
                    pe.wait_ge(s.sem, s.done(g))
                pe.wait_ge(v_mask.sem, v_mask.done(g))
                o = claim(pe, at, f"sc{layer}_{b}_{m_}")
                for jj in range(2):
                    nc.tensor.matmul(o[0:T, jj, 0:4 * T], add_mask[:, layer, b, :], ident_b[:, :].unsqueeze(1).to_broadcast([T, 4, T]),
                                     start=True, stop=False, skip_group_check=True)
                for c in range(C):
                    for e in range(2):
                        for jj in range(2):
                            r = 32 * (2 * m_ + jj)
                            m = nc.tensor.matmul(o[0:T, jj, (2 * c + e) * T:(2 * c + e + 1) * T], qf[r:r + 32, c, b, e, :],
                                                 kf[r:r + 32, c, b, :], start=False, stop=True, skip_group_check=True)
                end(m)

            def self_transposed(at, g, layer, b, m_):
                e_no = 4 * layer + 2 * b + m_
                o = claim(pe, at, f"pT{layer}_{b}_{m_}")
                pe.wait_ge(p_normA.sem, p_normA.at(g, e_no + 1))
                for jj in range(2):
                    for ce in range(4):
                        m = nc.tensor.transpose(o[0:T, jj, ce * T:(ce + 1) * T], probs[0][:, e_no % NP, jj, ce * T:(ce + 1) * T], ident[0:T, 0:T])
                end(m)

            def add_values(stage, hd, vals, ps_t, opens):
                s, p = hd // 4, hd % 4
                return nc.tensor.matmul(acc[stage][32 * p:32 * p + D, s, 0:T], vals, ps_t, start=opens, stop=True,
                                        skip_group_check=True, tile_position=(0, 32 * p))

            def self_sum(at, g, layer, b, m_):
                e_no = 4 * layer + 2 * b + m_
                if m_ == 0:
                    s = (v_v0, v_v1)[layer]
                    pe.wait_ge(s.sem, s.done(g))
                    pe.wait_ge(a_accA.sem, a_accA.at(g, 2 * layer + b))
                pe.wait_ge(a_pt.sem, a_pt.at(g, e_no + 1))
                for jj in range(2):
                    for ce in range(4):
                        hd = 8 * (ce // 2) + 2 * (2 * m_ + jj) + ce % 2
                        m = add_values(0, hd, v[:, b, hd, :], probs_t[0][:, e_no % NT[0], jj, ce * T:(ce + 1) * T], m_ == 0 and ce < 2)
                t_pvA.step(m)

            def out0_folded(at, g, b):
                o = claim(pe, at, f"out0_{b}")
                pe.wait_ge(v_cnt.sem, v_cnt.done(g))
                nc.tensor.matmul(o[0:T, 0, 0:U], empty[:, b, :], v_all_g[:, b, :], start=True, stop=False, skip_group_check=True)
                pe.wait_ge(a_accA.sem, a_accA.at(g, b + 1))
                for i in range(4):
                    m = nc.tensor.matmul(o[0:T, 0, 4 * D * i:4 * D * (i + 1)], acc_sb[0][:, i, :], fold[:, :], start=False, stop=True, skip_group_check=True)
                end(m)

            def out_folded(at, g, name, stage, copied, k_):
                o = claim(pe, at, name)
                pe.wait_ge(copied.sem, copied.at(g, k_))
                for i in range(4):
                    r = 64 * (i % 2)
                    m = nc.tensor.matmul(o[r:r + 64, 0, i // 2 * T:(i // 2 + 1) * T], fold[:, :], acc_sb[stage][:, i, :],
                                         start=i < 2, stop=True, skip_group_check=True, tile_position=(0, r))
                end(m)

            def x_transposed(at, g):
                o = claim(pe, at, "xT")
                rows_transposed(lambda c, b: o[:, c, b * T:(b + 1) * T], xh, v_post0, lambda b: v_post0.at(g, OUT0 * (b + 1) - 1))

            def weights_split(at, g, i):
                pe.wait_ge(split_lo, i + 1)

            def project_q1(at, g):
                pe.wait_ge(p_n_lo.sem, p_n_lo.at(g, 1))
                features_out(at, "q1", w["wqkv1"], 0, n1)

            def project_out1(at, g):
                pe.wait_ge(v_ot_lo.sem, v_ot_lo.done(g))
                tokens_out(at, "proj", lambda b: split_pairs(o_t[0], b, w["wp1"]))

            def xq_transposed(at, g):
                o = claim(pe, at, "xqT")
                rows_transposed(lambda c, b: o[:, c, b * T:(b + 1) * T], xh, v_proj, lambda b: v_proj.at(g, 4 * G + 2 * b + 1))

            def project_q2(at, g):
                pe.wait_ge(p_xq_lo.sem, p_xq_lo.done(g))
                features_out(at, "q2", w["wq2"], 0, n1)

            def hidden(at, g, i):
                pe.wait_ge(p_n_lo.sem, p_n_lo.done(g))
                features_out(at, f"h{i}", w["w1"], 512 * i, n3, tiles=4, per_bank=2)

            def context_transposed(at, g, b):
                o = claim(pe, at, f"cT_{b}")
                pe.wait_ge(v_ctxln.sem, v_ctxln.done(g))
                for c in range(C):
                    for ch in range(NCH):
                        m = nc.tensor.transpose(o[:, c, ch * CH:(ch + 1) * CH], c_nat[0:CH, b, ch, c * 128:(c + 1) * 128], ident[0:CH, 0:CH])
                end(m)

            def project_k2(at, g, b):
                o = claim(pe, at, f"k2_{b}")
                pe.wait_ge(p_ct_lo.sem, p_ct_lo.at(g, b + 1))
                for i in range(C):
                    m = products([(w["wkv2"][:, wp, ci, 128 * i:128 * (i + 1)], ct[:, ap, ci, :]) for ci in range(C) for wp, ap in TERMS], o[:, i, 0:SP])
                end(m)

            def project_v2(at, g, b):
                o = claim(pe, at, f"v2_{b}")
                for ch in range(NCH):
                    m = products([(ct[:, ap, ci, ch * CH:(ch + 1) * CH], w["wkv2"][:, wp, ci, U:2 * U]) for ci in range(C) for wp, ap in TERMS],
                                 o[0:CH, ch // 2, (ch % 2) * U:(ch % 2 + 1) * U], start=ch % 2 == 0)
                end(m)

            def cross_scores(at, g, b, i):
                o = claim(pe, at, f"sc2_{b}_{i}")
                pe.wait_ge(p_q2_lo.sem, p_q2_lo.done(g))
                pe.wait_ge(v_k2_lo.sem, v_k2_lo.at(g, b + 1))
                c, e = (i % 4) // 2, i % 2
                for n, (qp, kp) in enumerate(TERMS):
                    for jj in range(2):
                        r = 32 * (2 * (i // 4) + jj)
                        m = nc.tensor.matmul(o[0:T, jj, 0:SP], q2[r:r + 32, qp, c, b, e, :], k2[r:r + 32, kp, c, :], start=n == 0, stop=n == 2)
                end(m)

            def cross_transposed(at, g, b, i):
                o = claim(pe, at, f"pT2_{b}_{i}")
                pe.wait_ge(p_normB.sem, p_normB.at(g, 8 * b + i + 1))
                for jj in range(2):
                    for ch in range(NCH):
                        m = nc.tensor.transpose(o[0:CH, jj, ch * T:(ch + 1) * T], probs[1][:, i % NP, jj, ch * CH:(ch + 1) * CH], ident[0:T, 0:T])
                end(m)

            def cross_sum(at, g, b, i):
                if i == 0:
                    pe.wait_ge(v_v2.sem, v_v2.at(g, b + 1))
                    pe.wait_ge(a_accB.sem, a_accB.at(g, b))
                pe.wait_ge(v_pt.sem, v_pt.at(g, 8 * b + i + 1))
                for jj in range(2):
                    hd = 8 * (i % 4 // 2) + 2 * (2 * (i // 4) + jj) + i % 2
                    for ch in range(NCH):
                        m = add_values(1, hd, v2[:, b, ch, hd, :], probs_t[1][:, i % NT[1], jj, ch * T:(ch + 1) * T], i < 2 and ch == 0)
                t_pvB.step(m)

            def project_y(at, g):
                pe.wait_ge(v_o2t_lo.sem, v_o2t_lo.done(g))
                pe.wait_ge(p_h_lo.sem, p_h_lo.done(g))
                tokens_out(at, "y", lambda b: split_pairs(h, b, w["w2"], tiles=FF) + split_pairs(o_t[1], b, w["wp2"]))

            pe.wait_ge(flag_made, 1)
            nc.tensor.matmul(ring[0][0:1, 0, 0:1], first_masked[:, :], ones[0:B, :], start=True, stop=True).then_inc(first_counted, 1)
            pe.wait_ge(const_loaded[1], 80)
            pe.wait_ge(w0_loaded, 16 * len(w0))
            pe.wait_ge(prep_dve, PREP_DVE)
            pe.wait_ge(flag_made, 2)
            with pe.If(pe.value_load(any_masked[0:1, 0:1]) > 0):
                with pe.Fori(0, B) as b:
                    for ch in range(NCH):
                        pe.wait_ge(gen_loaded, b * (16 * NCH) + 16 * ch + 16)
                        for ci in range(C):
                            m = nc.tensor.matmul(ring[1][0:CH, 0, 0:U], gen_c[:, ci, :], w0["wv0"][:, ci, :], start=ci == 0, stop=ci == C - 1)
                        m.then_inc(gen_values, 1)
                        pe.wait_ge(gen_ready, b * (2 * NCH) + 2 * ch + 2)
                        m = nc.tensor.matmul(ring[2][0:1, 0, 0:U], ones[0:CH, :], gen_v[:, :], start=ch == 0, stop=ch == NCH - 1)
                    m.then_inc(gen_summed, 1)
                    pe.wait_ge(gen_row, b + 1)
            run(pe, {"W.ready": weights_split,
                "A.masks": masks, "A.q0": project_q0, "A.k0": project_k0, "A.v0": project_v0,
                "A.sc0": lambda at, g, b, m_: self_scores(at, g, 0, b, m_), "A.sc1": lambda at, g, b, m_: self_scores(at, g, 1, b, m_),
                "A.tr0": lambda at, g, b, m_: self_transposed(at, g, 0, b, m_), "A.tr1": lambda at, g, b, m_: self_transposed(at, g, 1, b, m_),
                "A.pv0": lambda at, g, b, m_: self_sum(at, g, 0, b, m_), "A.pv1": lambda at, g, b, m_: self_sum(at, g, 1, b, m_),
                "A.out0": out0_folded, "A.xT": x_transposed, "A.q1": project_q1,
                "A.k1": lambda at, g: features_out(at, "k1", w["wqkv1"], U, n1),
                "A.v1": lambda at, g: tokens_out(at, "v1", lambda b: split_pairs(n1, b, w["wqkv1"], 2 * U)),
                "A.out1": lambda at, g, b: out_folded(at, g, f"out1_{b}", 0, a_accA, 2 + b + 1), "A.proj": project_out1, "A.xqT": xq_transposed,
                "B.q2": project_q2, "B.h0": lambda at, g: hidden(at, g, 0), "B.h1": lambda at, g: hidden(at, g, 1),
                "B.cT": context_transposed, "B.k2": project_k2, "B.v2": project_v2, "B.sc": cross_scores, "B.tr": cross_transposed,
                "B.pv": cross_sum, "B.out": lambda at, g, b: out_folded(at, g, f"out2_{b}", 1, a_accB, b + 1), "B.y": project_y})

        @block.scalar
        def _(act):
            def two_heads(at, name, s, dst, scale, bias):
                o = is_filled(act, at, name)
                for c in range(C):
                    for e in range(2):
                        src = o[:, c, 0:G * T].rearrange("p (b t) -> p b t", b=G)
                        f = ACT.Identity if bias is None else ACT.Relu
                        s.step(nc.scalar.activation(dst[:, c, :, e, :], src, f, bias=0.0 if bias is None else bias[:, c, e:e + 1],
                                                    scale=eo_scale[:, scale, e:e + 1]))

            def affine(at, name, s, dst, scale, bias, func=ACT.Identity):
                o = is_filled(act, at, name)
                for c in range(C):
                    s.step(nc.scalar.activation(dst[:, c, :, :].rearrange("p b t -> p (b t)"), o[:, c, 0:G * T], func, bias=bias(c), scale=scale(c)))

            def col(name):
                return lambda c: vec[:, VEC[name] + c:VEC[name] + c + 1]

            def exponentials(at, g, name, stage, s, e_no, b, cols, maxima, before):
                o = is_filled(act, at, name)
                act.wait_ge(maxima[0].sem, maxima[0].at(g, maxima[1]))
                if before is not None:
                    is_filled(act, at, before)
                per, n = (4, T) if stage == 0 else (1, S)
                for x in range(2 * per):
                    jj, a = divmod(x, per)
                    m = nc.scalar.activation(probs[stage][:, e_no % NP, jj, a * n:(a + 1) * n], o[0:T, jj, a * n:(a + 1) * n], ACT.Exp,
                                             bias=negmax[stage][:, b, cols + x:cols + x + 1], accum_out=sums[stage][:, b, cols + x:cols + x + 1])
                s.step(m)

            def name_of(layer, n, per_b):
                return f"pT{layer}_{n // per_b}_{n % per_b}"

            def self_exp(at, g, layer, b, m_):
                n = 2 * b + m_
                exponentials(at, g, f"sc{layer}_{b}_{m_}", 0, a_expA, 4 * layer + n, b, 8 * m_, (v_max[layer], (2 - layer) * (n + 1)),
                             name_of(layer, n - NP, 2) if n >= NP else None)

            def cross_exp(at, g, b, i):
                n = 8 * b + i
                exponentials(at, g, f"sc2_{b}_{i}", 1, a_expB, n, b, 2 * i, (v_max[2], n + 1), name_of(2, n - NP, 8) if n >= NP else None)

            def copy_probs(at, g, layer, b, m_):
                n = 4 * layer + 2 * b + m_
                if n >= NT[0]:
                    act.wait_ge(t_pvA.sem, t_pvA.at(g, n - NT[0] + 1))
                a_pt.step(nc.scalar.activation(probs_t[0][:, n % NT[0], :, :], is_filled(act, at, f"pT{layer}_{b}_{m_}")[0:T, :, 0:4 * T], ACT.Copy))

            def copy_out(s, used, last_sum, stage):
                act.wait_ge(used.sem, last_sum)
                s.step(nc.scalar.activation(acc_sb[stage][:, :, :], acc[stage][:, :, 0:T], ACT.Copy))

            def out_hi(at, name, s, stage, b):
                s.step(nc.scalar.activation(o_t[stage][:, HI, :, b, :], is_filled(act, at, name)[:, 0, 0:C * T].rearrange("p (c t) -> p c t", c=C), ACT.Copy))

            def self_out(at, g, layer, b):
                copy_out(a_accA, t_pvA, t_pvA.at(g, 4 * layer + 2 * b + 2), 0)
                if layer == 1:
                    out_hi(at, f"out1_{b}", a_ot, 0, b)

            def cross_out(at, g, b):
                copy_out(a_accB, t_pvB, t_pvB.at(g, 8 * b + 8), 1)
                out_hi(at, f"out2_{b}", a_o2t, 1, b)

            def normed(at, g):
                if at.b is not None:
                    act.wait_ge(p_q2_lo.sem, p_q2_lo.done(at.b))
                affine(at, "xT", a_n, n_tmp[:, 0], col("g1"), col("b1"))
                affine(at, "xT", a_n, n_tmp[:, 1], col("g3"), col("b3"))

            def copy_k1(at, g):
                a_k1.step(nc.scalar.activation(kf[:, :, :, :].rearrange("p c b t -> p c (b t)"), is_filled(act, at, "k1")[:, :, 0:G * T], ACT.Copy))

            def scale_q2(at, g):
                act.wait_ge(p_n_lo.sem, p_n_lo.done(g))
                two_heads(at, "q2", a_q2, q2_tmp, 1, None)

            def hidden(at, g, i0):
                act.wait_ge(p_h_lo.sem, p_h_lo.at(g, i0))
                o = is_filled(act, at, f"h{i0}")
                for i in range(4):
                    a_h.step(nc.scalar.activation(h_tmp[:, i, :, :].rearrange("p b t -> p (b t)"), o[:, i // 2, (i % 2) * G * T:(i % 2 + 1) * G * T],
                                                  ACT.Relu, bias=vec[:, FB1 + 4 * i0 + i:FB1 + 4 * i0 + i + 1]))

            def context(at, g, b):
                act.wait_ge(p_ct_lo.sem, p_ct_lo.at(g, b))
                o = is_filled(act, at, f"cT_{b}")
                for c in range(C):
                    a_ct.step(nc.scalar.activation(ct_tmp[:, c, 0:S], o[:, c, 0:S], ACT.Identity, bias=col("b2")(c), scale=col("g2")(c)))

            def k2_hi(at, g, b):
                a_k2.step(nc.scalar.activation(k2[:, HI, :, :], is_filled(act, at, f"k2_{b}")[:, :, 0:SP], ACT.Copy))

            start_signals(act, "scalar")
            act.wait_ge(const_loaded[0], 32)
            for i in range(2):
                nc.scalar.activation(eo_scale[:, i, :], vec[:, EO:EO + 2], ACT.Copy, scale=(0.25, 0.0625)[i]).then_inc(prep_act, 1)
            act.wait_ge(prep_act, 2)
            act.wait_ge(prep_dve, PREP_DVE)
            run(act, {
                "A.q0": lambda at, g: two_heads(at, "q0", a_q0, qf, 0, bq0_eo),
                "A.k0": lambda at, g: affine(at, "k0", a_k0, kf, lambda c: 1.0, col("bk0"), ACT.Relu),
                "A.sc0": lambda at, g, b, m_: self_exp(at, g, 0, b, m_), "A.sc1": lambda at, g, b, m_: self_exp(at, g, 1, b, m_),
                "A.tr0": lambda at, g, b, m_: copy_probs(at, g, 0, b, m_), "A.tr1": lambda at, g, b, m_: copy_probs(at, g, 1, b, m_),
                "A.out0": lambda at, g, b: self_out(at, g, 0, b), "A.xT": normed,
                "A.q1": lambda at, g: two_heads(at, "q1", a_q1, qf, 1, None), "A.k1": copy_k1,
                "A.out1": lambda at, g, b: self_out(at, g, 1, b),
                "A.xqT": lambda at, g: affine(at, "xqT", a_xq, n_tmp[:, 0], col("g2"), col("b2")),
                "B.q2": scale_q2, "B.h0": lambda at, g: hidden(at, g, 0), "B.h1": lambda at, g: hidden(at, g, 1),
                "B.cT": context, "B.k2": k2_hi,
                "B.sc": cross_exp, "B.out": cross_out})

        @block.vector
        def _(dve):
            def after(s, g):
                dve.wait_ge(s.sem, s.at(g, s.given))

            def flat(t):
                return t.rearrange("p c b t -> p (c b t)")

            def high(s, g, a_s, k_, dst, src):
                dve.wait_ge(a_s.sem, a_s.at(g, k_))
                s.step(nc.vector.tensor_copy(dst, src))

            def masks(at, g):
                s = v_mask
                dve.wait_ge(x_loaded, g * 96 + 96)
                dve.wait_ge(a_expA.sem, a_expA.before(g))
                s.step(nc.vector.reduce_sum(ksum[:, :], key_nat[:, :, :], AX.X))
                s.step(nc.vector.reduce_sum(qsum[:, :], x_nat[:, :, :], AX.X))
                s.step(nc.vector.tensor_copy(pad1[:, :], pad1_all[:, bass.ds(g * G, G)]))
                after(s, g)
                s.step(nc.vector.tensor_scalar(keep0[:, :], ksum[:, :], 0.0, None, ALU.not_equal))
                s.step(nc.vector.tensor_scalar(keep0b[:, :], ksum[:, :], 0.0, None, ALU.not_equal))
                s.step(nc.vector.tensor_scalar(pad0[:, :], ksum[:, :], 0.0, BIG, ALU.is_equal, ALU.mult))
                s.step(nc.vector.tensor_scalar(qkeep[:, :], qsum[:, :], 0.0, None, ALU.not_equal))
                s.step(nc.vector.tensor_scalar(keep1b[:, :], pad1[:, :], 0.0, None, ALU.is_equal))
                after(s, g)
                for b in range(G):
                    s.step(nc.vector.tensor_scalar(add_mask[:, 0, b, :], causal[:, :], pad0[:, b:b + 1], None, ALU.min))
                    s.step(nc.vector.tensor_scalar(add_mask[:, 1, b, :], causal[:, :], pad1[:, b:b + 1], None, ALU.min))
                o = is_filled(dve, at, "counts")
                s = v_cnt
                s.step(nc.vector.tensor_scalar(valid[:, :], o[0:T, 0, 0:G], 1.0, None, ALU.min))
                s.step(nc.vector.tensor_scalar(empty[:, :, :].rearrange("p b t -> p (b t)"), o[0:1, 1, 0:G * T], 0.0, 1.0 / S, ALU.is_equal, ALU.mult))
                s.step(nc.vector.tensor_scalar(seen0[:, :], o[0:T, 0, G:2 * G], 1.0, None, ALU.min))
                after(s, g)
                s.step(nc.vector.reciprocal(rvalid[:, :], valid[:, :]))
                after(s, g)
                s.step(nc.vector.tensor_tensor(nanf[:, :], valid[:, :], rvalid[:, :], ALU.mult))

            def values0(at, g):
                o = is_filled(dve, at, "v0")
                dve.wait_ge(a_xq.sem, a_xq.before(g))
                v_v0.step(nc.vector.tensor_tensor(v_tmp[:, :, :], o[0:T, :, 0:U], rowv["bv0"][0:T, :].unsqueeze(1).to_broadcast([T, G, U]), ALU.add))
                after(v_v0, g)
                o = v_tmp[:, :, :].rearrange("p b (h d) -> p b h d", h=H)
                v_v0.step(nc.vector.tensor_scalar(v[:, :, :, :], o, 0.0, None, ALU.max))

            def self_maxima(at, g, layer, b, m_):
                o, s, cols = is_filled(dve, at, f"sc{layer}_{b}_{m_}"), v_max[layer], slice(8 * m_, 8 * m_ + 8)
                s.step(nc.vector.tensor_reduce(negmax[0][:, b, cols], o[0:T, :, 0:4 * T].rearrange("p j (a t) -> p j a t", a=4), AX.X, ALU.max, negate=True))
                if layer == 0:
                    after(s, g)
                    s.step(nc.vector.tensor_scalar(negmax[0][:, b, cols], negmax[0][:, b, cols], seen0[:, b:b + 1], None, ALU.mult))

            def sums_inverted(s, g, stage, b, first_, n, a_s, k_, floor):
                to = sums[stage][:, b, first_:first_ + n]
                dve.wait_ge(a_s.sem, a_s.at(g, k_))
                if floor:
                    s.step(nc.vector.tensor_scalar(to, to, 0.5, None, ALU.max))
                    after(s, g)
                s.step(nc.vector.reciprocal(to, to))

            def self_sums(at, g, layer, b, m_):
                sums_inverted(v_sum[layer], g, 0, b, 8 * m_, 8, a_expA, 4 * layer + 2 * b + m_ + 1, layer == 0)

            def cross_sums(at, g, b, i):
                sums_inverted(v_sum[2], g, 1, b, 2 * i, 2, a_expB, 8 * b + i + 1, False)

            def copy_probs(at, g, b, i):
                n = 8 * b + i
                if n >= NT[1]:
                    dve.wait_ge(t_pvB.sem, t_pvB.at(g, n - NT[1] + 1))
                v_pt.step(nc.vector.tensor_copy(probs_t[1][:, n % NT[1], :, :], is_filled(dve, at, f"pT2_{b}_{i}")[0:CH, :, 0:NCH * T]))

            def statistics(s, g, src, b):
                s.step(nc.vector.bn_stats(stats[0:T, b, :], src))
                after(s, g)
                alone(dve)
                s.step(nc.vector.bn_aggr(mv[0:T, b, :], stats[0:T, b, :]))
                after(s, g)

            def out0(at, g, b):
                s = v_post0
                if at.b is not None:
                    dve.wait_ge(p_r1.sem, p_r1.done(at.b))
                o = is_filled(dve, at, f"out0_{b}")
                s.step(nc.vector.scalar_tensor_tensor(x1[:, b, :], o[0:T, 0, 0:U], qkeep[:, b:b + 1], x_nat[:, b, :], ALU.mult, ALU.add))
                after(s, g)
                statistics(s, g, x1[:, b, :], b)
                s.step(nc.vector.tensor_scalar(sd[:, b:b + 1], mv[0:T, b, 1:2], U / (U - 1), None, ALU.mult))

            def deviation0(at, g, b):
                s = v_post0
                dve.wait_ge(p_rstd.sem, p_rstd.at(g, 2 * b + 1))
                s.step(nc.vector.tensor_scalar(sd[:, b:b + 1], sd_r[:, b:b + 1], 1e-8, None, ALU.add))
                after(s, g)
                s.step(nc.vector.reciprocal(sd_r[:, b:b + 1], sd[:, b:b + 1]))
                after(s, g)
                s.step(nc.vector.tensor_scalar(y[:, b, :], x1[:, b, :], mv[0:T, b, 0:1], sd_r[:, b:b + 1], ALU.subtract, ALU.mult))
                after(s, g)
                s.step(nc.vector.tensor_tensor(y[:, b, :], y[:, b, :], rowv["gamma0"][:, :], ALU.mult))
                after(s, g)
                s.step(nc.vector.tensor_tensor(x1[:, b, :], y[:, b, :], rowv["beta0"][:, :], ALU.add))
                after(s, g)
                statistics(s, g, x1[:, b, :], b)
                s.step(nc.vector.tensor_scalar(var_e[0:T, b:b + 1], mv[0:T, b, 1:2], 1e-5, None, ALU.add))

            def norm1(at, g, b):
                s = v_post0
                dve.wait_ge(p_rstd.sem, p_rstd.at(g, 2 * b + 2))
                s.step(nc.vector.tensor_scalar(xh[:, b, :], x1[:, b, :], mv[0:T, b, 0:1], rstd[0:T, b:b + 1], ALU.subtract, ALU.mult))
                s.step(nc.vector.tensor_tensor(x1[:, b, :], x1[:, b, :], rowv["bp1"][:, :], ALU.add))

            def norm_hi(at, g):
                high(v_n_hi, g, a_n, 2, flat(n1[:, HI]), flat(n_tmp[:, 0]))
                high(v_n_hi, g, a_n, 4, flat(n3[:, HI]), flat(n_tmp[:, 1]))

            def values1(at, g):
                o = is_filled(dve, at, "v1")[0:T, :, 0:U].rearrange("p b (h d) -> p b h d", h=H)
                v_v1.step(nc.vector.tensor_copy(v[:, :, :, :], o))

            def out_lo(at, g, stage, b, s, a_s, name):
                dve.wait_ge(a_s.sem, a_s.at(g, b + 1))
                s.step(nc.vector.tensor_tensor(o_t[stage][:, LO, :, b, :], is_filled(dve, at, name)[:, 0, 0:C * T].rearrange("p (c t) -> p c t", c=C),
                                               o_t[stage][:, HI, :, b, :].bitcast(F32), ALU.subtract))

            def residual1(at, g):
                s = v_proj
                o = is_filled(dve, at, "proj")
                dve.wait_ge(v_post0.sem, v_post0.done(g))
                for b in range(G):
                    s.step(nc.vector.tensor_tensor(x1[:, b, :], o[0:T, b, 0:U], x1[:, b, :], ALU.add))
                after(s, g)
                for b in range(G):
                    statistics(s, g, x1[:, b, :], b)
                    s.step(nc.vector.tensor_scalar(var_e[0:T, b:b + 1], mv[0:T, b, 1:2], 1e-5, None, ALU.add))

            def norm2(at, g):
                s = v_proj
                for b in range(G):
                    dve.wait_ge(p_rstd.sem, p_rstd.at(g, 2 * G + b + 1))
                    s.step(nc.vector.tensor_scalar(xh[:, b, :], x1[:, b, :], mv[0:T, b, 0:1], rstd[0:T, b:b + 1], ALU.subtract, ALU.mult))
                    s.step(nc.vector.scalar_tensor_tensor(x1[:, b, :], x1[:, b, :], nanf[:, b:b + 1], rowv["bp2"][:, :], ALU.mult, ALU.add))

            def query2_hi(at, g):
                high(v_q2_hi, g, a_q2, 4, q2[:, HI].rearrange("p c b e t -> p (c b e t)"), q2_tmp[:, :, :, :, :].rearrange("p c b e t -> p (c b e t)"))

            def hidden_hi(at, g, i):
                high(v_h_hi, g, a_h, 4 * (i + 1), flat(h[:, HI, 4 * i:4 * (i + 1)]), flat(h_tmp[:, :, :, :]))

            def context_statistics(at, g):
                s = v_ctxln
                dve.wait_ge(c_loaded, g * 32 + 32)
                for i in range(G * NCH):
                    s.step(nc.vector.bn_stats(c_stats[:, i, :], c_nat[:, i // NCH, i % NCH, :]))
                after(s, g)
                alone(dve)
                for i in range(G * NCH):
                    s.step(nc.vector.bn_aggr(c_mv[:, i, :], c_stats[:, i, :]))
                after(s, g)
                s.step(nc.vector.tensor_scalar(c_var[:, :], c_mv[:, :, 1], 1e-5, None, ALU.add))

            def context_normed(at, g):
                dve.wait_ge(p_crstd.sem, p_crstd.done(g))
                for i in range(G * NCH):
                    v_ctxln.step(nc.vector.tensor_scalar(c_nat[0:CH, i // NCH, i % NCH, :], c_nat[:, i // NCH, i % NCH, :],
                                                         c_mv[:, i, 0:1], c_rstd[:, i:i + 1], ALU.subtract, ALU.mult))

            def context_hi(at, g, b):
                if b:
                    is_filled(dve, at, f"v2_{b - 1}")
                high(v_ct_hi, g, a_ct, 2 * b + 2, ct[:, HI, :, :], ct_tmp[:, :, :])

            def k2_lo(at, g, b):
                dve.wait_ge(a_k2.sem, a_k2.at(g, b + 1))
                v_k2_lo.step(nc.vector.tensor_tensor(k2[:, LO, :, :], is_filled(dve, at, f"k2_{b}")[:, :, 0:SP], k2[:, HI, :, :].bitcast(F32), ALU.subtract))

            def values2(at, g, b):
                o = is_filled(dve, at, f"v2_{b}")
                v_v2.step(nc.vector.tensor_copy(v2[:, b, :, :, :], o[0:CH, :, :].rearrange("p j n -> p (j n)")[:, 0:NCH * U].rearrange("p (n h d) -> p n h d", n=NCH, h=H)))

            def cross_maxima(at, g, b, i):
                v_max[2].step(nc.vector.tensor_reduce(negmax[1][:, b, 2 * i:2 * i + 2], is_filled(dve, at, f"sc2_{b}_{i}")[0:T, :, 0:S], AX.X, ALU.max, negate=True))

            def result(at, g):
                o = is_filled(dve, at, "y")
                dve.wait_ge(p_r1.sem, p_r1.done(g))
                v_res.step(nc.vector.tensor_tensor(res[:, :, :], o[0:T, :, 0:U], r1[:, :, :], ALU.add))

            def split_weights(at, g, i):
                dve.wait_ge(w_loaded[i], 16)
                nc.vector.tensor_copy(weight(i, HI), unsplit(i)).then_inc(split_hi, 1)
                if i == len(PIECES) - 1:
                    dve.wait_ge(split_lo, i + 1)
                    nc.vector.memset(ct_tmp[:, :, S:SP], 0.0).then_inc(prep_dve, 1)

            start_signals(dve, "vector")
            dve.wait_ge(const_loaded[0], 32)
            nc.vector.tensor_scalar(pad1_all[:, :], mask_u8[:, :], BIG, None, ALU.mult).then_inc(prep_dve, 1)
            nc.vector.memset(row, 0.0).then_inc(prep_dve, 1)
            for i in range(2):
                nc.vector.memset(acc[i][:, :, :], 0.0).then_inc(prep_dve, 1)
            nc.vector.memset(ones[:, :], 1.0).then_inc(flag_steps, 1)
            dve.wait_ge(first_loaded, 16)
            nc.vector.reduce_sum(first_sum[:, :], first_keys, AX.X).then_inc(flag_steps, 1)
            dve.wait_ge(flag_steps, 2)
            nc.vector.tensor_scalar(first_masked[:, :], first_sum[:, :], 0.0, None, ALU.is_equal).then_inc(flag_made, 1)
            dve.wait_ge(first_counted, 1)
            nc.vector.tensor_copy(any_masked[:, :], ring[0][0:1, 0, 0:1]).then_inc(flag_made, 1)
            dve.wait_ge(prep_act, 2)
            for e in range(2):
                nc.vector.tensor_scalar(bq0_eo[:, :, e], vec[:, VEC["bq0"]:VEC["bq0"] + C], eo_scale[:, 0, e:e + 1], None, ALU.mult).then_inc(prep_dve, 1)
            dve.wait_ge(const_loaded[2], 16 * len(rowv))
            nc.vector.tensor_tensor(rowv["bp2"][:, :], rowv["bp2"][:, :], rowv["fb2"][:, :], ALU.add).then_inc(prep_dve, 1)
            dve.wait_ge(prep_dve, PREP_DVE)
            dve.wait_ge(const_loaded[1], 80)
            dve.wait_ge(flag_made, 2)
            with dve.If(dve.value_load(any_masked[0:1, 0:1]) > 0):
                with dve.Fori(0, B) as b:
                    for ch in range(NCH):
                        dve.wait_ge(gen_values, b * NCH + ch + 1)
                        nc.vector.tensor_tensor(gen_v[:, :], ring[1][0:CH, 0, 0:U], rowv["bv0"][:, :], ALU.add).then_inc(gen_ready, 1)
                        dve.wait_ge(gen_ready, b * (2 * NCH) + 2 * ch + 1)
                        nc.vector.tensor_scalar(gen_v[:, :], gen_v[:, :], 0.0, None, ALU.max).then_inc(gen_ready, 1)
                    dve.wait_ge(gen_summed, b + 1)
                    dve.wait_ge(v_all_stored, b * 16 + 16)
                    nc.vector.tensor_copy(row, ring[2][0:1, 0, 0:U]).then_inc(gen_row, 1)
            run(dve, {"W.split": split_weights,
                "A.masks": masks, "A.v0": values0, "A.sc0": lambda at, g, b, m_: self_maxima(at, g, 0, b, m_), "A.nm0": lambda at, g, b, m_: self_sums(at, g, 0, b, m_),
                "A.out0": out0, "A.xT": norm_hi, "A.v1": values1, "A.sc1": lambda at, g, b, m_: self_maxima(at, g, 1, b, m_),
                "A.nm1": lambda at, g, b, m_: self_sums(at, g, 1, b, m_),
                "A.out1": lambda at, g, b: out_lo(at, g, 0, b, v_ot_lo, a_ot, f"out1_{b}"), "A.proj": residual1, "A.dev": deviation0, "A.norm": norm1, "A.norm2": norm2,
                "A.xqT": lambda at, g: high(v_xq_hi, g, a_xq, 2, flat(n1[:, HI]), flat(n_tmp[:, 0])),
                "B.q2": query2_hi, "B.norm": context_statistics, "B.scale": context_normed,
                "B.h0": lambda at, g: hidden_hi(at, g, 0), "B.h1": lambda at, g: hidden_hi(at, g, 1), "B.cT": context_hi,
                "B.k2": k2_lo, "B.v2": values2, "B.sc": cross_maxima, "B.nm": cross_sums,
                "B.tr": copy_probs,
                "B.out": lambda at, g, b: out_lo(at, g, 1, b, v_o2t_lo, a_o2t, f"out2_{b}"), "B.y": result})

        @block.gpsimd
        def _(pool):
            def flat(t):
                return t.rearrange("p c b t -> p (c b t)")

            def low(s, g, v_s, k_, dst, src, hi):
                pool.wait_ge(v_s.sem, v_s.at(g, k_))
                s.step(nc.gpsimd.tensor_tensor(dst, src, hi.bitcast(F32), ALU.subtract))

            def power(s, out, in_, neg, n):
                base = 0 if neg else G * NCH
                s.step(nc.gpsimd.tensor_tensor(out, in_, half[0:out.shape[0], base:base + n], ALU.pow))

            def deviation0(at, g, b):
                pool.wait_ge(v_post0.sem, v_post0.at(g, OUT0 * b + 4))
                power(p_rstd, sd_r[:, b:b + 1], sd[:, b:b + 1], False, 1)

            def deviation1(at, g, b):
                pool.wait_ge(v_post0.sem, v_post0.at(g, OUT0 * b + 12))
                power(p_rstd, rstd[0:T, b:b + 1], var_e[0:T, b:b + 1], True, 1)

            def norm_lo(at, g):
                low(p_n_lo, g, v_n_hi, 1, flat(n1[:, LO]), flat(n_tmp[:, 0]), flat(n1[:, HI]))
                low(p_n_lo, g, v_n_hi, 2, flat(n3[:, LO]), flat(n_tmp[:, 1]), flat(n3[:, HI]))

            def deviations2(at, g):
                for b in range(G):
                    pool.wait_ge(v_proj.sem, v_proj.at(g, G + 3 * b + 3))
                    power(p_rstd, rstd[0:T, b:b + 1], var_e[0:T, b:b + 1], True, 1)

            def context_deviations(at, g):
                pool.wait_ge(v_ctxln.sem, v_ctxln.at(g, 2 * G * NCH + 1))
                power(p_crstd, c_rstd[:, :], c_var[:, :], True, G * NCH)

            def normed(s, g, stage, b, first_, e_no, v_s, k_):
                pool.wait_ge(v_s.sem, v_s.at(g, k_))
                per, n = (4, T) if stage == 0 else (1, S)
                to = probs[stage][:, e_no % NP, :, 0:per * n].rearrange("p j (a t) -> p j a t", a=per)
                by = sums[stage][:, b, first_:first_ + 2 * per].rearrange("p (j a) -> p j a", j=2).unsqueeze(3).to_broadcast([T, 2, per, n])
                s.step(nc.gpsimd.tensor_tensor(to, to, by, ALU.mult))

            def residual_copied(at, g):
                pool.wait_ge(v_proj.sem, v_proj.done(g))
                alone(pool)
                pool.wait_ge(stored, g * 16 + 16)
                alone(pool)
                p_r1.step(nc.gpsimd.tensor_copy(r1[:, :, :], x1[:, :, :]))

            def query2_lo(at, g):
                residual_copied(at, g)
                low(p_q2_lo, g, v_q2_hi, 1, q2[:, LO].rearrange("p c b e t -> p (c b e t)"), q2_tmp[:, :, :, :, :].rearrange("p c b e t -> p (c b e t)"),
                    q2[:, HI].rearrange("p c b e t -> p (c b e t)"))

            def hidden_lo(at, g, i):
                low(p_h_lo, g, v_h_hi, i + 1, flat(h[:, LO, 4 * i:4 * (i + 1)]), flat(h_tmp[:, :, :, :]), flat(h[:, HI, 4 * i:4 * (i + 1)]))

            def split_weights(at, g, i):
                if i == 0:
                    pool.wait_ge(prep_pool, 2)
                pool.wait_ge(split_hi, i + 1)
                nc.gpsimd.tensor_tensor(weight(i, LO), unsplit(i), weight(i, HI).bitcast(F32), ALU.subtract).then_inc(split_lo, 1)

            start_signals(pool, "gpsimd")
            nc.gpsimd.memset(half[:, 0:G * NCH], -0.5).then_inc(prep_pool, 1)
            nc.gpsimd.memset(half[:, G * NCH:2 * G * NCH], 0.5).then_inc(prep_pool, 1)
            run(pool, {"W.split": split_weights,
                "A.nm0": lambda at, g, b, m_: normed(p_normA, g, 0, b, 8 * m_, 2 * b + m_, v_sum[0], 2 * (2 * b + m_ + 1)),
                "A.nm1": lambda at, g, b, m_: normed(p_normA, g, 0, b, 8 * m_, 4 + 2 * b + m_, v_sum[1], 2 * b + m_ + 1),
                "B.nm": lambda at, g, b, i: normed(p_normB, g, 1, b, 2 * i, 8 * b + i, v_sum[2], 8 * b + i + 1),
                "A.out0": deviation0, "A.dev": deviation1, "A.xT": norm_lo, "A.proj": deviations2,
                "A.xqT": lambda at, g: low(p_xq_lo, g, v_xq_hi, 1, flat(n1[:, LO]), flat(n_tmp[:, 0]), flat(n1[:, HI])),
                "B.q2": query2_lo, "B.norm": context_deviations, "B.h0": lambda at, g: hidden_lo(at, g, 0), "B.h1": lambda at, g: hidden_lo(at, g, 1),
                "B.cT": lambda at, g, b: low(p_ct_lo, g, v_ct_hi, b + 1, ct[:, LO, :, :], ct_tmp[:, :, :], ct[:, HI, :, :])})

        assert made == set(sig), set(sig) - made


def kernel(**inputs):
    import concourse.bacc as bacc
    from concourse.bass_utils import run_bass_kernel_spmd

    a = {n: np.asarray(x) for n, x in inputs.items()}

    def layer(prefix, n):
        return a[prefix + n]

    cols = lambda x: np.ascontiguousarray(x.reshape(-1, 128).T)
    t = np.ascontiguousarray
    rows = np.arange(128)
    even = ((rows // D) % 2 == 0).astype(np.float32)[:, None]
    vec = np.concatenate([cols(a[n]) for n in (
        "L0_xattn_bq", "L0_xattn_bk", "L1_xattn_ln1_g", "L1_xattn_ln1_b", "L1_xattn_ln3_g", "L1_xattn_ln3_b",
        "L1_xattn_ln2_g", "L1_xattn_ln2_b", "L1_xattn_ff_b1")] + [even, 1 - even], axis=1)
    p, d_ = np.meshgrid(np.arange(4), np.arange(D), indexing="ij")
    fold = np.zeros((128, 4 * D), np.float32)
    fold[(32 * p + d_).ravel(), (D * p + d_).ravel()] = 1.0
    kq = np.arange(T)[:, None] <= np.arange(T)[None, :]
    bf = mybir.dt.np(BF16)
    data = {
        "x": t(a["x"]), "x_t": t(a["x"].reshape(B * T, U).T),
        "ctx": t(a["ctx_1024"]), "ctx_t": t(a["ctx_1024"].reshape(B * S, U).T),
        "mask": t(a["mask_BxS_bf0"].T), "vec": t(vec),
        "w_wq0": t(a["L0_xattn_Wq"].T), "w_wk0": t(a["L0_xattn_Wk"].T), "w_wv0": t(a["L0_xattn_Wv"].T),
        "w_wqkv1": t(a["L1_xattn_sa_wqkv"]), "w_wp1": t(a["L1_xattn_sa_wproj"]), "w_wq2": t(a["L1_xattn_ed_wq"]),
        "w_wkv2": t(a["L1_xattn_ed_wkv"]), "w_wp2": t(a["L1_xattn_ed_wproj"]), "w_w1": t(a["L1_xattn_ff_w1"]),
        "w_w2": t(a["L1_xattn_ff_w2"]),
        "r_bv0": t(a["L0_xattn_bv"]), "r_gamma0": t(a["L0_xattn_gamma"]), "r_beta0": t(a["L0_xattn_beta"]),
        "r_bp1": t(a["L1_xattn_sa_bproj"]), "r_bp2": t(a["L1_xattn_ed_bproj"]), "r_fb2": t(a["L1_xattn_ff_b2"]),
        "c_ident": np.eye(128, dtype=np.float32), "c_ident_b": np.eye(T).astype(bf),
        "c_causal": np.where(kq, 0.0, BIG).astype(bf), "c_tril": kq.astype(bf), "c_fold": fold,
    }
    nc = bacc.Bacc("TRN2", target_bir_lowering=False, num_devices=1)
    d = {n: nc.dram_tensor("in_" + n, x.shape, mybir.dt.from_np(x.dtype), kind="ExternalInput").ap() for n, x in data.items()}
    out = nc.dram_tensor("out", [B, T, U], F32, kind="ExternalOutput").ap()

    def group(prefix):
        return {n[len(prefix):]: ap for n, ap in d.items() if n.startswith(prefix)}

    build(nc, d["x"], d["x_t"], d["ctx"], d["ctx_t"], d["ctx"][:, 0, :], d["mask"], group("w_"), d["vec"], group("r_"), group("c_"), out)
    r = run_bass_kernel_spmd(nc, [{"in_" + n: x for n, x in data.items()}], core_ids=[0])
    return r.results[0]["out"]
```
